# Optimizing a Trainium2 kernel written in Bass

```python
import numpy as np
import jax
import jax.numpy as jnp

def _softmax(x, axis=-1):
    return jax.nn.softmax(x, axis=axis)

def _gelu(x):
    return jax.nn.gelu(x, approximate=True)

def _silu(x):
    return jax.nn.silu(x)

def _sigmoid(x):
    return jax.nn.sigmoid(x)

def _layernorm(x, axis=-1, eps=1e-05):
    m = jnp.mean(x, axis=axis, keepdims=True)
    v = jnp.var(x, axis=axis, keepdims=True)
    return (x - m) / jnp.sqrt(v + eps)

def _scatter_add(tgt, idx, src, axis=0):
    return tgt.at[idx].add(src)

def _segment_sum(src, seg, n):
    return jax.ops.segment_sum(src, seg, n)
kernel_name = 'mk_adaln_attn_ffn_d2_seqx_r8_00ec2e'

def setup_inputs(seed: int=0):
    np.random.seed(seed)
    _w = jnp.asarray

    def _rec_inputs():
        import jax
        import jax.numpy as jnp
        _rk = jax.random.key(seed)
        x = -0.000125 + 0.9999 * jax.random.normal(jax.random.fold_in(_rk, 1), (4, 256, 256), jnp.float32)
        _lenS = 256 - jax.random.randint(jax.random.fold_in(_rk, 7), (4,), 0, max(1, 256 // 4) + 1, jnp.int32)
        _lenS2 = 256 - jax.random.randint(jax.random.fold_in(_rk, 8), (4,), 0, max(1, 256 // 4) + 1, jnp.int32)
        fside_BxSxS_0 = -1.52775e-05 + 0.999936 * jax.random.normal(jax.random.fold_in(_rk, 11), (4, 256, 256), jnp.float32)
        cond_512 = -5.03954e-05 + 1.00559 * jax.random.normal(jax.random.fold_in(_rk, 12), (4, 64), jnp.float32)
        return (x, fside_BxSxS_0, cond_512)
    x, fside_BxSxS_0, cond_512 = _rec_inputs()

    def _L0_cond_setup():
        import jax, jax.numpy as jnp
        from jax import lax
        import numpy as np
        B, T, C, TD = (8, 256, 256, 64)

        def _bi_wkv(r, k, v, w, u, time_emb):
            tf = jax.nn.sigmoid(jnp.sum(time_emb, axis=-1))[:, None, None]
            decay = jnp.exp(-jnp.exp(w.astype(jnp.float32)))[None, :] * (0.5 + 0.5 * tf[:, :, 0])
            kf = k.astype(jnp.float32)
            vf = v.astype(jnp.float32)
            ek = jnp.exp(jnp.minimum(kf, 30.0))
            ekv = ek * vf

            def step(carry, x):
                a, b = carry
                ekv_t, ek_t = x
                a = a * decay + ekv_t
                b = b * decay + ek_t
                return ((a, b), (a, b))
            ekv_t = jnp.swapaxes(ekv, 0, 1)
            ek_t = jnp.swapaxes(ek, 0, 1)
            init = (jnp.zeros_like(decay), jnp.zeros_like(decay))
            _, (nf, df) = lax.scan(step, init, (ekv_t, ek_t))
            _, (nb, db) = lax.scan(step, init, (ekv_t, ek_t), reverse=True)
            nf = jnp.swapaxes(nf, 0, 1)
            df = jnp.swapaxes(df, 0, 1)
            nb = jnp.swapaxes(nb, 0, 1)
            db = jnp.swapaxes(db, 0, 1)
            euk = jnp.exp(jnp.minimum(u.astype(jnp.float32)[None, None, :] + kf, 30.0))
            num = nf + nb - ekv + euk * vf
            den = df + db - ek + euk
            base = jax.nn.sigmoid(r.astype(jnp.float32)) * (num / jnp.maximum(den, 1e-08))
            out = base * (0.8 + 0.2 * tf)
            return out.astype(r.dtype)
        key = jax.random.key(seed)
        ks = jax.random.split(key, 6)
        return {'r': jax.random.normal(ks[0], (B, T, C), dtype=jnp.float32), 'k': jax.random.normal(ks[1], (B, T, C), dtype=jnp.float32), 'v': jax.random.normal(ks[2], (B, T, C), dtype=jnp.float32), 'w': jax.random.normal(ks[3], (C,), dtype=jnp.float32), 'u': jax.random.normal(ks[4], (C,), dtype=jnp.float32), 'time_emb': jax.random.normal(ks[5], (B, TD), dtype=jnp.float32)}
    _L0_cond_all = _L0_cond_setup()
    _L0_cond_in = {k: v for k, v in _L0_cond_all.items() if k in ('w', 'u')}
    del _L0_cond_all

    def _L0_attn_setup():
        import jax, jax.numpy as jnp
        import numpy as np
        D_MODEL = 256
        N_HEADS = 16
        D_HEAD = D_MODEL // N_HEADS
        B, S = (2, 256)
        key = jax.random.key(seed)
        ks = jax.random.split(key, 9)
        sd = 1.0 / np.sqrt(D_MODEL)
        return {'X': jax.random.normal(ks[0], (B, S, D_MODEL), dtype=jnp.float32), 'Wq': jax.random.normal(ks[1], (D_MODEL, D_MODEL), dtype=jnp.float32) * sd, 'bq': jax.random.normal(ks[2], (D_MODEL,), dtype=jnp.float32) * sd, 'Wk': jax.random.normal(ks[3], (D_MODEL, D_MODEL), dtype=jnp.float32) * sd, 'bk': jax.random.normal(ks[4], (D_MODEL,), dtype=jnp.float32) * sd, 'Wv': jax.random.normal(ks[5], (D_MODEL, D_MODEL), dtype=jnp.float32) * sd, 'bv': jax.random.normal(ks[6], (D_MODEL,), dtype=jnp.float32) * sd, 'Wo': jax.random.normal(ks[7], (D_MODEL, D_MODEL), dtype=jnp.float32) * sd, 'bo': jax.random.normal(ks[8], (D_MODEL,), dtype=jnp.float32) * sd}
    _L0_attn_all = _L0_attn_setup()
    _L0_attn_in = {k: v for k, v in _L0_attn_all.items() if k in ('Wq', 'bq', 'Wk', 'bk', 'Wv', 'bv', 'Wo', 'bo')}
    del _L0_attn_all

    def _L0_cond2_setup():
        import jax, jax.numpy as jnp
        from jax import lax
        import numpy as np
        B, T, C, TD = (8, 256, 256, 64)

        def _bi_wkv(r, k, v, w, u, time_emb):
            tf = jax.nn.sigmoid(jnp.sum(time_emb, axis=-1))[:, None, None]
            decay = jnp.exp(-jnp.exp(w.astype(jnp.float32)))[None, :] * (0.5 + 0.5 * tf[:, :, 0])
            kf = k.astype(jnp.float32)
            vf = v.astype(jnp.float32)
            ek = jnp.exp(jnp.minimum(kf, 30.0))
            ekv = ek * vf

            def step(carry, x):
                a, b = carry
                ekv_t, ek_t = x
                a = a * decay + ekv_t
                b = b * decay + ek_t
                return ((a, b), (a, b))
            ekv_t = jnp.swapaxes(ekv, 0, 1)
            ek_t = jnp.swapaxes(ek, 0, 1)
            init = (jnp.zeros_like(decay), jnp.zeros_like(decay))
            _, (nf, df) = lax.scan(step, init, (ekv_t, ek_t))
            _, (nb, db) = lax.scan(step, init, (ekv_t, ek_t), reverse=True)
            nf = jnp.swapaxes(nf, 0, 1)
            df = jnp.swapaxes(df, 0, 1)
            nb = jnp.swapaxes(nb, 0, 1)
            db = jnp.swapaxes(db, 0, 1)
            euk = jnp.exp(jnp.minimum(u.astype(jnp.float32)[None, None, :] + kf, 30.0))
            num = nf + nb - ekv + euk * vf
            den = df + db - ek + euk
            base = jax.nn.sigmoid(r.astype(jnp.float32)) * (num / jnp.maximum(den, 1e-08))
            out = base * (0.8 + 0.2 * tf)
            return out.astype(r.dtype)
        key = jax.random.key(seed)
        ks = jax.random.split(key, 6)
        return {'r': jax.random.normal(ks[0], (B, T, C), dtype=jnp.float32), 'k': jax.random.normal(ks[1], (B, T, C), dtype=jnp.float32), 'v': jax.random.normal(ks[2], (B, T, C), dtype=jnp.float32), 'w': jax.random.normal(ks[3], (C,), dtype=jnp.float32), 'u': jax.random.normal(ks[4], (C,), dtype=jnp.float32), 'time_emb': jax.random.normal(ks[5], (B, TD), dtype=jnp.float32)}
    _L0_cond2_all = _L0_cond2_setup()
    _L0_cond2_in = {k: v for k, v in _L0_cond2_all.items() if k in ('w', 'u')}
    del _L0_cond2_all

    def _L0_ffn_setup():
        import jax, jax.numpy as jnp
        import numpy as np
        THRESHOLD = 0.05
        ACT_BITS = 4
        QMAX = 2 ** (ACT_BITS - 1) - 1
        EPS = 1e-08

        def ternarize(W, threshold):
            absW = jnp.abs(W)
            delta = threshold * jnp.max(absW)
            mask = absW > delta
            n = jnp.maximum(jnp.sum(mask), 1)
            alpha = jnp.sum(jnp.where(mask, absW, 0.0)) / n
            Wt = alpha * jnp.sign(W) * mask
            return W + jax.lax.stop_gradient(Wt - W)

        def ternary_linear(x, W, b, threshold=THRESHOLD):
            Wq = ternarize(W, threshold)
            return jnp.einsum('bsd,hd->bsh', x, Wq) + b

        def fp4_activation(x):
            scale = jnp.max(jnp.abs(x)) / QMAX + EPS
            q = jnp.clip(jnp.round(x / scale), -QMAX, QMAX) * scale
            return x + jax.lax.stop_gradient(q - x)
        key = jax.random.key(seed)
        k1, k2, k3, k4, k5 = jax.random.split(key, 5)
        B, S, D, H = (2, 512, 256, 1024)
        x = jax.random.normal(k1, (B, S, D), dtype=jnp.float32)
        W1 = jax.random.normal(k2, (H, D), dtype=jnp.float32) * (1.0 / np.sqrt(D))
        b1 = jax.random.normal(k3, (H,), dtype=jnp.float32) * 0.02
        W2 = jax.random.normal(k4, (D, H), dtype=jnp.float32) * (1.0 / np.sqrt(H))
        b2 = jax.random.normal(k5, (D,), dtype=jnp.float32) * 0.02
        return {'x': x, 'W1': W1, 'b1': b1, 'W2': W2, 'b2': b2}
    _L0_ffn_all = _L0_ffn_setup()
    _L0_ffn_in = {k: v for k, v in _L0_ffn_all.items() if k in ('W1', 'b1', 'W2', 'b2')}
    del _L0_ffn_all

    def _L1_cond_setup():
        import jax, jax.numpy as jnp
        from jax import lax
        import numpy as np
        B, T, C, TD = (8, 256, 256, 64)

        def _bi_wkv(r, k, v, w, u, time_emb):
            tf = jax.nn.sigmoid(jnp.sum(time_emb, axis=-1))[:, None, None]
            decay = jnp.exp(-jnp.exp(w.astype(jnp.float32)))[None, :] * (0.5 + 0.5 * tf[:, :, 0])
            kf = k.astype(jnp.float32)
            vf = v.astype(jnp.float32)
            ek = jnp.exp(jnp.minimum(kf, 30.0))
            ekv = ek * vf

            def step(carry, x):
                a, b = carry
                ekv_t, ek_t = x
                a = a * decay + ekv_t
                b = b * decay + ek_t
                return ((a, b), (a, b))
            ekv_t = jnp.swapaxes(ekv, 0, 1)
            ek_t = jnp.swapaxes(ek, 0, 1)
            init = (jnp.zeros_like(decay), jnp.zeros_like(decay))
            _, (nf, df) = lax.scan(step, init, (ekv_t, ek_t))
            _, (nb, db) = lax.scan(step, init, (ekv_t, ek_t), reverse=True)
            nf = jnp.swapaxes(nf, 0, 1)
            df = jnp.swapaxes(df, 0, 1)
            nb = jnp.swapaxes(nb, 0, 1)
            db = jnp.swapaxes(db, 0, 1)
            euk = jnp.exp(jnp.minimum(u.astype(jnp.float32)[None, None, :] + kf, 30.0))
            num = nf + nb - ekv + euk * vf
            den = df + db - ek + euk
            base = jax.nn.sigmoid(r.astype(jnp.float32)) * (num / jnp.maximum(den, 1e-08))
            out = base * (0.8 + 0.2 * tf)
            return out.astype(r.dtype)
        key = jax.random.key(seed)
        ks = jax.random.split(key, 6)
        return {'r': jax.random.normal(ks[0], (B, T, C), dtype=jnp.float32), 'k': jax.random.normal(ks[1], (B, T, C), dtype=jnp.float32), 'v': jax.random.normal(ks[2], (B, T, C), dtype=jnp.float32), 'w': jax.random.normal(ks[3], (C,), dtype=jnp.float32), 'u': jax.random.normal(ks[4], (C,), dtype=jnp.float32), 'time_emb': jax.random.normal(ks[5], (B, TD), dtype=jnp.float32)}
    _L1_cond_all = _L1_cond_setup()
    _L1_cond_in = {k: v for k, v in _L1_cond_all.items() if k in ('w', 'u')}
    del _L1_cond_all

    def _L1_attn_setup():
        import jax, jax.numpy as jnp
        import numpy as np
        HID = 256
        H = 16
        D = HID // H
        THETA = 10000.0

        def _rope(q, k):
            T = q.shape[1]
            half = D // 2
            inv_freq = 1.0 / THETA ** (jnp.arange(half, dtype=jnp.float32) / half)
            ang = jnp.arange(T, dtype=jnp.float32)[:, None] * inv_freq[None, :]
            cos = jnp.cos(ang)[None, :, None, :]
            sin = jnp.sin(ang)[None, :, None, :]

            def rot(x):
                x1, x2 = (x[..., :half], x[..., half:])
                return jnp.concatenate([x1 * cos - x2 * sin, x2 * cos + x1 * sin], axis=-1)
            return (rot(q), rot(k))
        key = jax.random.key(seed)
        ks = jax.random.split(key, 7)
        B, T = (1, 256)
        s = 1.0 / np.sqrt(HID)
        return {'hidden_states': jax.random.normal(ks[0], (B, T, HID), dtype=jnp.float32), 'Wq': jax.random.normal(ks[1], (HID, HID), dtype=jnp.float32) * s, 'Wk': jax.random.normal(ks[2], (HID, HID), dtype=jnp.float32) * s, 'Wv': jax.random.normal(ks[3], (HID, HID), dtype=jnp.float32) * s, 'Wb': jax.random.normal(ks[4], (HID, H), dtype=jnp.float32) * s, 'bb': jnp.zeros((H,), dtype=jnp.float32), 'Wo': jax.random.normal(ks[5], (HID, HID), dtype=jnp.float32) * s}
    _L1_attn_all = _L1_attn_setup()
    _L1_attn_in = {k: v for k, v in _L1_attn_all.items() if k in ('Wq', 'Wk', 'Wv', 'Wb', 'bb', 'Wo')}
    del _L1_attn_all

    def _L1_cond2_setup():
        import jax, jax.numpy as jnp
        from jax import lax
        import numpy as np
        B, T, C, TD = (8, 256, 256, 64)

        def _bi_wkv(r, k, v, w, u, time_emb):
            tf = jax.nn.sigmoid(jnp.sum(time_emb, axis=-1))[:, None, None]
            decay = jnp.exp(-jnp.exp(w.astype(jnp.float32)))[None, :] * (0.5 + 0.5 * tf[:, :, 0])
            kf = k.astype(jnp.float32)
            vf = v.astype(jnp.float32)
            ek = jnp.exp(jnp.minimum(kf, 30.0))
            ekv = ek * vf

            def step(carry, x):
                a, b = carry
                ekv_t, ek_t = x
                a = a * decay + ekv_t
                b = b * decay + ek_t
                return ((a, b), (a, b))
            ekv_t = jnp.swapaxes(ekv, 0, 1)
            ek_t = jnp.swapaxes(ek, 0, 1)
            init = (jnp.zeros_like(decay), jnp.zeros_like(decay))
            _, (nf, df) = lax.scan(step, init, (ekv_t, ek_t))
            _, (nb, db) = lax.scan(step, init, (ekv_t, ek_t), reverse=True)
            nf = jnp.swapaxes(nf, 0, 1)
            df = jnp.swapaxes(df, 0, 1)
            nb = jnp.swapaxes(nb, 0, 1)
            db = jnp.swapaxes(db, 0, 1)
            euk = jnp.exp(jnp.minimum(u.astype(jnp.float32)[None, None, :] + kf, 30.0))
            num = nf + nb - ekv + euk * vf
            den = df + db - ek + euk
            base = jax.nn.sigmoid(r.astype(jnp.float32)) * (num / jnp.maximum(den, 1e-08))
            out = base * (0.8 + 0.2 * tf)
            return out.astype(r.dtype)
        key = jax.random.key(seed)
        ks = jax.random.split(key, 6)
        return {'r': jax.random.normal(ks[0], (B, T, C), dtype=jnp.float32), 'k': jax.random.normal(ks[1], (B, T, C), dtype=jnp.float32), 'v': jax.random.normal(ks[2], (B, T, C), dtype=jnp.float32), 'w': jax.random.normal(ks[3], (C,), dtype=jnp.float32), 'u': jax.random.normal(ks[4], (C,), dtype=jnp.float32), 'time_emb': jax.random.normal(ks[5], (B, TD), dtype=jnp.float32)}
    _L1_cond2_all = _L1_cond2_setup()
    _L1_cond2_in = {k: v for k, v in _L1_cond2_all.items() if k in ('w', 'u')}
    del _L1_cond2_all

    def _L1_ffn_setup():
        import jax, jax.numpy as jnp
        import numpy as np
        D_MODEL = 256
        HIDDEN = 4 * D_MODEL
        N_EXPERTS = 8
        TOP_K = 2
        CAP_FACTOR = 1.0
        key = jax.random.key(seed)
        ks = jax.random.split(key, 6)
        x = jax.random.normal(ks[0], (4, 256, D_MODEL), dtype=jnp.float32)
        wg = jax.random.normal(ks[1], (D_MODEL, N_EXPERTS), dtype=jnp.float32) * (1.0 / np.sqrt(D_MODEL))
        fc1_w = jax.random.normal(ks[2], (N_EXPERTS, D_MODEL, HIDDEN), dtype=jnp.float32) * 0.02
        fc1_b = jnp.zeros((N_EXPERTS, HIDDEN), dtype=jnp.float32)
        fc2_w = jax.random.normal(ks[3], (N_EXPERTS, HIDDEN, D_MODEL), dtype=jnp.float32) * 0.02
        fc2_b = jnp.zeros((N_EXPERTS, D_MODEL), dtype=jnp.float32)
        return {'x': x, 'wg': wg, 'fc1_w': fc1_w, 'fc1_b': fc1_b, 'fc2_w': fc2_w, 'fc2_b': fc2_b}
    _L1_ffn_all = _L1_ffn_setup()
    _L1_ffn_in = {k: v for k, v in _L1_ffn_all.items() if k in ('wg', 'fc1_w', 'fc1_b', 'fc2_w', 'fc2_b')}
    del _L1_ffn_all
    return {'x': x, 'fside_BxSxS_0': fside_BxSxS_0, 'cond_512': cond_512, 'L0_cond_w': _L0_cond_in['w'], 'L0_cond_u': _L0_cond_in['u'], 'L0_attn_Wq': _L0_attn_in['Wq'], 'L0_attn_bq': _L0_attn_in['bq'], 'L0_attn_Wk': _L0_attn_in['Wk'], 'L0_attn_bk': _L0_attn_in['bk'], 'L0_attn_Wv': _L0_attn_in['Wv'], 'L0_attn_bv': _L0_attn_in['bv'], 'L0_attn_Wo': _L0_attn_in['Wo'], 'L0_attn_bo': _L0_attn_in['bo'], 'L0_cond2_w': _L0_cond2_in['w'], 'L0_cond2_u': _L0_cond2_in['u'], 'L0_ffn_W1': _L0_ffn_in['W1'], 'L0_ffn_b1': _L0_ffn_in['b1'], 'L0_ffn_W2': _L0_ffn_in['W2'], 'L0_ffn_b2': _L0_ffn_in['b2'], 'L1_cond_w': _L1_cond_in['w'], 'L1_cond_u': _L1_cond_in['u'], 'L1_attn_Wq': _L1_attn_in['Wq'], 'L1_attn_Wk': _L1_attn_in['Wk'], 'L1_attn_Wv': _L1_attn_in['Wv'], 'L1_attn_Wb': _L1_attn_in['Wb'], 'L1_attn_bb': _L1_attn_in['bb'], 'L1_attn_Wo': _L1_attn_in['Wo'], 'L1_cond2_w': _L1_cond2_in['w'], 'L1_cond2_u': _L1_cond2_in['u'], 'L1_ffn_wg': _L1_ffn_in['wg'], 'L1_ffn_fc1_w': _L1_ffn_in['fc1_w'], 'L1_ffn_fc1_b': _L1_ffn_in['fc1_b'], 'L1_ffn_fc2_w': _L1_ffn_in['fc2_w'], 'L1_ffn_fc2_b': _L1_ffn_in['fc2_b']}

def reference(x, fside_BxSxS_0, cond_512, L0_cond_w, L0_cond_u, L0_attn_Wq, L0_attn_bq, L0_attn_Wk, L0_attn_bk, L0_attn_Wv, L0_attn_bv, L0_attn_Wo, L0_attn_bo, L0_cond2_w, L0_cond2_u, L0_ffn_W1, L0_ffn_b1, L0_ffn_W2, L0_ffn_b2, L1_cond_w, L1_cond_u, L1_attn_Wq, L1_attn_Wk, L1_attn_Wv, L1_attn_Wb, L1_attn_bb, L1_attn_Wo, L1_cond2_w, L1_cond2_u, L1_ffn_wg, L1_ffn_fc1_w, L1_ffn_fc1_b, L1_ffn_fc2_w, L1_ffn_fc2_b):
    import jax
    import jax.numpy as jnp

    def _L0_cond_ref(r, k, v, w, u, time_emb):
        import jax, jax.numpy as jnp
        from jax import lax
        import numpy as np
        B, T, C, TD = (8, 256, 256, 64)

        def _bi_wkv(r, k, v, w, u, time_emb):
            tf = jax.nn.sigmoid(jnp.sum(time_emb, axis=-1))[:, None, None]
            decay = jnp.exp(-jnp.exp(w.astype(jnp.float32)))[None, :] * (0.5 + 0.5 * tf[:, :, 0])
            kf = k.astype(jnp.float32)
            vf = v.astype(jnp.float32)
            ek = jnp.exp(jnp.minimum(kf, 30.0))
            ekv = ek * vf

            def step(carry, x):
                a, b = carry
                ekv_t, ek_t = x
                a = a * decay + ekv_t
                b = b * decay + ek_t
                return ((a, b), (a, b))
            ekv_t = jnp.swapaxes(ekv, 0, 1)
            ek_t = jnp.swapaxes(ek, 0, 1)
            init = (jnp.zeros_like(decay), jnp.zeros_like(decay))
            _, (nf, df) = lax.scan(step, init, (ekv_t, ek_t))
            _, (nb, db) = lax.scan(step, init, (ekv_t, ek_t), reverse=True)
            nf = jnp.swapaxes(nf, 0, 1)
            df = jnp.swapaxes(df, 0, 1)
            nb = jnp.swapaxes(nb, 0, 1)
            db = jnp.swapaxes(db, 0, 1)
            euk = jnp.exp(jnp.minimum(u.astype(jnp.float32)[None, None, :] + kf, 30.0))
            num = nf + nb - ekv + euk * vf
            den = df + db - ek + euk
            base = jax.nn.sigmoid(r.astype(jnp.float32)) * (num / jnp.maximum(den, 1e-08))
            out = base * (0.8 + 0.2 * tf)
            return out.astype(r.dtype)
        return _bi_wkv(r, k, v, w, u, time_emb)

    def _L0_attn_ref(X, Wq, bq, Wk, bk, Wv, bv, Wo, bo):
        import jax, jax.numpy as jnp
        import numpy as np
        D_MODEL = 256
        N_HEADS = 16
        D_HEAD = D_MODEL // N_HEADS
        B, S = (2, 256)
        b, s, _ = X.shape

        def proj(W, bias):
            y = X @ W + bias
            return y.reshape(b, s, N_HEADS, D_HEAD).transpose(0, 2, 1, 3)
        q = proj(Wq, bq)
        k = proj(Wk, bk)
        v = proj(Wv, bv)
        scale = 1.0 / jnp.sqrt(jnp.asarray(D_HEAD, dtype=X.dtype))
        scores = jnp.einsum('bhqd,bhkd->bhqk', q, k) * scale
        causal = jnp.tril(jnp.ones((s, s), dtype=bool))
        scores = jnp.where(causal, scores, -jnp.inf)
        weights = jax.nn.softmax(scores, axis=-1)
        attn = jnp.einsum('bhqk,bhkd->bhqd', weights, v)
        attn = attn.transpose(0, 2, 1, 3).reshape(b, s, D_MODEL)
        return attn @ Wo + bo

    def _L0_cond2_ref(r, k, v, w, u, time_emb):
        import jax, jax.numpy as jnp
        from jax import lax
        import numpy as np
        B, T, C, TD = (8, 256, 256, 64)

        def _bi_wkv(r, k, v, w, u, time_emb):
            tf = jax.nn.sigmoid(jnp.sum(time_emb, axis=-1))[:, None, None]
            decay = jnp.exp(-jnp.exp(w.astype(jnp.float32)))[None, :] * (0.5 + 0.5 * tf[:, :, 0])
            kf = k.astype(jnp.float32)
            vf = v.astype(jnp.float32)
            ek = jnp.exp(jnp.minimum(kf, 30.0))
            ekv = ek * vf

            def step(carry, x):
                a, b = carry
                ekv_t, ek_t = x
                a = a * decay + ekv_t
                b = b * decay + ek_t
                return ((a, b), (a, b))
            ekv_t = jnp.swapaxes(ekv, 0, 1)
            ek_t = jnp.swapaxes(ek, 0, 1)
            init = (jnp.zeros_like(decay), jnp.zeros_like(decay))
            _, (nf, df) = lax.scan(step, init, (ekv_t, ek_t))
            _, (nb, db) = lax.scan(step, init, (ekv_t, ek_t), reverse=True)
            nf = jnp.swapaxes(nf, 0, 1)
            df = jnp.swapaxes(df, 0, 1)
            nb = jnp.swapaxes(nb, 0, 1)
            db = jnp.swapaxes(db, 0, 1)
            euk = jnp.exp(jnp.minimum(u.astype(jnp.float32)[None, None, :] + kf, 30.0))
            num = nf + nb - ekv + euk * vf
            den = df + db - ek + euk
            base = jax.nn.sigmoid(r.astype(jnp.float32)) * (num / jnp.maximum(den, 1e-08))
            out = base * (0.8 + 0.2 * tf)
            return out.astype(r.dtype)
        return _bi_wkv(r, k, v, w, u, time_emb)

    def _L0_ffn_ref(x, W1, b1, W2, b2):
        import jax, jax.numpy as jnp
        import numpy as np
        THRESHOLD = 0.05
        ACT_BITS = 4
        QMAX = 2 ** (ACT_BITS - 1) - 1
        EPS = 1e-08

        def ternarize(W, threshold):
            absW = jnp.abs(W)
            delta = threshold * jnp.max(absW)
            mask = absW > delta
            n = jnp.maximum(jnp.sum(mask), 1)
            alpha = jnp.sum(jnp.where(mask, absW, 0.0)) / n
            Wt = alpha * jnp.sign(W) * mask
            return W + jax.lax.stop_gradient(Wt - W)

        def ternary_linear(x, W, b, threshold=THRESHOLD):
            Wq = ternarize(W, threshold)
            return jnp.einsum('bsd,hd->bsh', x, Wq) + b

        def fp4_activation(x):
            scale = jnp.max(jnp.abs(x)) / QMAX + EPS
            q = jnp.clip(jnp.round(x / scale), -QMAX, QMAX) * scale
            return x + jax.lax.stop_gradient(q - x)
        h = ternary_linear(x, W1, b1)
        h = jax.nn.gelu(h, approximate=False)
        y = ternary_linear(h, W2, b2)
        return fp4_activation(y)

    def _L1_cond_ref(r, k, v, w, u, time_emb):
        import jax, jax.numpy as jnp
        from jax import lax
        import numpy as np
        B, T, C, TD = (8, 256, 256, 64)

        def _bi_wkv(r, k, v, w, u, time_emb):
            tf = jax.nn.sigmoid(jnp.sum(time_emb, axis=-1))[:, None, None]
            decay = jnp.exp(-jnp.exp(w.astype(jnp.float32)))[None, :] * (0.5 + 0.5 * tf[:, :, 0])
            kf = k.astype(jnp.float32)
            vf = v.astype(jnp.float32)
            ek = jnp.exp(jnp.minimum(kf, 30.0))
            ekv = ek * vf

            def step(carry, x):
                a, b = carry
                ekv_t, ek_t = x
                a = a * decay + ekv_t
                b = b * decay + ek_t
                return ((a, b), (a, b))
            ekv_t = jnp.swapaxes(ekv, 0, 1)
            ek_t = jnp.swapaxes(ek, 0, 1)
            init = (jnp.zeros_like(decay), jnp.zeros_like(decay))
            _, (nf, df) = lax.scan(step, init, (ekv_t, ek_t))
            _, (nb, db) = lax.scan(step, init, (ekv_t, ek_t), reverse=True)
            nf = jnp.swapaxes(nf, 0, 1)
            df = jnp.swapaxes(df, 0, 1)
            nb = jnp.swapaxes(nb, 0, 1)
            db = jnp.swapaxes(db, 0, 1)
            euk = jnp.exp(jnp.minimum(u.astype(jnp.float32)[None, None, :] + kf, 30.0))
            num = nf + nb - ekv + euk * vf
            den = df + db - ek + euk
            base = jax.nn.sigmoid(r.astype(jnp.float32)) * (num / jnp.maximum(den, 1e-08))
            out = base * (0.8 + 0.2 * tf)
            return out.astype(r.dtype)
        return _bi_wkv(r, k, v, w, u, time_emb)

    def _L1_attn_ref(hidden_states, Wq, Wk, Wv, Wb, bb, Wo):
        import jax, jax.numpy as jnp
        import numpy as np
        HID = 256
        H = 16
        D = HID // H
        THETA = 10000.0

        def _rope(q, k):
            T = q.shape[1]
            half = D // 2
            inv_freq = 1.0 / THETA ** (jnp.arange(half, dtype=jnp.float32) / half)
            ang = jnp.arange(T, dtype=jnp.float32)[:, None] * inv_freq[None, :]
            cos = jnp.cos(ang)[None, :, None, :]
            sin = jnp.sin(ang)[None, :, None, :]

            def rot(x):
                x1, x2 = (x[..., :half], x[..., half:])
                return jnp.concatenate([x1 * cos - x2 * sin, x2 * cos + x1 * sin], axis=-1)
            return (rot(q), rot(k))
        B, T, _ = hidden_states.shape
        scale = 1.0 / np.sqrt(D)
        q = (hidden_states @ Wq).reshape(B, T, H, D)
        k = (hidden_states @ Wk).reshape(B, T, H, D)
        v = (hidden_states @ Wv).reshape(B, T, H, D)
        beta = hidden_states @ Wb + bb
        q, k = _rope(q, k)
        s = jnp.einsum('bihd,bjhd->bhij', k, k) * scale
        idx = jnp.arange(T)
        strict = idx[:, None] > idx[None, :]
        s = jnp.where(strict, s, -jnp.inf)
        m = jnp.max(s, axis=-1, keepdims=True)
        e = jnp.exp(s - jnp.where(jnp.isfinite(m), m, 0.0))
        e = jnp.where(strict, e, 0.0)
        denom = jnp.sum(e, axis=-1, keepdims=True)
        p = e / jnp.where(denom == 0, 1.0, denom)
        L = p * beta.transpose(0, 2, 1)[..., None]
        A = L + jnp.eye(T, dtype=L.dtype)[None, None]
        u = jax.scipy.linalg.solve_triangular(A, v.transpose(0, 2, 1, 3), lower=True)
        sc = jnp.einsum('bihd,bjhd->bhij', q, k) * scale
        causal = idx[:, None] >= idx[None, :]
        sc = jnp.where(causal, sc, -jnp.inf)
        attn = jax.nn.softmax(sc, axis=-1)
        o = jnp.einsum('bhij,bhjd->bihd', attn, u).reshape(B, T, HID)
        return o @ Wo

    def _L1_cond2_ref(r, k, v, w, u, time_emb):
        import jax, jax.numpy as jnp
        from jax import lax
        import numpy as np
        B, T, C, TD = (8, 256, 256, 64)

        def _bi_wkv(r, k, v, w, u, time_emb):
            tf = jax.nn.sigmoid(jnp.sum(time_emb, axis=-1))[:, None, None]
            decay = jnp.exp(-jnp.exp(w.astype(jnp.float32)))[None, :] * (0.5 + 0.5 * tf[:, :, 0])
            kf = k.astype(jnp.float32)
            vf = v.astype(jnp.float32)
            ek = jnp.exp(jnp.minimum(kf, 30.0))
            ekv = ek * vf

            def step(carry, x):
                a, b = carry
                ekv_t, ek_t = x
                a = a * decay + ekv_t
                b = b * decay + ek_t
                return ((a, b), (a, b))
            ekv_t = jnp.swapaxes(ekv, 0, 1)
            ek_t = jnp.swapaxes(ek, 0, 1)
            init = (jnp.zeros_like(decay), jnp.zeros_like(decay))
            _, (nf, df) = lax.scan(step, init, (ekv_t, ek_t))
            _, (nb, db) = lax.scan(step, init, (ekv_t, ek_t), reverse=True)
            nf = jnp.swapaxes(nf, 0, 1)
            df = jnp.swapaxes(df, 0, 1)
            nb = jnp.swapaxes(nb, 0, 1)
            db = jnp.swapaxes(db, 0, 1)
            euk = jnp.exp(jnp.minimum(u.astype(jnp.float32)[None, None, :] + kf, 30.0))
            num = nf + nb - ekv + euk * vf
            den = df + db - ek + euk
            base = jax.nn.sigmoid(r.astype(jnp.float32)) * (num / jnp.maximum(den, 1e-08))
            out = base * (0.8 + 0.2 * tf)
            return out.astype(r.dtype)
        return _bi_wkv(r, k, v, w, u, time_emb)

    def _L1_ffn_ref(x, wg, fc1_w, fc1_b, fc2_w, fc2_b):
        import jax, jax.numpy as jnp
        import numpy as np
        D_MODEL = 256
        HIDDEN = 4 * D_MODEL
        N_EXPERTS = 8
        TOP_K = 2
        CAP_FACTOR = 1.0
        B, L, D = x.shape
        S = B * L
        E = wg.shape[1]
        K = TOP_K
        C = int(K * S * CAP_FACTOR) // E
        xt = x.reshape(S, D)
        scores = jax.nn.softmax(xt.astype(jnp.float32) @ wg.astype(jnp.float32), axis=-1)
        gate_vals, idx = jax.lax.top_k(scores, K)
        gate_vals = gate_vals / jnp.clip(jnp.sum(gate_vals, axis=-1, keepdims=True), 1e-09)
        counts = jnp.zeros((E,), jnp.int32)
        disp = jnp.zeros((E, C, D), x.dtype)
        pos_safe_l, valid_l = ([], [])
        for s in range(K):
            mask = jax.nn.one_hot(idx[:, s], E, dtype=jnp.int32)
            loc = jnp.cumsum(mask, axis=0) - 1 + counts[None, :]
            pos = jnp.sum(loc * mask, axis=-1)
            counts = counts + jnp.sum(mask, axis=0)
            valid = pos < C
            pos_safe = jnp.where(valid, pos, 0)
            disp = disp.at[idx[:, s], pos_safe].add(xt * valid[:, None].astype(x.dtype))
            pos_safe_l.append(pos_safe)
            valid_l.append(valid)
        h = jax.nn.gelu(jnp.einsum('ecd,edh->ech', disp, fc1_w) + fc1_b[:, None, :], approximate=False)
        eo = jnp.einsum('ech,ehd->ecd', h, fc2_w) + fc2_b[:, None, :]
        y = jnp.zeros((S, D), x.dtype)
        for s in range(K):
            g = (gate_vals[:, s] * valid_l[s].astype(gate_vals.dtype)).astype(x.dtype)
            y = y + g[:, None] * eo[idx[:, s], pos_safe_l[s]]
        return y.reshape(B, L, D)
    x = x + _L0_attn_ref(_L0_cond_ref(x, fside_BxSxS_0, fside_BxSxS_0, L0_cond_w, L0_cond_u, cond_512), L0_attn_Wq, L0_attn_bq, L0_attn_Wk, L0_attn_bk, L0_attn_Wv, L0_attn_bv, L0_attn_Wo, L0_attn_bo)
    x = x + _L0_ffn_ref(_L0_cond2_ref(x, fside_BxSxS_0, fside_BxSxS_0, L0_cond2_w, L0_cond2_u, cond_512), L0_ffn_W1, L0_ffn_b1, L0_ffn_W2, L0_ffn_b2)
    x = x + _L1_attn_ref(_L1_cond_ref(x, fside_BxSxS_0, fside_BxSxS_0, L1_cond_w, L1_cond_u, cond_512), L1_attn_Wq, L1_attn_Wk, L1_attn_Wv, L1_attn_Wb, L1_attn_bb, L1_attn_Wo)
    x = x + _L1_ffn_ref(_L1_cond2_ref(x, fside_BxSxS_0, fside_BxSxS_0, L1_cond2_w, L1_cond2_u, cond_512), L1_ffn_wg, L1_ffn_fc1_w, L1_ffn_fc1_b, L1_ffn_fc2_w, L1_ffn_fc2_b)
    return x

_drawn_inputs = setup_inputs


def setup_inputs(seed=0):
    import zlib

    import numpy as np

    out = dict(_drawn_inputs(seed))
    spreads = {'L1_attn_bb': (0.0, 0.1), 'L1_ffn_fc1_b': (0.0, 0.438), 'L1_ffn_fc2_b': (0.0, 0.1)}
    factors = {'L0_attn_Wq': 4.617,
     'L0_attn_bq': 8.0,
     'L0_attn_Wk': 4.447,
     'L0_attn_bk': 8.0,
     'L1_attn_Wq': 4.779,
     'L1_attn_Wk': 4.706}
    for name, (base, spread) in spreads.items():
        noise = np.random.default_rng([zlib.crc32(name.encode()), seed]).standard_normal(out[name].shape)
        drawn = base * np.exp(spread * noise) if base else spread * noise
        out[name] = jnp.asarray(drawn.astype(out[name].dtype))
    for name, factor in factors.items():
        out[name] = (out[name] * factor).astype(out[name].dtype)
    return out
```

```python
from contextlib import ExitStack

import numpy as np

import concourse.bass as bass
from concourse import mybir

F32 = mybir.dt.float32
BF16 = mybir.dt.bfloat16
I32 = mybir.dt.int32
ALU = mybir.AluOpType
ACT = mybir.ActivationFunctionType
AX = mybir.AxisListType

P = 128
B, T, D = 4, 256, 256
N = B * T
CT = D // P
H = 16
HD = D // H
HALF = HD // 2
QT = T // P
VW = HD + 1
GH = 4
NG = H // GH
HID = 1024
MT = HID // P
E = 8
CAP = 2 * N // E
TD = 64
NT = N // P
BLK = 32
NB = P // BLK
PAIRS_Q = (0, 0, 1, 1, 0, 2)
PAIRS_K = (0, 1, 0, 1, 2, 0)
SROWS = len(PAIRS_Q) * HD
MROWS = SROWS + 2
MASKED = -1e30
NO_KEY = 1e20
TWO_BF16_ONES = float(np.array([0x3F803F80], np.uint32).view(np.float32)[0])
EXP30 = float(np.exp(np.float32(30.0)))
ROUND = 12582912.0
QMAX = 7.0
THRESHOLD = 0.05
SCORE_SCALE = 1.0 / HD ** 0.5

RINGS = {
    "proj": ("big", ("act", "dve")), "scores": ("big", ("dve",)), "probs": ("big", ("act",)),
    "kscores": ("big", ("dve",)), "kprobs": ("big", ("act",)),
    "oT": ("big", ("act",)), "wo": ("big", ("dve",)),
    "fc1": ("big", ("act",)), "fc2": ("big", ("act",)),
    "w1": None,
    "ytok": ("big", ("act",)), "xtok": ("big", ("dve",)), "dispT": ("big", ("dve",)),
    "up": ("big", ("act",)), "down": ("big", ("dve",)),
    "max": ("small", ("act",)), "kmax": ("small", ("act",)), "pv": ("small", ("dve",)),
    "beta": ("small", ("dve",)), "den": ("small", ("dve",)),
    "gather": ("small", ("dve",)), "solve": ("small", ("dve",)),
    "route": ("small", ("dve",)), "rank": ("small", ("dve",)),
}


def make_order():
    o = []
    o += [("wkv", 0, 0), ("gate", 0, 0), ("proj", 0, 0), ("wkv", 0, 1), ("gate", 0, 1), ("proj", 0, 1)]
    o += [("scores", 0, 0, j) for j in range(NG)] + [("max", 0, 0)]
    o += [("wkv", 0, 2), ("wkv", 0, 3), ("ternary", 0), ("ternary", 1)]
    for b in range(B):
        for j in range(NG):
            if b + 1 < B:
                o.append(("scores", 0, b + 1, j))
            o.append(("probs", 0, b, j))
        if b + 1 < B:
            o.append(("max", 0, b + 1))
        if b + 2 < B:
            o += [("gate", 0, b + 2), ("proj", 0, b + 2)]
        o += [("pv", 0, b, 0), ("pv", 0, b, 1), ("wkv", 1, b), ("oT", 0, b), ("wo", 0, b), ("gate", 1, b),
              ("wkv", 2, b)]
    o += [("fc1", h, m) for h in range(2) for m in range(MT)]
    o += [("fc2", h, c) for h in range(2) for c in range(CT)]
    o += [("wkv", 3, b) for b in range(B)]
    o += [("quant",)] + [("requant", b) for b in range(B)]
    o += [("gate", 2, 0), ("proj", 1, 0), ("beta", 0)]
    o += [("kscores", 1, 0, j) for j in range(NG)] + [("kmax", 1, 0)]
    o += [("gate", 2, 1), ("proj", 1, 1), ("beta", 1)]
    o += [("kprobs", 1, 0, j) for j in range(NG)] + [("den", 0), ("blocks", 0)]
    for b in range(B):
        groups = [("scores", 1, b, j) for j in range(NG)] + [("max", 1, b)]
        if b + 1 < B:
            groups += [("kscores", 1, b + 1, j) for j in range(NG)] + [("kmax", 1, b + 1)]
        groups += [("probs", 1, b, j) for j in range(NG)]
        if b + 1 < B:
            groups += [("kprobs", 1, b + 1, j) for j in range(NG)]
        solve = [("inverse", b)]
        for s in range(QT * NB):
            if s:
                solve.append(("gather", b, s))
            solve.append(("solve", b, s))
        steps = []
        while groups or solve:
            if solve:
                steps.append(solve.pop(0))
            if groups:
                steps.append(groups.pop(0))
        o += steps
        if b + 1 < B:
            o += [("den", b + 1), ("blocks", b + 1)]
        if b + 2 < B:
            o += [("gate", 2, b + 2), ("proj", 1, b + 2), ("beta", b + 2)]
        o += [("pv", 1, b, 0), ("pv", 1, b, 1), ("oT", 1, b), ("wo", 1, b), ("gate", 3, b)]
    o += [("route",)] + [("ytok", i) for i in range(B)] + [("rank",)] + [("xtok", i) for i in range(B)]
    o += [("dispT", 0)]
    for e in range(E):
        o += [("up", e, 0), ("up", e, 1)]
        if e + 1 < E:
            o.append(("dispT", e + 1))
        o.append(("down", e))
    o += [("combine", t) for t in range(NT)]
    return o


ORDER = make_order()


def count_rings():
    seen = {"big": 0, "small": 0}
    freed = {(r, s, e): 0 for r in seen for s in range(2) for e in ("act", "dve")}
    out = {}
    for step in ORDER:
        use = RINGS.get(step[0])
        if use is None:
            continue
        ring, engines = use
        n = seen[ring]
        slot = n % 2
        out[step] = (ring, slot, n, {e: freed[ring, slot, e] for e in ("act", "dve")})
        seen[ring] += 1
        for e in engines:
            freed[ring, slot, e] += 1
    return out


USE = count_rings()
NUMBER = {}
for _step in ORDER:
    NUMBER[_step] = sum(1 for s in NUMBER if s[0] == _step[0])

CONSTS = {"ident": P, "tri": P, "ones": P, "cos": T, "sin": CT * T, "masks": 4 * P, "rev": E,
          "trash": 2 * NT}
CONST_W = sum(CONSTS.values())
CONST_AT = {}
_at = 0
for _k, _w in CONSTS.items():
    CONST_AT[_k] = _at
    _at += _w
COLS = {"w": 4 * CT, "u": 4 * CT, "bq": CT, "bk": CT, "bo": CT, "b1": MT, "b2": CT, "fb1": E * MT}
COL_W = sum(COLS.values())
COL_AT = {}
_at = 0
for _k, _w in COLS.items():
    COL_AT[_k] = _at
    _at += _w


def program(nc, d):
    with ExitStack() as ctx:
        def sem(name):
            return ctx.enter_context(nc.semaphore(name))

        words = (nc.sbuf_usable_end - nc.sbuf_base) // 4 - 16
        arena = ctx.enter_context(nc.sbuf_tensor("arena", [P, words], F32))
        psum = ctx.enter_context(nc.psum_tensor("psum", [P, 8, 512], F32))
        top = [0]

        def take(n, at=None):
            if at is None:
                at, top[0] = top[0], top[0] + n
                assert top[0] <= words, (top[0], words)
            return arena[:, at:at + n]

        def v3(ap, a):
            return ap.rearrange("p (a b) -> p a b", a=a)

        const = take(CONST_W)
        c_ = {k: const[:, CONST_AT[k]:CONST_AT[k] + w] for k, w in CONSTS.items()}
        ident, tri, ones = c_["ident"], c_["tri"], c_["ones"]
        cols = take(COL_W)
        col = {k: cols[:, COL_AT[k]:COL_AT[k] + w] for k, w in COLS.items()}
        identb = take(P // 2).bitcast(BF16)
        maskb = take(4 * P // 2).bitcast(BF16).rearrange("p (a b) -> p a b", a=4)
        QK, KQ, QK_STRICT, KQ_STRICT = range(4)
        tf = take(4 * B)
        dec = take(4 * CT * B)
        bvb = take(D)
        bbb = take(H)
        small = take(80)

        xT = v3(take(CT * N), CT)
        G = [v3(take(CT * N), CT) for _ in range(2)]
        wq, wk, wv, wo = (v3(take(CT * D), CT) for _ in range(4))
        wb = v3(take(CT * H), CT)
        th = v3(take(CT * T), CT)
        cond = v3(th[:, 0, :], B)

        r1 = top[0]
        stack = {}
        for name in ("q", "k", "kq"):
            for par in range(2):
                stack[name, par] = take(H * T // 2).bitcast(BF16).rearrange("p (h t) -> p h t", h=H)
        hid = v3(take(MT * N, at=r1), MT)
        ffn = v3(take(CT * N, at=r1 + MT * N), CT)

        part = {o: take(3 * CT * T // 2).bitcast(BF16).rearrange("p (a c t) -> p a c t", a=3, c=CT)
                for o in ("q", "k")}
        qf = {o: v3(take(CT * T), CT) for o in ("q", "k")}
        rest = v3(take(CT * T), CT)
        vaug = [take(QT * H * VW).rearrange("p (t h e) -> p t h e", t=QT, h=H) for _ in range(2)]
        uaug = [take(QT * H * VW).rearrange("p (t h e) -> p t h e", t=QT, h=H) for _ in range(2)]
        prob = take(H * (T + P)).rearrange("p (h t) -> p h t", h=H)
        otok = v3(take(QT * D), QT)
        oT = v3(take(CT * T), CT)
        mneg = take(QT * H)
        mpart = take(2 * QT * H // 2).bitcast(BF16)
        mT = [take(P // 2).bitcast(BF16) for _ in range(2)]
        rec = take(QT * 8)

        r2 = top[0]
        fsT, ek, ekv = (v3(take(CT * N), CT) for _ in range(3))
        scan = [v3(take(CT * T), CT) for _ in range(4)]
        euk, gk = (v3(take(CT * T), CT) for _ in range(2))
        w1 = v3(take(CT * HID), CT)
        w2 = v3(take(MT * D), MT)
        e_end = top[0]
        top[0] = r2
        kprob = [take(H * (T + P)).rearrange("p (h t) -> p h t", h=H) for _ in range(2)]
        blkA = take(BLK * BLK)
        blkX = take(BLK * BLK)
        blkT = take(BLK * BLK // 4)
        invT = [take(BLK * BLK) for _ in range(2)]
        cT = take(BLK)
        beta = [take(QT * H) for _ in range(2)]
        cc = [take(QT * H) for _ in range(2)]
        zz, zt = (c_["masks"][:, i * D:(i + 1) * D] for i in range(2))
        top[0] = max(top[0], e_end)

        top_all = top[0]
        top[0] = r1
        fcw = [(v3(take(CT * HID), CT), v3(take(MT * D), MT)) for _ in range(2)]
        hE = [v3(take(MT * CAP), MT) for _ in range(2)]
        b2b = v3(take(E * D), E)
        ytok = v3(take(NT * D), NT)
        xtok = v3(take(NT * D), NT)
        dtok = [v3(take(2 * D), 2) for _ in range(2)]
        dT = [v3(take(CT * CAP), CT) for _ in range(2)]
        eo = [v3(take(2 * D), 2) for _ in range(2)]
        got = [v3(take(NT * D), NT) for _ in range(2)]
        outt = v3(take(NT * D), NT)
        rt = take(24 * NT * E)
        idx = take(4 * NT).bitcast(I32)
        zero = take(D)
        assert top[0] <= words, (top[0], words)
        top[0] = max(top[0], top_all)

        rows_order = [s for s in ORDER if s[0] in ("max", "kmax")]
        tern_flat = take(2 * 2048, at=r1 + 4 * (H * T // 2))

        def tern_tmp(i):
            return v3(tern_flat[:, i * 2048:(i + 1) * 2048], (CT, MT)[i])

        def x_count(g, b):
            return (g - 1) * B + b + 1

        def stack_count(name, layer, b):
            n = b // 2 + 1
            if layer and name != "kq":
                n += B // 2
            return 16 * len(PAIRS_Q) * CT * n

        def row_count(name, layer, b):
            n = b // 2 + 1
            if layer and name == "q":
                n += B // 2
            return 16 * 2 * QT * n

        R = {}
        rt_at = [0]

        def ra(n):
            rt_at[0] += n
            return rt[:, rt_at[0] - n:rt_at[0]]
        for k in ("logit", "exp", "score", "score2", "t1"):
            R[k] = ra(NT * E)
        for k in ("oh", "pre"):
            R[k] = [ra(NT * E) for _ in range(2)]
        for k in ("mx", "sum", "rec"):
            R[k] = ra(NT)
        for k in ("m", "key", "gate", "pos", "valid", "slot", "tmp", "base"):
            R[k] = [ra(NT) for _ in range(2)]
        idx_s = [idx[:, s * NT:(s + 1) * NT] for s in range(2)]
        idx_g = [idx[:, (2 + s) * NT:(3 + s) * NT] for s in range(2)]

        def big(slot, bank):
            return psum[:, 3 * slot + bank, :]

        def wide(slot):
            return psum[:, 3 * slot:3 * slot + 2, :]

        def single(slot):
            return psum[:, 6 + slot, :]

        loaded = {k: sem(f"loaded_{k}") for k in
                  ("const", "cond", "fs", "x", "att0", "tern", "att1")}
        written = {"big": sem("big_psum_written"), "small": sem("small_psum_written")}
        freed = {(r, s, e): sem(f"{r}_slot{s}_freed_by_{e}")
                 for r in ("big", "small") for s in range(2) for e in ("act", "dve")}
        act_own, dve_own, pool_own = sem("act_steps"), sem("dve_steps"), sem("pool_steps")
        ones_ready = sem("ones_rows_ready")
        consts_ready = sem("consts_ready")
        exps_ready = sem("exps_ready")
        ek_ready = sem("ek_ready")
        euk_ready = sem("euk_ready")
        euk_used = sem("euk_used")
        gate_ready = sem("gate_ready")
        tanh_ready = sem("tanh_ready")
        gated = sem("gated")
        x_ready = sem("x_ready")
        split_from = sem("operands_ready")
        v_by_act = sem("values_ready_act")
        parts_ready = sem("parts_ready")
        v_ready = sem("values_ready")
        stacked = {(o, p): sem(f"stacked_{o}{p}") for o in ("q", "k", "kq") for p in range(2)}
        parts_used = sem("parts_stacked")
        mparts_ready = sem("max_parts_ready")
        mT_ready = sem("max_rows_ready")
        mrows = {(o, p): sem(f"max_rows_{o}{p}") for o in ("q", "kq") for p in range(2)}
        probs_ready = sem("probs_ready")
        kprobs_ready = sem("kprobs_ready")
        o_ready = sem("attended")
        oT_ready = sem("attended_T")
        tern_in = sem("ternary_abs")
        tern_max = sem("ternary_max")
        tern_sum_in = sem("ternary_sums_in")
        tern_sum = sem("ternary_sums")
        tern_abs = sem("ternary_absolute")
        tern_cnt = sem("ternary_counts")
        tern_ready = sem("ternary_ready")
        hid_ready = sem("hidden_ready")
        ffn_ready = sem("ffn_ready")
        amax_in, amax_out = sem("quant_max_in"), sem("quant_max_out")
        blocks_ready = sem("blocks_ready")
        inv_ready = sem("inverses_ready")
        invT_ready = sem("inverses_T_ready")
        z_ready = sem("rhs_ready")
        u_ready = sem("solved_ready")
        coef_ready = sem("coefficients_ready")
        zeroed = sem("zero_rows_ready")
        disp_zero = sem("dispatch_zeroed")
        ytok_ready, xtok_ready = sem("ytok_ready"), sem("xtok_ready")
        logits_exp_in, logits_exp = sem("logits_in"), sem("logits_exp")
        choice_ready = sem("choice_ready")
        rt_ready = sem("indices_ready")
        scattered = sem("scattered")
        w_loaded = [sem(f"expert_weights_{i}") for i in range(2)]
        b2_loaded = sem("expert_bias_loaded")
        dtok_loaded = [sem(f"dispatched_{i}") for i in range(2)]
        dT_ready = sem("dispatched_T")
        hE_ready = sem("expert_hidden")
        eo_ready = sem("expert_out")
        eo_stored = [sem(f"expert_out_stored_{i}") for i in range(2)]
        gathered = sem("gathered")
        out_ready = sem("out_ready")
        stored = sem("out_stored")

        block = ctx.enter_context(nc.Block())

        def bt(b):
            return slice(b * T, (b + 1) * T)

        def n_before(step, kind=None):
            return NUMBER[step]

        @block.sync
        def _(sp):
            sp.dma_start(const, d["consts"]).then_inc(loaded["const"], 16)
            sp.dma_start(cols, d["columns"]).then_inc(loaded["const"], 16)
            sp.dma_start(cond, d["cond"].rearrange("(o b) t -> o b t", o=1).to_broadcast([P, B, TD])).then_inc(loaded["cond"], 16)
            sp.dma_start(fsT, d["fsT"]).then_inc(loaded["fs"], 16)
            sp.dma_start(xT, d["xT"]).then_inc(loaded["x"], 16)
            for w_, n_ in ((wq, "wq0"), (wk, "wk0"), (wv, "wv0"), (wo, "wo0")):
                sp.dma_start(w_, d[n_]).then_inc(loaded["att0"], 16)
            sp.dma_start(bvb, d["bv"].rearrange("(o c) -> o c", o=1).to_broadcast([P, D])).then_inc(loaded["att0"], 16)
            sp.dma_start(bbb, d["bb"].rearrange("(o c) -> o c", o=1).to_broadcast([P, H])).then_inc(loaded["att0"], 16)
            sp.dma_start(wb, d["wb"]).then_inc(loaded["att0"], 16)
            sp.dma_start(w1, d["w1T"]).then_inc(loaded["tern"], 16)
            sp.dma_start(w2, d["w2T"]).then_inc(loaded["tern"], 16)

            n_stack = {k: 0 for k in stacked}
            n_rows = 0
            experts_loaded = 0

            def load_expert(e):
                if e >= 2:
                    sp.wait_ge(written["big"], USE["down", e - 2][2] + 1)
                sp.dma_start(fcw[e % 2][0], d["fc1"][e]).then_inc(w_loaded[e % 2], 16)
                sp.dma_start(fcw[e % 2][1], d["fc2"][e]).then_inc(w_loaded[e % 2], 16)

            def load_dispatched(e):
                if e >= 2:
                    sp.wait_ge(written["big"], USE["dispT", e - 2][2] + 1)
                sp.dma_start(dtok[e % 2], d["disp"][e * CAP:(e + 1) * CAP, :].rearrange("(s p) c -> p s c", p=P)
                             ).then_inc(dtok_loaded[e % 2], 16)

            for step in ORDER:
                kind = step[0]
                if kind == "proj":
                    _, layer, b = step
                    par = b % 2
                    n = n_before(step)
                    sp.wait_ge(parts_ready, n + 1)
                    if b >= 2:
                        sp.wait_ge(written["big"], USE["probs", layer, b - 2, NG - 1][2] + 1)
                    elif layer == 1:
                        sp.wait_ge(written["big"], USE["probs", 0, b + 2, NG - 1][2] + 1)
                    names = [("q", "q", PAIRS_Q), ("k", "k", PAIRS_K)] + ([("kq", "k", PAIRS_Q)] if layer else [])
                    for name, src, pairs in names:
                        for g, pt in enumerate(pairs):
                            for ct in range(CT):
                                r = g * HD + ct * HALF
                                sp.dma_start(stack[name, par][r:r + HALF, :, :], part[src][:, pt, ct, :]
                                             ).then_inc(stacked[name, par], 16)
                                n_stack[name, par] += 16
                    for name, _, _ in names:
                        sp.wait_ge(stacked[name, par], n_stack[name, par])
                    sp.nop().then_inc(parts_used, 1)
                elif kind in ("max", "kmax"):
                    _, layer, b = step
                    name = "q" if kind == "max" else "kq"
                    sp.wait_ge(mT_ready, rows_order.index(step) + 1)
                    src = mT[rows_order.index(step) % 2]
                    for pt in range(2):
                        for t in range(QT):
                            r = (pt * QT + t) * H
                            sp.dma_start(stack[name, b % 2][SROWS + pt:SROWS + pt + 1, :, t * P:(t + 1) * P],
                                         src[r:r + H, :]).then_inc(mrows[name, b % 2], 16)
                elif kind == "route":
                    sp.wait_ge(gated, NUMBER["gate", 3, B - 1] + 1)
                    load_expert(0)
                    load_expert(1)
                    sp.dma_start(b2b, d["fb2"].rearrange("(o e) c -> o e c", o=1).to_broadcast([P, E, D])).then_inc(b2_loaded, 16)
                    sp.wait_ge(zeroed, 1)
                    sp.dma_start(d["disp"][0:E * CAP, :].rearrange("(p a) c -> p a c", p=P),
                                 zero[:, :].unsqueeze(1).to_broadcast([P, E * CAP // P, D])).then_inc(disp_zero, 16)
                elif kind == "dispT":
                    if step[1] == 0:
                        sp.wait_ge(scattered, 16 * 2 * NT)
                        load_dispatched(0)
                        load_dispatched(1)
                elif kind == "down":
                    e = step[1]
                    if e + 2 < E:
                        load_dispatched(e + 2)
                        load_expert(e + 2)
                    sp.wait_ge(eo_ready, e + 1)
                    sp.dma_start(d["eo"][e * CAP:(e + 1) * CAP, :].rearrange("(s p) c -> p s c", p=P), eo[e % 2]
                                 ).then_inc(eo_stored[e % 2], 16)
                elif kind == "combine":
                    t = step[1]
                    sp.wait_ge(out_ready, t + 1)
                    sp.dma_start(d["out"][t * P:(t + 1) * P, :], outt[:, t, :]).then_inc(stored, 16)
            sp.wait_ge(stored, 16 * NT)

        @block.tensor
        def _(pe):
            def acquire(step):
                ring, slot, n, before = USE[step]
                for e in ("act", "dve"):
                    if before[e]:
                        pe.wait_ge(freed[ring, slot, e], before[e])
                return slot

            def mm(out, lhsT, rhs, start=True, stop=True):
                return nc.tensor.matmul(out, lhsT, rhs, start=start, stop=stop)

            def wrote(step, ins):
                ins.then_inc(written[USE[step][0]], 1)

            count = {}
            for step in ORDER:
                kind = step[0]
                i = count.get(kind, 0)
                count[kind] = i + 1
                if kind == "proj":
                    _, layer, b = step
                    g = 0 if layer == 0 else 2
                    pe.wait_ge(gated, NUMBER["gate", g, b] + 1)
                    if b == 0:
                        pe.wait_ge(loaded[f"att{layer}"], 16 * (7 if layer == 0 else 4))
                    slot = acquire(step)
                    y = G[g % 2]
                    for bank, w_ in ((0, wq), (1, wk)):
                        for co in range(CT):
                            for ci in range(CT):
                                mm(big(slot, bank)[:, co * T:(co + 1) * T], w_[:, ci, co * P:(co + 1) * P],
                                   y[:, ci, bt(b)], ci == 0, ci == CT - 1)
                    for t in range(QT):
                        for ci in range(CT):
                            tok = b * T + t * P
                            last = mm(big(slot, 2)[:, t * D:(t + 1) * D], y[:, ci, tok:tok + P], wv[:, ci, :],
                                      ci == 0, ci == CT - 1)
                    wrote(step, last)
                elif kind == "beta":
                    b = step[1]
                    slot = acquire(step)
                    for t in range(QT):
                        for ci in range(CT):
                            tok = b * T + t * P
                            last = mm(single(slot)[:, t * H:(t + 1) * H], G[0][:, ci, tok:tok + P], wb[:, ci, :],
                                      ci == 0, ci == CT - 1)
                    wrote(step, last)
                elif kind in ("scores", "kscores"):
                    _, layer, b, j = step
                    par = b % 2
                    qn = "q" if kind == "scores" else "kq"
                    if j == 0:
                        pe.wait_ge(stacked[qn, par], stack_count(qn, layer, b))
                        pe.wait_ge(stacked["k", par], stack_count("k", layer, b))
                        if i == 0 and kind == "scores":
                            pe.wait_ge(consts_ready, 1)
                    slot = acquire(step)
                    q_, k_ = stack[qn, par], stack["k", par]
                    mask = maskb[:, QK if kind == "scores" else QK_STRICT, :]
                    for jj in range(GH):
                        h = j * GH + jj
                        out = wide(slot)[:, jj // 2, (jj % 2) * T:(jj % 2 + 1) * T]
                        mm(out, q_[0:SROWS, h, P:T], k_[0:SROWS, h, 0:T], True, False)
                        mm(out[:, P:T], identb, mask, False, True)
                    for jj in range(GH):
                        h = j * GH + jj
                        out = big(slot, 2)[:, jj * P:(jj + 1) * P]
                        mm(out, q_[0:SROWS, h, 0:P], k_[0:SROWS, h, 0:P], True, False)
                        last = mm(out, identb, mask, False, True)
                    wrote(step, last)
                elif kind in ("max", "kmax"):
                    n = rows_order.index(step)
                    pe.wait_ge(mparts_ready, n + 1)
                    slot = acquire(step)
                    out = single(slot)[:, 0:P // 2].bitcast(BF16)
                    wrote(step, nc.tensor.transpose(out[0:2 * QT * H, :], mpart, identb))
                elif kind in ("probs", "kprobs"):
                    _, layer, b, j = step
                    par = b % 2
                    qn = "q" if kind == "probs" else "kq"
                    if j == 0:
                        pe.wait_ge(mrows[qn, par], row_count(qn, layer, b))
                        if b == 0:
                            pe.wait_ge(ones_ready, 2 * (layer + 1))
                    slot = acquire(step)
                    q_, k_ = stack[qn, par], stack["k", par]
                    mask = maskb[:, KQ if kind == "probs" else KQ_STRICT, :]
                    for jj in range(GH):
                        h = j * GH + jj
                        out = wide(slot)[:, jj // 2, (jj % 2) * T:(jj % 2 + 1) * T]
                        mm(out, k_[0:MROWS, h, 0:P], q_[0:MROWS, h, 0:T], True, False)
                        mm(out[:, 0:P], identb, mask, False, True)
                    for jj in range(GH):
                        h = j * GH + jj
                        out = big(slot, 2)[:, jj * P:(jj + 1) * P]
                        mm(out, k_[0:MROWS, h, P:T], q_[0:MROWS, h, P:T], True, False)
                        last = mm(out, identb, mask, False, True)
                    wrote(step, last)
                elif kind == "pv":
                    _, layer, b, half = step
                    pe.wait_ge(probs_ready, NUMBER["probs", layer, b, 2 * half + 1] + 1)
                    if layer == 0:
                        pe.wait_ge(v_ready, NUMBER["proj", 0, b] + 1)
                        val = vaug[b % 2]
                    else:
                        pe.wait_ge(u_ready, QT * NB * (b + 1))
                        val = uaug[b % 2]
                    slot = acquire(step)
                    out = single(slot)[:, 0:QT * 8 * VW].rearrange("p (t h e) -> p t h e", t=QT, h=8)
                    for hh in range(8):
                        h = half * 8 + hh
                        mm(out[:, 0, hh, :], prob[:, h, 0:P], val[:, 0, h, :])
                        mm(out[:, 1, hh, :], prob[:, h, P:T], val[:, 0, h, :], True, False)
                        last = mm(out[:, 1, hh, :], prob[:, h, T:T + P], val[:, 1, h, :], False, True)
                    wrote(step, last)
                elif kind == "oT":
                    _, layer, b = step
                    pe.wait_ge(o_ready, 2 * (layer * B + b) + 2)
                    slot = acquire(step)
                    out = v3(big(slot, 0), CT)
                    for ct in range(CT):
                        for t in range(QT):
                            last = nc.tensor.transpose(out[:, ct, t * P:(t + 1) * P], otok[:, t, ct * P:(ct + 1) * P],
                                                       ident)
                    wrote(step, last)
                elif kind == "wo":
                    _, layer, b = step
                    pe.wait_ge(oT_ready, layer * B + b + 1)
                    slot = acquire(step)
                    out = v3(big(slot, 0), CT)
                    for co in range(CT):
                        for ci in range(CT):
                            last = mm(out[:, co, :], wo[:, ci, co * P:(co + 1) * P], oT[:, ci, :],
                                      ci == 0, ci == CT - 1)
                    wrote(step, last)
                elif kind == "fc1":
                    _, h, m = step
                    if i == 0:
                        pe.wait_ge(gated, NUMBER["gate", 1, B - 1] + 1)
                        pe.wait_ge(tern_ready, 2)
                    slot = acquire(step)
                    for ci in range(CT):
                        last = mm(big(slot, 0), w1[:, ci, m * P:(m + 1) * P], G[1][:, ci, h * 512:(h + 1) * 512],
                                  ci == 0, ci == CT - 1)
                    wrote(step, last)
                elif kind == "fc2":
                    _, h, c = step
                    pe.wait_ge(hid_ready, MT * (h + 1))
                    slot = acquire(step)
                    for m in range(MT):
                        last = mm(big(slot, 0), w2[:, m, c * P:(c + 1) * P], hid[:, m, h * 512:(h + 1) * 512],
                                  m == 0, m == MT - 1)
                    wrote(step, last)
                elif kind == "den":
                    b = step[1]
                    pe.wait_ge(kprobs_ready, NG * (b + 1))
                    slot = acquire(step)
                    kp = kprob[b % 2]
                    for h in range(H):
                        mm(single(slot)[:, h:h + 1], kp[:, h, 0:P], ones[:, 0:1])
                        out = single(slot)[:, H + h:H + h + 1]
                        mm(out, kp[:, h, P:T], ones[:, 0:1], True, False)
                        last = mm(out, kp[:, h, T:T + P], ones[:, 0:1], False, True)
                    wrote(step, last)
                elif kind == "gather":
                    _, b, s = step
                    t, r = divmod(s, NB)
                    pe.wait_ge(u_ready, QT * NB * b + s)
                    slot = acquire(step)
                    kp, u = kprob[b % 2], uaug[b % 2]
                    rows = slice(r * BLK, (r + 1) * BLK)
                    for h in range(H):
                        out = single(slot)[rows, h * HD:(h + 1) * HD]
                        if t == 0:
                            last = mm(out, kp[0:r * BLK, h, rows], u[0:r * BLK, 0, h, 0:HD])
                        else:
                            last = mm(out, kp[:, h, P + r * BLK:P + (r + 1) * BLK], u[:, 0, h, 0:HD], True, r == 0)
                            if r:
                                last = mm(out, kp[0:r * BLK, h, T + r * BLK:T + (r + 1) * BLK],
                                          u[0:r * BLK, 1, h, 0:HD], False, True)
                    wrote(step, last)
                elif kind == "solve":
                    _, b, s = step
                    t, r = divmod(s, NB)
                    if s == 0:
                        pe.wait_ge(invT_ready, b + 1)
                    pe.wait_ge(z_ready, QT * NB * b + s + 1)
                    slot = acquire(step)
                    rows = slice(r * BLK, (r + 1) * BLK)
                    for h in range(H):
                        n = t * H + h
                        last = mm(single(slot)[rows, h * HD:(h + 1) * HD], invT[b % 2][rows, n * BLK:(n + 1) * BLK],
                                  zz[rows, h * HD:(h + 1) * HD])
                    wrote(step, last)
                elif kind == "route":
                    pe.wait_ge(gated, NUMBER["gate", 3, B - 1] + 1)
                    slot = acquire(step)
                    wg = wb[:, :, 0:E]
                    pe.wait_ge(loaded["att1"], 16 * 5)
                    for t in range(NT):
                        for ci in range(CT):
                            last = mm(single(slot)[:, t * E:(t + 1) * E], G[1][:, ci, t * P:(t + 1) * P], wg[:, ci, :],
                                      ci == 0, ci == CT - 1)
                    wrote(step, last)
                elif kind in ("ytok", "xtok"):
                    n = step[1]
                    slot = acquire(step)
                    src = G[1] if kind == "ytok" else xT
                    out = big(slot, 0).rearrange("p (t c) -> p t c", t=2)
                    for t in range(2):
                        for ct in range(CT):
                            tok = (2 * n + t) * P
                            last = nc.tensor.transpose(out[:, t, ct * P:(ct + 1) * P], src[:, ct, tok:tok + P], ident)
                    wrote(step, last)
                elif kind == "rank":
                    pe.wait_ge(choice_ready, 1)
                    slot = acquire(step)
                    for s in range(2):
                        out = single(slot)[:, s * NT * E:(s + 1) * NT * E]
                        mm(out, tri, R["oh"][s], True, False)
                        last = mm(out, ones, R["pre"][s], False, True)
                    wrote(step, last)
                elif kind == "dispT":
                    e = step[1]
                    pe.wait_ge(dtok_loaded[e % 2], 16 * (e // 2 + 1))
                    slot = acquire(step)
                    out = v3(big(slot, 0), CT)
                    for ct in range(CT):
                        for s in range(2):
                            last = nc.tensor.transpose(out[:, ct, s * P:(s + 1) * P], dtok[e % 2][:, s, ct * P:(ct + 1) * P],
                                                       ident)
                    wrote(step, last)
                elif kind == "up":
                    _, e, half = step
                    if half == 0:
                        pe.wait_ge(dT_ready, e + 1)
                        pe.wait_ge(w_loaded[e % 2], 32 * (e // 2 + 1))
                    slot = acquire(step)
                    out = wide(slot).rearrange("p a (m t) -> p (a m) t", m=2)
                    for mm_ in range(MT // 2):
                        m = half * (MT // 2) + mm_
                        for ci in range(CT):
                            last = mm(out[:, mm_, :], fcw[e % 2][0][:, ci, m * P:(m + 1) * P], dT[e % 2][:, ci, :],
                                      ci == 0, ci == CT - 1)
                    wrote(step, last)
                elif kind == "down":
                    e = step[1]
                    pe.wait_ge(hE_ready, 2 * e + 2)
                    slot = acquire(step)
                    out = v3(big(slot, 0), 2)
                    for s in range(2):
                        for m in range(MT):
                            last = mm(out[:, s, :], hE[e % 2][:, m, s * P:(s + 1) * P], fcw[e % 2][1][:, m, :],
                                      m == 0, m == MT - 1)
                    wrote(step, last)

        @block.scalar
        def _(act):
            own = [0]

            def step_(ins):
                own[0] += 1
                ins.then_inc(act_own, 1)

            def settle():
                act.wait_ge(act_own, own[0])

            def filled(step):
                ring, slot, n, before = USE[step]
                act.wait_ge(written[ring], n + 1)
                return slot

            def give_back(step, ins):
                ring, slot, n, before = USE[step]
                ins.then_inc(freed[ring, slot, "act"], 1)

            A = nc.scalar.activation
            act.wait_ge(exps_ready, 1)
            A(tf[:, B:2 * B], tf[:, 0:B], ACT.Exp, scale=-1.0).then_inc(ek_ready, 1)
            act.wait_ge(loaded["const"], 32)
            A(small[:, 0:4 * CT], col["w"], ACT.Exp).then_inc(ek_ready, 1)
            act.wait_ge(exps_ready, 2)
            A(ek, ekv, ACT.Exp).then_inc(ek_ready, 1)
            act.wait_ge(exps_ready, 3)
            A(dec, dec, ACT.Exp).then_inc(ek_ready, 1)

            for step in ORDER:
                kind = step[0]
                if kind == "wkv":
                    _, c, b = step
                    n = NUMBER[step]
                    if n == 0:
                        act.wait_ge(loaded["fs"], 16)
                    else:
                        act.wait_ge(euk_used, n)
                    for ct in range(CT):
                        A(euk[:, ct, :], fsT[:, ct, bt(b)], ACT.Exp, bias=col["u"][:, c * CT + ct:c * CT + ct + 1]
                          ).then_inc(euk_ready, 1)
                elif kind == "gate":
                    _, g, b = step
                    n = NUMBER[step]
                    if n == 0:
                        act.wait_ge(loaded["x"], 16)
                    if g:
                        act.wait_ge(x_ready, x_count(g, b))
                    if n:
                        act.wait_ge(gated, n)
                    A(th, xT[:, :, bt(b)], ACT.Tanh, scale=0.5).then_inc(tanh_ready, 1)
                elif kind == "proj":
                    _, layer, b = step
                    n = NUMBER[step]
                    slot = filled(step)
                    if layer == 0:
                        if n:
                            act.wait_ge(parts_ready, n)
                            act.wait_ge(parts_used, n)
                        for bank, o, bias in ((0, "q", col["bq"]), (1, "k", col["bk"])):
                            for ct in range(CT):
                                src = big(slot, bank)[:, ct * T:(ct + 1) * T]
                                step_(A(part[o][:, 0, ct, :], src, ACT.Identity, bias=bias[:, ct:ct + 1]))
                                ins = A(qf[o][:, ct, :], src, ACT.Identity, bias=bias[:, ct:ct + 1])
                                if o == "k" and ct == CT - 1:
                                    give_back(step, ins)
                                else:
                                    step_(ins)
                    else:
                        if b >= 2:
                            act.wait_ge(z_ready, QT * NB * (b - 1))
                        else:
                            act.wait_ge(written["small"], USE["pv", 0, b + 2, 1][2] + 1)
                        give_back(step, A(vaug[b % 2][:, :, :, 0:HD],
                                          big(slot, 2).rearrange("p (t h e) -> p t h e", t=QT, h=H), ACT.Copy))
                elif kind in ("max", "kmax"):
                    n = rows_order.index(step)
                    slot = filled(step)
                    if n >= 2:
                        prev = rows_order[n - 2]
                        nm = "q" if prev[0] == "max" else "kq"
                        act.wait_ge(mrows[nm, prev[2] % 2], row_count(nm, prev[1], prev[2]))
                    out = single(slot)[:, 0:P // 2].bitcast(BF16)
                    give_back(step, A(mT[n % 2][0:2 * QT * H, :], out[0:2 * QT * H, :], ACT.Copy))
                    ring, sl, nn, before = USE[step]
                    act.wait_ge(freed[ring, sl, "act"], before["act"] + 1)
                    act.nop().then_inc(mT_ready, 1)
                elif kind in ("probs", "kprobs"):
                    _, layer, b, j = step
                    slot = filled(step)
                    n = NUMBER[step]
                    if kind == "probs":
                        dst = prob
                        if b or layer:
                            pl, pb = (layer, b - 1) if b else (0, B - 1)
                            act.wait_ge(written["small"], USE["pv", pl, pb, j // 2][2] + 1)
                    else:
                        dst = kprob[b % 2]
                        if b >= 2:
                            act.wait_ge(written["small"], USE["gather", b - 2, QT * NB - 1][2] + 1)
                        elif b == 0 and j == 0:
                            act.wait_ge(gate_ready, NUMBER["wkv", 3, B - 1] + 1)
                            act.wait_ge(written["big"], USE["fc2", 1, CT - 1][2] + 1)
                    hs = slice(j * GH, (j + 1) * GH)
                    step_(A(dst[:, hs, 0:T], wide(slot).rearrange("p a (h t) -> p (a h) t", h=2), ACT.Exp,
                            scale=SCORE_SCALE))
                    give_back(step, A(dst[:, hs, T:T + P], big(slot, 2).rearrange("p (h t) -> p h t", h=GH), ACT.Exp,
                                      scale=SCORE_SCALE))
                    ring, sl, nn, before = USE[step]
                    act.wait_ge(freed[ring, sl, "act"], before["act"] + 1)
                    act.nop().then_inc(probs_ready if kind == "probs" else kprobs_ready, 1)
                elif kind == "oT":
                    slot = filled(step)
                    n = NUMBER[step]
                    if n:
                        prev = [s for s in ORDER if s[0] == "wo"][n - 1]
                        act.wait_ge(written["big"], USE[prev][2] + 1)
                    give_back(step, A(oT, v3(big(slot, 0), CT), ACT.Copy))
                    ring, sl, nn, before = USE[step]
                    act.wait_ge(freed[ring, sl, "act"], before["act"] + 1)
                    act.nop().then_inc(oT_ready, 1)
                elif kind == "ternary":
                    i = step[1]
                    w_ = (w1, w2)[i]
                    if i == 0:
                        act.wait_ge(loaded["tern"], 32)
                    act.wait_ge(tern_cnt, i + 1)
                    A(tern_tmp(i), w_, ACT.Square, accum_out=small[:, 40 + i:41 + i]).then_inc(tern_abs, 1)
                elif kind == "fc1":
                    _, h, m = step
                    slot = filled(step)
                    if NUMBER[step] == 0:
                        act.wait_ge(tern_ready, 2)
                        act.wait_ge(written["big"], USE["probs", 0, B - 1, NG - 1][2] + 1)
                    give_back(step, A(hid[:, m, h * 512:(h + 1) * 512], big(slot, 0), ACT.Gelu,
                                      bias=col["b1"][:, m:m + 1], scale=small[:, 50:51]))
                    ring, sl, nn, before = USE[step]
                    act.wait_ge(freed[ring, sl, "act"], before["act"] + 1)
                    act.nop().then_inc(hid_ready, 1)
                elif kind == "fc2":
                    _, h, c = step
                    slot = filled(step)
                    give_back(step, A(ffn[:, c, h * 512:(h + 1) * 512], big(slot, 0), ACT.Identity,
                                      bias=col["b2"][:, c:c + 1], scale=small[:, 51:52]))
                    ring, sl, nn, before = USE[step]
                    act.wait_ge(freed[ring, sl, "act"], before["act"] + 1)
                    act.nop().then_inc(ffn_ready, 1)
                elif kind == "route":
                    act.wait_ge(logits_exp_in, 1)
                    A(R["exp"], R["logit"], ACT.Exp).then_inc(logits_exp, 1)
                elif kind == "ytok":
                    n = step[1]
                    slot = filled(step)
                    give_back(step, A(ytok[:, 2 * n:2 * n + 2, :], v3(big(slot, 0), 2), ACT.Copy))
                    ring, sl, nn, before = USE[step]
                    act.wait_ge(freed[ring, sl, "act"], before["act"] + 1)
                    act.nop().then_inc(ytok_ready, 1)
                elif kind == "up":
                    _, e, half = step
                    slot = filled(step)
                    out = wide(slot).rearrange("p a (m t) -> p (a m) t", m=2)
                    if e >= 2:
                        act.wait_ge(written["big"], USE["down", e - 2][2] + 1)
                    for mm_ in range(MT // 2):
                        m = half * (MT // 2) + mm_
                        ins = A(hE[e % 2][:, m, :], out[:, mm_, :], ACT.Gelu,
                                bias=col["fb1"][:, e * MT + m:e * MT + m + 1])
                        if mm_ < MT // 2 - 1:
                            step_(ins)
                        else:
                            give_back(step, ins)
                    ring, sl, nn, before = USE[step]
                    act.wait_ge(freed[ring, sl, "act"], before["act"] + 1)
                    act.nop().then_inc(hE_ready, 1)

        @block.vector
        def _(dve):
            V = nc.vector
            own = [0]

            def st(ins):
                own[0] += 1
                ins.then_inc(dve_own, 1)

            def settle():
                dve.wait_ge(dve_own, own[0])

            def link(ins):
                st(ins)
                settle()

            def filled(step):
                ring, slot, n, before = USE[step]
                dve.wait_ge(written[ring], n + 1)
                return slot

            def give_back(step, ins):
                ring, slot, n, before = USE[step]
                ins.then_inc(freed[ring, slot, "dve"], 1)

            def after_give_back(step):
                ring, slot, n, before = USE[step]
                dve.wait_ge(freed[ring, slot, "dve"], before["dve"] + 1)

            dve.wait_ge(loaded["cond"], 16)
            V.tensor_reduce(tf[:, 0:B], cond, axis=AX.X, op=ALU.add).then_inc(exps_ready, 1)
            dve.wait_ge(loaded["fs"], 16)
            V.tensor_scalar_min(ekv, fsT, 30.0).then_inc(exps_ready, 1)
            dve.wait_ge(loaded["const"], 32)
            st(V.tensor_copy(identb, ident))
            st(V.tensor_copy(maskb, v3(c_["masks"], 4)))
            for a in (vaug, uaug):
                for par in range(2):
                    st(V.memset(a[par][:, :, :, HD:VW], 1.0))
            dve.wait_ge(ek_ready, 2)
            link(V.tensor_scalar_add(tf[:, 0:B], tf[:, B:2 * B], 1.0))
            link(V.reciprocal(tf[:, B:2 * B], tf[:, 0:B]))
            st(V.tensor_scalar(tf[:, 2 * B:3 * B], tf[:, B:2 * B], 0.5, 0.5, ALU.mult, ALU.add))
            st(V.tensor_scalar(tf[:, 3 * B:4 * B], tf[:, B:2 * B], 0.1, 0.4, ALU.mult, ALU.add))
            dec3 = dec.rearrange("p (c b) -> p c b", b=B)
            V.tensor_scalar(dec3, small[:, 0:4 * CT].unsqueeze(2).to_broadcast([P, 4 * CT, B]), -1.0, None, ALU.mult
                            ).then_inc(exps_ready, 1)
            dve.wait_ge(ek_ready, 4)
            settle()
            link(V.tensor_tensor(dec3, dec3, tf[:, 2 * B:3 * B].unsqueeze(1).to_broadcast([P, 4 * CT, B]), ALU.mult))
            V.tensor_tensor(ekv, ek, fsT, ALU.mult).then_inc(consts_ready, 1)
            dve.wait_ge(consts_ready, 1)

            for step in ORDER:
                kind = step[0]
                if kind == "wkv":
                    _, c, b = step
                    n = NUMBER[step]
                    if c >= 2:
                        if c == 2:
                            dve.wait_ge(written["big"], USE["proj", 0, b][2] + 1)
                        else:
                            dve.wait_ge(written["big"], USE["fc1", 1, MT - 1][2] + 1)
                    for ct in range(CT):
                        i = c * CT + ct
                        dd = dec[:, i * B + b:i * B + b + 1].to_broadcast([P, T])
                        for s, src in ((0, ekv), (2, ek)):
                            x_ = src[:, ct, bt(b)]
                            st(V.tensor_tensor_scan(scan[s][:, ct, :], dd, x_, 0.0, ALU.mult, ALU.add))
                            st(V.tensor_tensor_scan(scan[s + 1][:, ct, ::-1], dd, x_[:, ::-1], 0.0, ALU.mult,
                                                    ALU.add))
                    dve.wait_ge(euk_ready, CT * (n + 1))
                    V.scalar_tensor_tensor(out=gk, in0=euk, scalar=EXP30, in1=ek[:, :, bt(b)], op0=ALU.min,
                                           op1=ALU.subtract).then_inc(euk_used, 1)
                    settle()
                    st(V.tensor_tensor(scan[0], scan[0], scan[1], ALU.add))
                    st(V.tensor_tensor(scan[2], scan[2], scan[3], ALU.add))
                    settle()
                    dve.wait_ge(euk_used, n + 1)
                    st(V.tensor_tensor(scan[2], scan[2], gk, ALU.add))
                    link(V.tensor_tensor(scan[1], gk, fsT[:, :, bt(b)], ALU.mult))
                    st(V.tensor_tensor(scan[0], scan[0], scan[1], ALU.add))
                    link(V.tensor_scalar_max(scan[2], scan[2], 1e-8))
                    link(V.reciprocal(scan[3], scan[2]))
                    V.scalar_tensor_tensor(out=G[c % 2][:, :, bt(b)], in0=scan[0], scalar=tf[:, 3 * B + b:3 * B + b + 1],
                                           in1=scan[3], op0=ALU.mult, op1=ALU.mult).then_inc(gate_ready, 1)
                    dve.wait_ge(gate_ready, n + 1)
                elif kind == "gate":
                    _, g, b = step
                    n = NUMBER[step]
                    dve.wait_ge(tanh_ready, n + 1)
                    y = G[g % 2][:, :, bt(b)]
                    V.scalar_tensor_tensor(out=y, in0=th, scalar=1.0, in1=y, op0=ALU.add, op1=ALU.mult
                                           ).then_inc(gated, 1)
                    dve.wait_ge(gated, n + 1)
                elif kind == "proj":
                    _, layer, b = step
                    n = NUMBER[step]
                    slot = filled(step)
                    if layer == 0:
                        if b >= 2:
                            dve.wait_ge(written["small"], USE["pv", 0, b - 2, 1][2] + 1)
                        give_back(step, V.tensor_tensor(
                            vaug[b % 2][:, :, :, 0:HD], big(slot, 2).rearrange("p (t h e) -> p t h e", t=QT, h=H),
                            v3(bvb, H).unsqueeze(1).to_broadcast([P, QT, H, HD]), ALU.add))
                        after_give_back(step)
                        V.nop().then_inc(v_ready, 1)
                        ring, sl, nn, before = USE[step]
                        dve.wait_ge(freed[ring, sl, "act"], before["act"] + 1)
                    else:
                        if n:
                            dve.wait_ge(parts_used, n)
                        cosb = c_["cos"].unsqueeze(1).to_broadcast([P, CT, T])
                        for bank, o in ((0, "q"), (1, "k")):
                            src = v3(big(slot, bank), CT)
                            st(V.tensor_tensor(qf[o], src, cosb, ALU.mult))
                            ins = V.tensor_tensor(rest, src[:, ::-1, :], v3(c_["sin"], CT), ALU.mult)
                            if o == "k":
                                give_back(step, ins)
                                after_give_back(step)
                            else:
                                st(ins)
                            settle()
                            link(V.tensor_tensor(qf[o], qf[o], rest, ALU.add))
                            st(V.tensor_copy(part[o][:, 0], qf[o]))
                        settle()
                    for o in ("q", "k"):
                        link(V.tensor_tensor(rest, qf[o], part[o][:, 0], ALU.subtract))
                        link(V.tensor_copy(part[o][:, 1], rest))
                        ins = V.tensor_tensor(part[o][:, 2], rest, part[o][:, 1], ALU.subtract)
                        if o == "q":
                            link(ins)
                        else:
                            ins.then_inc(parts_ready, 1)
                            dve.wait_ge(parts_ready, n + 1)
                elif kind in ("scores", "kscores"):
                    _, layer, b, j = step
                    slot = filled(step)
                    hs = slice(j * GH, (j + 1) * GH)
                    st(V.tensor_reduce(mneg[:, H + j * GH:H + (j + 1) * GH],
                                       wide(slot).rearrange("p a (h t) -> p (a h) t", h=2), axis=AX.X, op=ALU.max,
                                       negate=True))
                    give_back(step, V.tensor_reduce(mneg[:, j * GH:(j + 1) * GH],
                                                    big(slot, 2).rearrange("p (h t) -> p h t", h=GH), axis=AX.X,
                                                    op=ALU.max, negate=True))
                elif kind in ("max", "kmax"):
                    _, layer, b = step
                    n = rows_order.index(step)
                    prev = ("scores" if kind == "max" else "kscores", layer, b, NG - 1)
                    after_give_back(prev)
                    settle()
                    link(V.tensor_scalar_min(mneg, mneg, NO_KEY))
                    if n:
                        dve.wait_ge(written["small"], USE[rows_order[n - 1]][2] + 1)
                    link(V.tensor_copy(mpart[:, 0:QT * H], mneg))
                    V.tensor_tensor(mpart[:, QT * H:2 * QT * H], mneg, mpart[:, 0:QT * H], ALU.subtract
                                    ).then_inc(mparts_ready, 1)
                    dve.wait_ge(mparts_ready, n + 1)
                elif kind == "pv":
                    _, layer, b, half = step
                    n = NUMBER[step]
                    slot = filled(step)
                    o_ = single(slot)[:, 0:QT * 8 * VW].rearrange("p (t h e) -> p t h e", t=QT, h=8)
                    if n >= 2 and half == 0:
                        prev = [s for s in ORDER if s[0] == "oT"][n // 2 - 1]
                        dve.wait_ge(written["big"], USE[prev][2] + 1)
                    r_ = v3(rec, QT)
                    link(V.reciprocal(r_, o_[:, :, :, HD]))
                    give_back(step, V.tensor_tensor(
                        otok[:, :, half * P:(half + 1) * P].rearrange("p t (h e) -> p t h e", h=8), o_[:, :, :, 0:HD],
                        r_.unsqueeze(3).to_broadcast([P, QT, 8, HD]), ALU.mult))
                    after_give_back(step)
                    V.nop().then_inc(o_ready, 1)
                elif kind == "wo":
                    _, layer, b = step
                    slot = filled(step)
                    y = xT[:, :, bt(b)]
                    src = v3(big(slot, 0), CT)
                    if layer == 0:
                        for ct in range(CT):
                            ins = V.scalar_tensor_tensor(out=y[:, ct, :], in0=src[:, ct, :],
                                                         scalar=col["bo"][:, ct:ct + 1], in1=y[:, ct, :], op0=ALU.add,
                                                         op1=ALU.add)
                            if ct < CT - 1:
                                st(ins)
                            else:
                                give_back(step, ins)
                    else:
                        give_back(step, V.tensor_tensor(y, src, y, ALU.add))
                    after_give_back(step)
                    V.nop().then_inc(x_ready, 1)
                elif kind == "ternary":
                    i = step[1]
                    w_ = (w1, w2)[i]
                    s_ = small
                    if i == 0:
                        dve.wait_ge(loaded["tern"], 32)
                    V.tensor_reduce(s_[:, 32 + i:33 + i], w_, axis=AX.XY, op=ALU.max, apply_absolute_value=True
                                    ).then_inc(tern_in, 1)
                    dve.wait_ge(tern_max, i + 1)
                    st(V.tensor_scalar(s_[:, 36:37], s_[:, 34 + i:35 + i], THRESHOLD, None, ALU.mult))
                    link(V.tensor_scalar(s_[:, 37:38], s_[:, 34 + i:35 + i], -THRESHOLD, None, ALU.mult))
                    tmp = tern_tmp(i)
                    link(V.tensor_scalar(tmp, w_, s_[:, 36:37], None, ALU.is_gt))
                    link(V.scalar_tensor_tensor(out=tmp, in0=w_, scalar=s_[:, 37:38], in1=tmp, op0=ALU.is_lt,
                                                op1=ALU.subtract))
                    link(V.scalar_tensor_tensor(out=w_, in0=w_, scalar=1.0, in1=tmp, op0=ALU.mult, op1=ALU.mult,
                                                accum_out=s_[:, 42 + i:43 + i]))
                    V.tensor_copy(w_, tmp).then_inc(tern_cnt, 1)
                    dve.wait_ge(tern_cnt, i + 1)
                    dve.wait_ge(tern_abs, i + 1)
                    st(V.tensor_copy(s_[:, 44:45], s_[:, 42 + i:43 + i]))
                    st(V.tensor_copy(s_[:, 45:46], s_[:, 40 + i:41 + i]))
                    settle()
                    V.nop().then_inc(tern_sum_in, 1)
                    dve.wait_ge(tern_sum, i + 1)
                    link(V.tensor_scalar_max(s_[:, 48:49], s_[:, 47:48], 1.0))
                    link(V.reciprocal(s_[:, 49:50], s_[:, 48:49]))
                    V.tensor_tensor(s_[:, 50 + i:51 + i], s_[:, 46:47], s_[:, 49:50], ALU.mult).then_inc(tern_ready, 1)
                    dve.wait_ge(tern_ready, i + 1)
                elif kind == "fc2":
                    _, h, c = step
                    n = NUMBER[step]
                    dve.wait_ge(ffn_ready, n + 1)
                    st(V.tensor_reduce(small[:, 60 + n:61 + n], ffn[:, c, h * 512:(h + 1) * 512], axis=AX.X,
                                       op=ALU.max, apply_absolute_value=True))
                elif kind == "quant":
                    settle()
                    V.tensor_reduce(small[:, 64:65], small[:, 60:64], axis=AX.X, op=ALU.max).then_inc(amax_in, 1)
                    dve.wait_ge(amax_out, 1)
                    link(V.tensor_scalar(small[:, 66:67], small[:, 65:66], 1.0 / QMAX, 1e-8, ALU.mult, ALU.add))
                    link(V.reciprocal(small[:, 67:68], small[:, 66:67]))
                elif kind == "requant":
                    b = step[1]
                    f = ffn[:, :, bt(b)]
                    link(V.tensor_scalar(f, f, small[:, 67:68], ROUND, ALU.mult, ALU.add))
                    link(V.tensor_scalar(f, f, -ROUND, QMAX, ALU.add, ALU.min))
                    link(V.tensor_scalar(f, f, -QMAX, small[:, 66:67], ALU.max, ALU.mult))
                    y = xT[:, :, bt(b)]
                    V.tensor_tensor(y, y, f, ALU.add).then_inc(x_ready, 1)
                elif kind == "beta":
                    b = step[1]
                    slot = filled(step)
                    give_back(step, V.tensor_tensor(v3(beta[b % 2], QT), v3(single(slot)[:, 0:QT * H], QT),
                                                    bbb.unsqueeze(1).to_broadcast([P, QT, H]), ALU.add))
                    after_give_back(step)
                elif kind == "den":
                    b = step[1]
                    slot = filled(step)
                    give_back(step, V.tensor_scalar_max(cc[b % 2], single(slot)[:, 0:QT * H], 1e-20))
                    after_give_back(step)
                    link(V.reciprocal(cT, cc[b % 2]))
                    link(V.tensor_tensor(cc[b % 2], cT, beta[b % 2], ALU.mult))
                elif kind == "blocks":
                    b = step[1]
                    if b:
                        dve.wait_ge(inv_ready, b)
                    if b >= 2:
                        dve.wait_ge(written["small"], USE["solve", b - 2, QT * NB - 1][2] + 1)
                    blk_src = invT[b % 2]
                    st(V.transpose(cT, cc[b % 2]))
                    kp = kprob[b % 2]
                    for r in range(NB):
                        rows = slice(r * BLK, (r + 1) * BLK)
                        for t in range(QT):
                            at = t * T + r * BLK
                            st(V.tensor_copy(v3(blk_src[rows, t * H * BLK:(t + 1) * H * BLK], H),
                                             kp[rows, :, at:at + BLK]))
                    settle()
                    V.transpose(blkA.rearrange("p (i j) -> p i j", i=BLK),
                                blk_src.rearrange("p (n i) -> p i n", i=BLK)).then_inc(blocks_ready, 1)
                    dve.wait_ge(blocks_ready, b + 1)
                elif kind == "inverse":
                    b = step[1]
                    dve.wait_ge(inv_ready, b + 1)
                    if b >= 2:
                        dve.wait_ge(written["small"], USE["solve", b - 2, QT * NB - 1][2] + 1)
                    V.transpose(invT[b % 2].rearrange("p (n i) -> p i n", i=BLK),
                                blkX.rearrange("p (i j) -> p i j", i=BLK)).then_inc(invT_ready, 1)
                    dve.wait_ge(invT_ready, b + 1)
                    ring, sl, nn, before = USE["proj", 1, b]
                    dve.wait_ge(freed[ring, sl, "act"], before["act"] + 1)
                    rows = slice(0, BLK)
                    V.tensor_copy(v3(zz[rows, :], H), vaug[b % 2][rows, 0, :, 0:HD]).then_inc(z_ready, 1)
                elif kind == "gather":
                    _, b, s = step
                    t, r = divmod(s, NB)
                    rows = slice(r * BLK, (r + 1) * BLK)
                    slot = filled(step)
                    cb = cc[b % 2][rows, t * H:(t + 1) * H].unsqueeze(2).to_broadcast([BLK, H, HD])
                    give_back(step, V.tensor_tensor(v3(zt[rows, :], H), v3(single(slot)[rows, 0:H * HD], H), cb,
                                                    ALU.mult))
                    after_give_back(step)
                    V.tensor_tensor(v3(zz[rows, :], H), vaug[b % 2][rows, t, :, 0:HD], v3(zt[rows, :], H),
                                    ALU.subtract).then_inc(z_ready, 1)
                elif kind == "solve":
                    _, b, s = step
                    t, r = divmod(s, NB)
                    rows = slice(r * BLK, (r + 1) * BLK)
                    slot = filled(step)
                    if s == 0 and b >= 2:
                        dve.wait_ge(written["small"], USE["pv", 1, b - 2, 1][2] + 1)
                    give_back(step, V.tensor_copy(uaug[b % 2][rows, t, :, 0:HD], v3(single(slot)[rows, 0:H * HD], H)))
                    after_give_back(step)
                    V.nop().then_inc(u_ready, 1)
                elif kind == "route":
                    slot = filled(step)
                    lg = v3(single(slot)[:, 0:NT * E], NT)

                    def e8(ap):
                        return ap.unsqueeze(2).to_broadcast([P, NT, E])

                    def r3(k):
                        return v3(R[k], NT)
                    st(V.memset(zero, 0.0))
                    settle()
                    V.nop().then_inc(zeroed, 1)
                    link(V.reduce_max(R["mx"], lg, AX.X))
                    give_back(step, V.tensor_tensor(r3("logit"), lg, e8(R["mx"]), ALU.subtract))
                    after_give_back(step)
                    V.nop().then_inc(logits_exp_in, 1)
                    dve.wait_ge(logits_exp, 1)
                    link(V.reduce_sum(R["sum"], r3("exp"), AX.X))
                    link(V.reciprocal(R["rec"], R["sum"]))
                    link(V.tensor_tensor(r3("score"), r3("exp"), e8(R["rec"]), ALU.mult))
                    revb = c_["rev"].unsqueeze(1).to_broadcast([P, NT, E])
                    cur = "score"
                    for s in range(2):
                        link(V.reduce_max(R["m"][s], r3(cur), AX.X))
                        link(V.tensor_tensor(r3("t1"), r3(cur), e8(R["m"][s]), ALU.is_equal))
                        link(V.tensor_tensor(r3("t1"), r3("t1"), revb, ALU.mult))
                        link(V.reduce_max(R["key"][s], r3("t1"), AX.X))
                        link(V.tensor_tensor(v3(R["oh"][s], NT), revb, e8(R["key"][s]), ALU.is_equal))
                        if s == 0:
                            link(V.scalar_tensor_tensor(out=r3("score2"), in0=v3(R["oh"][0], NT), scalar=-2.0,
                                                        in1=r3("score"), op0=ALU.mult, op1=ALU.add))
                            cur = "score2"
                    link(V.tensor_tensor(R["tmp"][0], R["m"][0], R["m"][1], ALU.add))
                    link(V.tensor_scalar_max(R["tmp"][0], R["tmp"][0], 1e-9))
                    link(V.reciprocal(R["tmp"][1], R["tmp"][0]))
                    for s in range(2):
                        st(V.tensor_tensor(R["gate"][s], R["m"][s], R["tmp"][1], ALU.mult))
                    st(V.memset(R["pre"][0][:, 0:E], 0.0))
                    settle()
                    for s in range(2):
                        oh, pre = v3(R["oh"][s], NT), v3(R["pre"][s], NT)
                        for t in range(1, NT):
                            link(V.tensor_tensor(pre[:, t], pre[:, t - 1], oh[:, t - 1], ALU.add))
                        if s == 0:
                            link(V.tensor_tensor(R["pre"][1][:, 0:E], pre[:, NT - 1], oh[:, NT - 1], ALU.add))
                    V.nop().then_inc(choice_ready, 1)
                elif kind == "rank":
                    slot = filled(step)
                    for s in range(2):
                        lo = single(slot)[:, s * NT * E:(s + 1) * NT * E]
                        ins = V.tensor_tensor(R["t1"] if s == 0 else R["exp"], lo, R["oh"][s], ALU.mult)
                        if s == 0:
                            st(ins)
                        else:
                            give_back(step, ins)
                    after_give_back(step)
                    settle()
                    for s in range(2):
                        pos, key = R["pos"][s], R["key"][s]
                        link(V.reduce_sum(pos, v3(R["t1"] if s == 0 else R["exp"], NT), AX.X))
                        link(V.tensor_scalar(R["valid"][s], pos, float(CAP), None, ALU.is_le))
                        link(V.tensor_scalar(R["base"][s], key, -float(CAP), float(E * CAP), ALU.mult, ALU.add))
                        link(V.tensor_scalar(R["tmp"][0], pos, -1.0, None, ALU.add))
                        link(V.tensor_tensor(R["slot"][s], R["base"][s], R["tmp"][0], ALU.add))
                        link(V.tensor_tensor(R["tmp"][0], R["tmp"][0], R["valid"][s], ALU.mult))
                        link(V.tensor_tensor(R["tmp"][1], R["base"][s], R["tmp"][0], ALU.add))
                        link(V.tensor_copy(idx_g[s], R["tmp"][1]))
                        tr = c_["trash"][:, s * NT:(s + 1) * NT]
                        link(V.tensor_tensor(R["tmp"][0], R["slot"][s], tr, ALU.subtract))
                        link(V.tensor_tensor(R["tmp"][0], R["tmp"][0], R["valid"][s], ALU.mult))
                        link(V.tensor_tensor(R["tmp"][0], R["tmp"][0], tr, ALU.add))
                        link(V.tensor_copy(idx_s[s], R["tmp"][0]))
                        link(V.tensor_tensor(R["gate"][s], R["gate"][s], R["valid"][s], ALU.mult))
                    V.nop().then_inc(rt_ready, 1)
                elif kind == "xtok":
                    n = step[1]
                    slot = filled(step)
                    give_back(step, V.tensor_copy(xtok[:, 2 * n:2 * n + 2, :], v3(big(slot, 0), 2)))
                    after_give_back(step)
                elif kind == "dispT":
                    e = step[1]
                    slot = filled(step)
                    if e >= 2:
                        dve.wait_ge(written["big"], USE["up", e - 2, 1][2] + 1)
                    give_back(step, V.tensor_copy(dT[e % 2], v3(big(slot, 0), CT)))
                    after_give_back(step)
                    V.nop().then_inc(dT_ready, 1)
                elif kind == "down":
                    e = step[1]
                    slot = filled(step)
                    if e == 0:
                        dve.wait_ge(b2_loaded, 16)
                    if e >= 2:
                        dve.wait_ge(eo_stored[e % 2], 16 * (e // 2))
                    give_back(step, V.tensor_tensor(eo[e % 2], v3(big(slot, 0), 2),
                                                    b2b[:, e, :].unsqueeze(1).to_broadcast([P, 2, D]), ALU.add))
                    after_give_back(step)
                    V.nop().then_inc(eo_ready, 1)
                elif kind == "combine":
                    t = step[1]
                    dve.wait_ge(gathered, 16 * 2 * NT)
                    link(V.scalar_tensor_tensor(out=outt[:, t, :], in0=got[0][:, t, :], scalar=R["gate"][0][:, t:t + 1],
                                                in1=xtok[:, t, :], op0=ALU.mult, op1=ALU.add))
                    V.scalar_tensor_tensor(out=outt[:, t, :], in0=got[1][:, t, :], scalar=R["gate"][1][:, t:t + 1],
                                           in1=outt[:, t, :], op0=ALU.mult, op1=ALU.add).then_inc(out_ready, 1)

        @block.gpsimd
        def _(pool):
            own = [0]

            def link(ins):
                own[0] += 1
                ins.then_inc(pool_own, 1)
                pool.wait_ge(pool_own, own[0])

            RED = bass.bass_isa.ReduceOp
            G_ = nc.gpsimd

            def ones_rows(layer):
                for par in range(2):
                    two = stack["k", par][SROWS:MROWS, :, :].rearrange("p h t -> p (h t)").bitcast(F32)
                    G_.memset(two, TWO_BF16_ONES).then_inc(ones_ready, 1)
                    pool.wait_ge(ones_ready, 2 * layer + par + 1)
            ones_rows(0)
            for step in ORDER:
                kind = step[0]
                if kind == "ternary":
                    i = step[1]
                    pool.wait_ge(tern_in, i + 1)
                    G_.partition_all_reduce(small[:, 34 + i:35 + i], small[:, 32 + i:33 + i], P, RED.max
                                            ).then_inc(tern_max, 1)
                    pool.wait_ge(tern_max, i + 1)
                    pool.wait_ge(tern_sum_in, i + 1)
                    G_.partition_all_reduce(small[:, 46:48], small[:, 44:46], P, RED.add).then_inc(tern_sum, 1)
                    pool.wait_ge(tern_sum, i + 1)
                elif kind == "quant":
                    pool.wait_ge(amax_in, 1)
                    G_.partition_all_reduce(small[:, 65:66], small[:, 64:65], P, RED.max).then_inc(amax_out, 1)
                    pool.wait_ge(amax_out, 1)
                elif kind == "requant" and step[1] == 0:
                    pool.wait_ge(ffn_ready, 2 * CT)
                    ones_rows(1)
                elif kind == "wo" and step[1] == 0 and step[2] == B - 1:
                    pool.wait_ge(written["big"], USE[step][2] + 1)
                    for w_, n_ in ((wq, "wq1"), (wk, "wk1"), (wv, "wv1"), (wo, "wo1")):
                        G_.dma_start(w_, d[n_]).then_inc(loaded["att1"], 16)
                elif kind == "route":
                    pool.wait_ge(written["small"], USE["beta", B - 1][2] + 1)
                    G_.dma_start(wb[:, :, 0:E], d["wg"]).then_inc(loaded["att1"], 16)
                elif kind == "blocks":
                    b = step[1]
                    pool.wait_ge(blocks_ready, b + 1)
                    if b:
                        pool.wait_ge(invT_ready, b)
                    A3 = blkA.rearrange("p (i j) -> p i j", i=BLK)
                    X3 = blkX.rearrange("p (i j) -> p i j", i=BLK)
                    link(G_.tensor_tensor(A3, A3, cT.unsqueeze(2).to_broadcast([P, BLK, BLK]), ALU.mult))
                    link(G_.memset(blkX, 0.0))
                    link(G_.affine_select(out=X3, in_=X3, compare_op=ALU.not_equal, fill=1.0, base=0,
                                          pattern=[[1, BLK], [-1, BLK]], channel_multiplier=0))
                    for k in range(BLK - 1):
                        rows, w = BLK - 1 - k, k + 1
                        tmp = blkT[:, 0:rows * w].rearrange("p (i j) -> p i j", i=rows)
                        link(G_.tensor_tensor(tmp, A3[:, k + 1:BLK, k:k + 1].to_broadcast([P, rows, w]),
                                              X3[:, k:k + 1, 0:w].to_broadcast([P, rows, w]), ALU.mult))
                        ins = G_.tensor_tensor(X3[:, k + 1:BLK, 0:w], X3[:, k + 1:BLK, 0:w], tmp, ALU.subtract)
                        if k < BLK - 2:
                            link(ins)
                        else:
                            ins.then_inc(inv_ready, 1)
                            pool.wait_ge(inv_ready, b + 1)
                elif kind == "dispT" and step[1] == 0:
                    pool.wait_ge(rt_ready, 1)
                    pool.wait_ge(ytok_ready, B)
                    pool.wait_ge(disp_zero, 16)
                    for s in range(2):
                        for t in range(NT):
                            G_.indirect_dma_start(out=d["disp"], out_offset=bass.IndirectOffsetOnAxis(
                                ap=idx_s[s][:, t:t + 1], axis=0), in_=ytok[:, t, :], in_offset=None
                            ).then_inc(scattered, 16)
                elif kind == "combine":
                    t = step[1]
                    if t == 0:
                        pool.wait_ge(eo_stored[0], 16 * (E // 2))
                        pool.wait_ge(eo_stored[1], 16 * (E // 2))
                    for s in range(2):
                        G_.indirect_dma_start(out=got[s][:, t, :], out_offset=None, in_=d["eo"],
                                              in_offset=bass.IndirectOffsetOnAxis(ap=idx_g[s][:, t:t + 1], axis=0)
                                              ).then_inc(gathered, 16)



def _tables():
    p = np.arange(P)
    out = {"ident": np.eye(P), "tri": p[:, None] <= p[None, :], "ones": np.ones((P, P))}
    inv_freq = 1.0 / np.float32(10000.0) ** (np.arange(HALF, dtype=np.float32) / HALF)
    ang = (np.arange(T, dtype=np.float32)[:, None] * inv_freq[None, :].astype(np.float32)).astype(np.float32)
    of = p // H
    cos, sin = np.cos(ang).T[of], np.sin(ang).T[of]
    out["cos"] = cos
    out["sin"] = np.concatenate([-sin, sin], axis=1)
    later = p[None, :] > p[:, None]
    masks = [later, later.T, later | np.eye(P, dtype=bool), later.T | np.eye(P, dtype=bool)]
    out["masks"] = np.concatenate([np.where(m, MASKED, 0.0) for m in masks], axis=1)
    out["rev"] = np.tile(E - np.arange(E), (P, 1))
    out["trash"] = E * CAP + np.arange(2 * NT)[None, :] * P + p[:, None]
    return np.concatenate([np.asarray(out[k], np.float32) for k in CONSTS], axis=1)


def _rows(a):
    return np.ascontiguousarray(a.reshape(-1, P, a.shape[-1]).transpose(1, 0, 2))


def _col(a):
    return a.reshape(-1, P).T


def kernel(**inputs):
    import concourse.bacc as bacc
    from concourse.bass_utils import run_bass_kernel_spmd

    a = {k: np.asarray(v) for k, v in inputs.items()}
    ct, dd, hh = np.meshgrid(np.arange(CT), np.arange(HALF), np.arange(H), indexing="ij")
    perm = (hh * HD + ct * HALF + dd).reshape(-1)
    cols = [_col(a[f"{g}_{k}"]) for k in "wu" for g in ("L0_cond", "L0_cond2", "L1_cond", "L1_cond2")]
    cols += [_col(a["L0_attn_bq"][perm]), _col(a["L0_attn_bk"][perm]), _col(a["L0_attn_bo"]), _col(a["L0_ffn_b1"]),
             _col(a["L0_ffn_b2"]), _col(a["L1_ffn_fc1_b"].reshape(-1))]
    arrays = {
        "consts": _tables(), "columns": np.ascontiguousarray(np.concatenate(cols, axis=1)), "cond": a["cond_512"],
        "fsT": _rows(a["fside_BxSxS_0"].reshape(N, D).T), "xT": _rows(a["x"].reshape(N, D).T),
        "bv": a["L0_attn_bv"], "bb": a["L1_attn_bb"], "wb": _rows(a["L1_attn_Wb"]), "wg": _rows(a["L1_ffn_wg"]),
        "w1T": _rows(a["L0_ffn_W1"].T), "w2T": _rows(a["L0_ffn_W2"].T),
        "fc1": np.stack([_rows(w) for w in a["L1_ffn_fc1_w"]]), "fc2": np.stack([_rows(w) for w in a["L1_ffn_fc2_w"]]),
        "fb2": a["L1_ffn_fc2_b"],
    }
    for layer in range(2):
        for name, cols_ in (("q", perm), ("k", perm), ("v", slice(None)), ("o", slice(None))):
            arrays[f"w{name}{layer}"] = _rows(a[f"L{layer}_attn_W{name}"][:, cols_])
    nc = bacc.Bacc("TRN2", target_bir_lowering=False, num_devices=1)
    d = {}
    for name, arr in arrays.items():
        arrays[name] = np.ascontiguousarray(arr)
        d[name] = nc.dram_tensor(name, arr.shape, mybir.dt.from_np(arr.dtype), kind="ExternalInput").ap()
    d["disp"] = nc.dram_tensor("dispatched", (E * CAP + 2 * N, D), F32, kind="Internal").ap()
    d["eo"] = nc.dram_tensor("expert_rows", (E * CAP, D), F32, kind="Internal").ap()
    d["out"] = nc.dram_tensor("out", (N, D), F32, kind="ExternalOutput").ap()
    program(nc, d)
    r = run_bass_kernel_spmd(nc, [arrays], core_ids=[0])
    return r.results[0]["out"].reshape(B, T, D)
```

```python
from contextlib import ExitStack

import numpy as np

import concourse.bass as bass
from concourse import mybir

F32 = mybir.dt.float32
BF16 = mybir.dt.bfloat16
I32 = mybir.dt.int32
ALU = mybir.AluOpType
ACT = mybir.ActivationFunctionType
AX = mybir.AxisListType

P = 128
B, T, D = 4, 256, 256
N = B * T
CT = D // P
H = 16
HD = D // H
HALF = HD // 2
QT = T // P
VW = HD + 1
NV = 3
GH = 4
NG = H // GH
HID = 1024
MT = HID // P
E = 8
CAP = 2 * N // E
TD = 64
NT = N // P
BLK = 32
NB = P // BLK
PAIRS_Q = (0, 0, 1, 1, 0, 2)
PAIRS_K = (0, 1, 0, 1, 2, 0)
SROWS = len(PAIRS_Q) * HD
MROWS = SROWS + 2
MASKED = -1e30
NO_KEY = 1e20
TWO_BF16_ONES = float(np.array([0x3F803F80], np.uint32).view(np.float32)[0])
EXP30 = float(np.exp(np.float32(30.0)))
ROUND = 12582912.0
QMAX = 7.0
THRESHOLD = 0.05
SCORE_SCALE = 1.0 / HD ** 0.5

RINGS = {
    "proj": ("big", ("act", "dve")), "scores": ("big", ("dve",)), "probs": ("big", ("act",)),
    "kscores": ("big", ("act",)), "kprobs": ("big", ("act",)),
    "pv": ("big", ("act",)), "otr": ("big", ("dve",)),
    "oT": ("big", ("act",)), "wo": ("big", ("dve",)),
    "fc1": ("big", ("act",)), "fc2": ("big", ("act",)),
    "ytok": ("big", ("act",)), "xtok": ("big", ("dve",)), "dispT": ("big", ("dve",)),
    "up": ("big", ("act",)), "down": ("big", ("dve",)),
    "max": ("small", ("act",)), "kmax": ("small", ("act",)),
    "beta": ("small", ("dve",)),
    "gather": ("small", ("dve",)), "solve": ("small", ("dve",)),
    "route": ("small", ("dve",)), "rank": ("small", ("dve",)),
}


def interleave(first, second):
    o = []
    for i in range(max(len(first), len(second))):
        o += first[i:i + 1] + second[i:i + 1]
    return o


def make_order():
    def groups(kind, layer, b):
        return [(kind, layer, b, j) for j in range(NG)]

    o = [("wkv", 0, 0), ("wkv", 0, 1), ("weigh", 0, 0), ("gate", 0, 0), ("proj", 0, 0), ("weigh", 0, 1), ("gate", 0, 1),
         ("proj", 0, 1), ("wkv", 0, 2)] + groups("scores", 0, 0) + [("max", 0, 0), ("weigh", 0, 2)]
    for b in range(B):
        if b + 2 < B:
            o += [("gate", 0, b + 2), ("proj", 0, b + 2)]
        o += [("probs", 0, b, 0), ("probs", 0, b, 1)]
        if b + 1 < B:
            o.append(("scores", 0, b + 1, 0))
        o += [("probs", 0, b, 2), ("probs", 0, b, 3)]
        if b + 1 < B:
            o += [("scores", 0, b + 1, j) for j in range(1, NG)] + [("max", 0, b + 1)]
        o += [("pv", 0, b), ("wkv", 1, b)]
        if b == 0:
            o += [("wkv", 0, 3), ("otr", 0, b), ("weigh", 1, 0), ("oT", 0, b), ("wo", 0, b), ("gate", 1, b),
                  ("weigh", 0, 3), ("wkv", 2, b), ("largest", 0), ("largest", 1), ("weigh", 2, b)]
        else:
            o += [("otr", 0, b), ("wkv", 2, b), ("weigh", 1, b), ("oT", 0, b), ("wo", 0, b), ("gate", 1, b)]
            if b < 3:
                o += [("ternary", b - 1)]
            else:
                o += [("alpha", 0), ("alpha", 1)]
            o += [("weigh", 2, b)]
    o += [("wkv", 3, 0), ("wkv", 3, 1)]
    o += [("fc1", h, m) for h in range(2) for m in range(MT)]
    o += [("weigh", 3, 0), ("wkv", 3, 2), ("weigh", 3, 1), ("fc2", 0, 0), ("wkv", 3, 3), ("weigh", 3, 2), ("fc2", 0, 1),
          ("weigh", 3, 3), ("fc2", 1, 0), ("fc2", 1, 1), ("quant",)]
    o += [("requant", 0), ("gate", 2, 0)] + [("requant", b) for b in range(1, B)] + [("proj", 1, 0), ("beta", 0),
                                                                                 ("gate", 2, 1)]
    o += groups("kscores", 1, 0) + [("kmax", 1, 0), ("proj", 1, 1), ("beta", 1)]
    o += groups("kprobs", 1, 0) + [("den", 0), ("blocks", 0)]
    for b in range(B):
        ahead = []
        if b + 1 < B:
            ahead += groups("kscores", 1, b + 1) + [("kmax", 1, b + 1)]
        ahead += groups("scores", 1, b) + [("max", 1, b)]
        if b + 1 < B:
            ahead += groups("kprobs", 1, b + 1)
        late = groups("probs", 1, b)
        invert = [("den", b + 1), ("blocks", b + 1)] if b + 1 < B else []
        solve = [("inverse", b)]
        for s in range(QT * NB):
            if s:
                solve.append(("gather", b, s))
            solve.append(("solve", b, s))
        if b == 0:
            o += ahead + late + interleave(solve, invert)
            late = []
        elif b + 1 == B:
            o += interleave(solve, ahead + late)
            late = []
        else:
            o += interleave(solve, ahead + invert)
        if b + 2 < B:
            o += [("gate", 2, b + 2), ("proj", 1, b + 2), ("beta", b + 2)]
        o += late + [("pv", 1, b), ("otr", 1, b), ("oT", 1, b), ("wo", 1, b), ("gate", 3, b)]
    o += [("route",)] + [("ytok", i) for i in range(B)] + [("rank",)] + [("xtok", i) for i in range(B)]
    o += [("dispT", 0), ("up", 0, 0), ("dispT", 1), ("up", 0, 1)]
    for e in range(E):
        if e + 1 < E:
            o.append(("up", e + 1, 0))
            if e + 2 < E:
                o.append(("dispT", e + 2))
        o.append(("down", e))
        if e + 1 < E:
            o.append(("up", e + 1, 1))
    o += [("combine", t) for t in range(NT)]
    return o


ORDER = make_order()


def count_rings():
    seen = {"big": 0, "small": 0}
    freed = {(r, s, e): 0 for r in seen for s in range(2) for e in ("act", "dve")}
    out = {}
    for step in ORDER:
        use = RINGS.get(step[0])
        if use is None:
            continue
        ring, engines = use
        n = seen[ring]
        slot = n % 2
        out[step] = (ring, slot, n, {e: freed[ring, slot, e] for e in ("act", "dve")})
        seen[ring] += 1
        for e in engines:
            freed[ring, slot, e] += 1
    return out


USE = count_rings()
NUMBER = {}
for _step in ORDER:
    NUMBER[_step] = sum(1 for s in NUMBER if s[0] == _step[0])

CONSTS = {"ident": P, "tri": P, "ones": P, "cos": T, "sin": CT * T, "masks": 4 * P, "rev": E,
          "trash": 2 * NT}
CONST_W = sum(CONSTS.values())
CONST_AT = {}
_at = 0
for _k, _w in CONSTS.items():
    CONST_AT[_k] = _at
    _at += _w
COLS = {"w": 4 * CT, "u": 4 * CT, "bq": CT, "bk": CT, "bo": CT, "b1": MT, "b2": CT, "fb1": E * MT}
COL_W = sum(COLS.values())
COL_AT = {}
_at = 0
for _k, _w in COLS.items():
    COL_AT[_k] = _at
    _at += _w


def program(nc, d):
    with ExitStack() as ctx:
        def sem(name):
            return ctx.enter_context(nc.semaphore(name))

        words = (nc.sbuf_usable_end - nc.sbuf_base) // 4 - 16
        arena = ctx.enter_context(nc.sbuf_tensor("arena", [P, words], F32))
        psum = ctx.enter_context(nc.psum_tensor("psum", [P, 8, 512], F32))
        top = [0]

        def take(n, at=None):
            if at is None:
                at, top[0] = top[0], top[0] + n
                assert top[0] <= words, (top[0], words)
            return arena[:, at:at + n]

        def v3(ap, a):
            return ap.rearrange("p (a b) -> p a b", a=a)

        const = take(CONST_W)
        c_ = {k: const[:, CONST_AT[k]:CONST_AT[k] + w] for k, w in CONSTS.items()}
        ident, tri, ones = c_["ident"], c_["tri"], c_["ones"]
        cols = take(COL_W)
        col = {k: cols[:, COL_AT[k]:COL_AT[k] + w] for k, w in COLS.items()}
        identb = take(P // 2).bitcast(BF16)
        maskb = take(4 * P // 2).bitcast(BF16).rearrange("p (a b) -> p a b", a=4)
        QK, KQ, QK_STRICT, KQ_STRICT = range(4)
        tf = take(4 * B)
        dec = take(4 * CT * B)
        bvb = take(D)
        bbb = take(H)
        small = take(80)

        xT = v3(take(CT * N), CT)
        G = [v3(take(CT * N), CT) for _ in range(2)]
        wq, wk, wv, wo = (v3(take(CT * D), CT) for _ in range(4))
        wb = v3(take(CT * H), CT)
        th = v3(take(CT * T), CT)
        cond = v3(th[:, 0, :], B)

        r1 = top[0]
        stack = {}
        for name in ("q", "k", "kq"):
            for par in range(2):
                stack[name, par] = take(H * T // 2).bitcast(BF16).rearrange("p (h t) -> p h t", h=H)
        hid = v3(take(MT * N, at=r1), MT)
        ffn = v3(take(CT * N, at=r1 + MT * N), CT)

        part = {o: take(3 * CT * T // 2).bitcast(BF16).rearrange("p (a c t) -> p a c t", a=3, c=CT)
                for o in ("q", "k")}
        qf = {o: v3(take(CT * T), CT) for o in ("q", "k")}
        rest = v3(take(CT * T), CT)
        vflat = [take(QT * H * VW + 32 - VW) for _ in range(NV)]
        uflat = take(QT * H * VW + 32 - VW)
        vaug = [f[:, 0:QT * H * VW].rearrange("p (t h e) -> p t h e", t=QT, h=H) for f in vflat]
        uaug = uflat[:, 0:QT * H * VW].rearrange("p (t h e) -> p t h e", t=QT, h=H)
        prob = take(H * (T + P)).rearrange("p (h t) -> p h t", h=H)
        otok = v3(take(QT * D), QT)
        oT = v3(take(CT * T), CT)
        mneg = take(QT * H)
        mpart = take(2 * QT * H // 2).bitcast(BF16)
        mT = [take(P // 2).bitcast(BF16) for _ in range(2)]
        rec = take(QT * H)

        r2 = top[0]
        fsT, ek, ekv = (v3(take(CT * N), CT) for _ in range(3))
        scans = [[v3(take(CT * T), CT) for _ in range(4)] for _ in range(2)]
        euks, gks = ([v3(take(CT * T), CT) for _ in range(2)] for _ in range(2))
        w1 = v3(take(CT * HID), CT)
        w2 = v3(take(MT * D), MT)
        e_end = top[0]
        top[0] = r2
        kprob = [take(H * (T + P)).rearrange("p (h t) -> p h t", h=H) for _ in range(2)]
        blkA = take(BLK * BLK)
        blkX = take(BLK * BLK)
        blkT = take(BLK * BLK // 4)
        invT = [take(BLK * BLK) for _ in range(2)]
        cT = take(BLK)
        beta = [take(QT * H) for _ in range(2)]
        cc = [take(QT * H) for _ in range(2)]
        nbias = take(QT * H)
        zz, zt = (c_["masks"][:, i * D:(i + 1) * D] for i in range(2))
        top[0] = max(top[0], e_end)

        def oraw(layer, b):
            return oraw0 if layer == 0 else kprob[b % 2][:, 0:4, 0:T].rearrange("p h t -> p h t")

        top_all = top[0]
        top[0] = r1
        fcw = [(v3(take(CT * HID), CT), v3(take(MT * D), MT)) for _ in range(2)]
        hE = [v3(take(MT * CAP), MT) for _ in range(2)]
        b2b = v3(take(E * D), E)
        ytok = v3(take(NT * D), NT)
        xtok = v3(take(NT * D), NT)
        dtok = [v3(take(2 * D), 2) for _ in range(2)]
        dT = [v3(take(CT * CAP), CT) for _ in range(2)]
        eo = [v3(take(2 * D), 2) for _ in range(2)]
        got = [v3(take(NT * D), NT) for _ in range(2)]
        outt = v3(take(NT * D), NT)
        rt = take(24 * NT * E)
        idx = take(4 * NT).bitcast(I32)
        zero = take(D)
        assert top[0] <= words, (top[0], words)
        top[0] = max(top[0], top_all)

        rows_order = [s for s in ORDER if s[0] in ("max", "kmax")]
        tern_flat = take(CT * HID, at=r1 + 4 * (H * T // 2))
        oraw0 = take(QT * H * 32, at=r1 + 5 * (H * T // 2))

        def tern_tmp(i):
            return v3(tern_flat, (CT, MT)[i])

        def x_count(g, b):
            return (g - 1) * B + b + 1

        def stack_count(name, layer, b):
            n = b // 2 + 1
            if layer and name != "kq":
                n += B // 2
            return 16 * len(PAIRS_Q) * CT * n

        def row_count(name, layer, b):
            n = b // 2 + 1
            if layer and name == "q":
                n += B // 2
            return 16 * 2 * QT * n

        R = {}
        rt_at = [0]

        def ra(n):
            rt_at[0] += n
            return rt[:, rt_at[0] - n:rt_at[0]]
        for k in ("logit", "exp", "score", "score2", "t1"):
            R[k] = ra(NT * E)
        for k in ("oh", "pre"):
            R[k] = [ra(NT * E) for _ in range(2)]
        for k in ("mx", "sum", "rec"):
            R[k] = ra(NT)
        for k in ("m", "key", "gate", "pos", "valid", "slot", "tmp", "base"):
            R[k] = [ra(NT) for _ in range(2)]
        idx_s = [idx[:, s * NT:(s + 1) * NT] for s in range(2)]
        idx_g = [idx[:, (2 + s) * NT:(3 + s) * NT] for s in range(2)]

        def big(slot, bank):
            return psum[:, 3 * slot + bank, :]

        def wide(slot):
            return psum[:, 3 * slot:3 * slot + 2, :]

        def single(slot):
            return psum[:, 6 + slot, :]

        loaded = {k: sem(f"loaded_{k}") for k in
                  ("const", "cond", "fs", "x", "att0", "tern", "att1")}
        written = {"big": sem("big_psum_written"), "small": sem("small_psum_written")}
        freed = {(r, s, e): sem(f"{r}_slot{s}_freed_by_{e}")
                 for r in ("big", "small") for s in range(2) for e in ("act", "dve")}
        act_own, dve_own, pool_own = sem("act_steps"), sem("dve_steps"), sem("pool_steps")
        ones_ready = sem("ones_rows_ready")
        consts_ready = sem("consts_ready")
        exps_ready = sem("exps_ready")
        ek_ready = sem("ek_ready")
        euk_ready = sem("euk_ready")
        euk_used = sem("euk_used")
        scanned = sem("recurrences_ready")
        summed = sem("sums_ready")
        oraw_ready = sem("attended_raw")
        nbias_ready = sem("minus_max_ready")
        gate_ready = sem("gate_ready")
        tanh_ready = sem("tanh_ready")
        gated = sem("gated")
        x_ready = sem("x_ready")
        split_from = sem("operands_ready")
        v_by_act = sem("values_ready_act")
        parts_ready = sem("parts_ready")
        v_ready = sem("values_ready")
        stacked = {(o, p): sem(f"stacked_{o}{p}") for o in ("q", "k", "kq") for p in range(2)}
        parts_used = sem("parts_stacked")
        mparts_ready = sem("max_parts_ready")
        mT_ready = sem("max_rows_ready")
        mrows = {(o, p): sem(f"max_rows_{o}{p}") for o in ("q", "kq") for p in range(2)}
        probs_ready = sem("probs_ready")
        kprobs_ready = sem("kprobs_ready")
        o_ready = sem("attended")
        oT_ready = sem("attended_T")
        tern_in = sem("ternary_abs")
        tern_max = sem("ternary_max")
        tern_sum_in = sem("ternary_sums_in")
        tern_sum = sem("ternary_sums")
        tern_abs = sem("ternary_absolute")
        tern_cnt = sem("ternary_counts")
        tern_ready = sem("ternary_ready")
        hid_ready = sem("hidden_ready")
        ffn_ready = sem("ffn_ready")
        amax_in, amax_out = sem("quant_max_in"), sem("quant_max_out")
        blocks_ready = sem("blocks_ready")
        inv_ready = sem("inverses_ready")
        invT_ready = sem("inverses_T_ready")
        z_ready = sem("rhs_ready")
        u_ready = sem("solved_ready")
        coef_ready = sem("coefficients_ready")
        zeroed = sem("zero_rows_ready")
        disp_zero = sem("dispatch_zeroed")
        ytok_ready, xtok_ready = sem("ytok_ready"), sem("xtok_ready")
        logits_exp_in, logits_exp = sem("logits_in"), sem("logits_exp")
        choice_ready = sem("choice_ready")
        rt_ready = sem("indices_ready")
        scattered = sem("scattered")
        w_loaded = [sem(f"expert_weights_{i}") for i in range(2)]
        b2_loaded = sem("expert_bias_loaded")
        dtok_loaded = [sem(f"dispatched_{i}") for i in range(2)]
        dT_ready = sem("dispatched_T")
        hE_ready = sem("expert_hidden")
        eo_ready = sem("expert_out")
        eo_stored = [sem(f"expert_out_stored_{i}") for i in range(2)]
        gathered = sem("gathered")
        out_ready = sem("out_ready")
        stored = sem("out_stored")

        block = ctx.enter_context(nc.Block())

        def bt(b):
            return slice(b * T, (b + 1) * T)

        def n_before(step, kind=None):
            return NUMBER[step]

        @block.sync
        def _(sp):
            sp.dma_start(cond, d["cond"].rearrange("(o b) t -> o b t", o=1).to_broadcast([P, B, TD])).then_inc(loaded["cond"], 16)
            sp.dma_start(cols, d["columns"]).then_inc(loaded["const"], 16)
            sp.dma_start(fsT, d["fsT"]).then_inc(loaded["fs"], 16)
            sp.dma_start(const, d["consts"]).then_inc(loaded["const"], 16)
            sp.dma_start(xT, d["xT"]).then_inc(loaded["x"], 16)
            for w_, n_ in ((wq, "wq0"), (wk, "wk0"), (wv, "wv0"), (wo, "wo0")):
                sp.dma_start(w_, d[n_]).then_inc(loaded["att0"], 16)
            sp.dma_start(bvb, d["bv"].rearrange("(o c) -> o c", o=1).to_broadcast([P, D])).then_inc(loaded["att0"], 16)
            sp.dma_start(bbb, d["bb"].rearrange("(o c) -> o c", o=1).to_broadcast([P, H])).then_inc(loaded["att0"], 16)
            sp.dma_start(wb, d["wb"]).then_inc(loaded["att0"], 16)
            sp.dma_start(w1, d["w1T"]).then_inc(loaded["tern"], 16)
            sp.dma_start(w2, d["w2T"]).then_inc(loaded["tern"], 16)

            n_stack = {k: 0 for k in stacked}
            n_rows = 0
            experts_loaded = 0

            def load_expert(e):
                if e >= 2:
                    sp.wait_ge(written["big"], USE["down", e - 2][2] + 1)
                sp.dma_start(fcw[e % 2][0], d["fc1"][e]).then_inc(w_loaded[e % 2], 16)
                sp.dma_start(fcw[e % 2][1], d["fc2"][e]).then_inc(w_loaded[e % 2], 16)

            def load_dispatched(e):
                if e >= 2:
                    sp.wait_ge(written["big"], USE["dispT", e - 2][2] + 1)
                sp.dma_start(dtok[e % 2], d["disp"][e * CAP:(e + 1) * CAP, :].rearrange("(s p) c -> p s c", p=P)
                             ).then_inc(dtok_loaded[e % 2], 16)

            for step in ORDER:
                kind = step[0]
                if kind == "proj":
                    _, layer, b = step
                    par = b % 2
                    n = n_before(step)
                    sp.wait_ge(parts_ready, n + 1)
                    if b >= 2:
                        sp.wait_ge(written["big"], USE["probs", layer, b - 2, NG - 1][2] + 1)
                    elif layer == 1:
                        sp.wait_ge(written["big"], USE["probs", 0, b + 2, NG - 1][2] + 1)
                    names = [("k", "k", PAIRS_K)] + ([("kq", "k", PAIRS_Q)] if layer else []) + [("q", "q", PAIRS_Q)]
                    for name, src, pairs in names:
                        if name == "kq" and b == 0:
                            sp.wait_ge(x_ready, 2 * B)
                        for g, pt in enumerate(pairs):
                            for ct in range(CT):
                                r = g * HD + ct * HALF
                                sp.dma_start(stack[name, par][r:r + HALF, :, :], part[src][:, pt, ct, :]
                                             ).then_inc(stacked[name, par], 16)
                                n_stack[name, par] += 16
                    for name, _, _ in names:
                        sp.wait_ge(stacked[name, par], n_stack[name, par])
                    sp.nop().then_inc(parts_used, 1)
                elif kind in ("max", "kmax"):
                    _, layer, b = step
                    name = "q" if kind == "max" else "kq"
                    sp.wait_ge(mT_ready, rows_order.index(step) + 1)
                    src = mT[rows_order.index(step) % 2]
                    for pt in range(2):
                        for t in range(QT):
                            r = (pt * QT + t) * H
                            sp.dma_start(stack[name, b % 2][SROWS + pt:SROWS + pt + 1, :, t * P:(t + 1) * P],
                                         src[r:r + H, :]).then_inc(mrows[name, b % 2], 16)
                elif kind == "route":
                    sp.wait_ge(gated, NUMBER["gate", 3, B - 1] + 1)
                    load_expert(0)
                    load_expert(1)
                    sp.dma_start(b2b, d["fb2"].rearrange("(o e) c -> o e c", o=1).to_broadcast([P, E, D])).then_inc(b2_loaded, 16)
                    sp.wait_ge(zeroed, 1)
                    sp.dma_start(d["disp"][0:E * CAP, :].rearrange("(p a) c -> p a c", p=P),
                                 zero[:, :].unsqueeze(1).to_broadcast([P, E * CAP // P, D])).then_inc(disp_zero, 16)
                elif kind == "dispT":
                    if step[1] == 0:
                        sp.wait_ge(scattered, 16 * 2 * NT)
                        load_dispatched(0)
                        load_dispatched(1)
                elif kind == "down":
                    e = step[1]
                    if e + 2 < E:
                        load_dispatched(e + 2)
                        load_expert(e + 2)
                    sp.wait_ge(eo_ready, e + 1)
                    sp.dma_start(d["eo"][e * CAP:(e + 1) * CAP, :].rearrange("(s p) c -> p s c", p=P), eo[e % 2]
                                 ).then_inc(eo_stored[e % 2], 16)
                elif kind == "combine":
                    t = step[1]
                    sp.wait_ge(out_ready, t + 1)
                    sp.dma_start(d["out"][t * P:(t + 1) * P, :], outt[:, t, :]).then_inc(stored, 16)
            sp.wait_ge(stored, 16 * NT)

        @block.tensor
        def _(pe):
            def acquire(step):
                ring, slot, n, before = USE[step]
                for e in ("act", "dve"):
                    if before[e]:
                        pe.wait_ge(freed[ring, slot, e], before[e])
                return slot

            def mm(out, lhsT, rhs, start=True, stop=True):
                return nc.tensor.matmul(out, lhsT, rhs, start=start, stop=stop)

            def wrote(step, ins):
                ins.then_inc(written[USE[step][0]], 1)

            count = {}
            for step in ORDER:
                kind = step[0]
                i = count.get(kind, 0)
                count[kind] = i + 1
                if kind == "proj":
                    _, layer, b = step
                    g = 0 if layer == 0 else 2
                    pe.wait_ge(gated, NUMBER["gate", g, b] + 1)
                    if b == 0:
                        pe.wait_ge(loaded[f"att{layer}"], 16 * (7 if layer == 0 else 4))
                    slot = acquire(step)
                    y = G[g % 2]
                    for bank, w_ in ((0, wq), (1, wk)):
                        for co in range(CT):
                            for ci in range(CT):
                                mm(big(slot, bank)[:, co * T:(co + 1) * T], w_[:, ci, co * P:(co + 1) * P],
                                   y[:, ci, bt(b)], ci == 0, ci == CT - 1)
                    for t in range(QT):
                        for ci in range(CT):
                            tok = b * T + t * P
                            last = mm(big(slot, 2)[:, t * D:(t + 1) * D], y[:, ci, tok:tok + P], wv[:, ci, :],
                                      ci == 0, ci == CT - 1)
                    wrote(step, last)
                elif kind == "beta":
                    b = step[1]
                    slot = acquire(step)
                    for t in range(QT):
                        for ci in range(CT):
                            tok = b * T + t * P
                            last = mm(single(slot)[:, t * H:(t + 1) * H], G[0][:, ci, tok:tok + P], wb[:, ci, :],
                                      ci == 0, ci == CT - 1)
                    wrote(step, last)
                elif kind in ("scores", "kscores"):
                    _, layer, b, j = step
                    par = b % 2
                    qn = "q" if kind == "scores" else "kq"
                    if j == 0:
                        pe.wait_ge(stacked[qn, par], stack_count(qn, layer, b))
                        pe.wait_ge(stacked["k", par], stack_count("k", layer, b))
                        if i == 0 and kind == "scores":
                            pe.wait_ge(consts_ready, 1)
                    slot = acquire(step)
                    q_, k_ = stack[qn, par], stack["k", par]
                    mask = maskb[:, QK if kind == "scores" else QK_STRICT, :]
                    for jj in range(GH):
                        h = j * GH + jj
                        out = wide(slot)[:, jj // 2, (jj % 2) * T:(jj % 2 + 1) * T]
                        mm(out, q_[0:SROWS, h, P:T], k_[0:SROWS, h, 0:T], True, False)
                        mm(out[:, P:T], identb, mask, False, True)
                    for jj in range(GH):
                        h = j * GH + jj
                        out = big(slot, 2)[:, jj * P:(jj + 1) * P]
                        mm(out, q_[0:SROWS, h, 0:P], k_[0:SROWS, h, 0:P], True, False)
                        last = mm(out, identb, mask, False, True)
                    wrote(step, last)
                elif kind in ("max", "kmax"):
                    n = rows_order.index(step)
                    pe.wait_ge(mparts_ready, n + 1)
                    slot = acquire(step)
                    out = single(slot)[:, 0:P // 2].bitcast(BF16)
                    wrote(step, nc.tensor.transpose(out[0:2 * QT * H, :], mpart, identb))
                elif kind in ("probs", "kprobs"):
                    _, layer, b, j = step
                    par = b % 2
                    qn = "q" if kind == "probs" else "kq"
                    if j == 0:
                        pe.wait_ge(mrows[qn, par], row_count(qn, layer, b))
                        if b == 0:
                            pe.wait_ge(ones_ready, 2 * (layer + 1))
                    slot = acquire(step)
                    q_, k_ = stack[qn, par], stack["k", par]
                    mask = maskb[:, KQ if kind == "probs" else KQ_STRICT, :]
                    for jj in range(GH):
                        h = j * GH + jj
                        out = wide(slot)[:, jj // 2, (jj % 2) * T:(jj % 2 + 1) * T]
                        mm(out, k_[0:MROWS, h, 0:P], q_[0:MROWS, h, 0:T], True, False)
                        mm(out[:, 0:P], identb, mask, False, True)
                    for jj in range(GH):
                        h = j * GH + jj
                        out = big(slot, 2)[:, jj * P:(jj + 1) * P]
                        mm(out, k_[0:MROWS, h, P:T], q_[0:MROWS, h, P:T], True, False)
                        last = mm(out, identb, mask, False, True)
                    wrote(step, last)
                elif kind == "pv":
                    _, layer, b = step
                    pe.wait_ge(probs_ready, NUMBER["probs", layer, b, NG - 1] + 1)
                    if layer == 0:
                        pe.wait_ge(v_ready, NUMBER["proj", 0, b] + 1)
                        val = vflat[b % NV]
                    else:
                        pe.wait_ge(u_ready, QT * NB * (b + 1))
                        val = uflat
                    slot = acquire(step)
                    for h in range(H):
                        out = wide(slot).rearrange("p a (g t) -> p (a g) t", g=2)[(h % 4) * 32:(h % 4) * 32 + 32, h // 4, :]
                        mm(out, val[:, h * VW:h * VW + 32], prob[:, h, 0:T], True, False)
                        at = (H + h) * VW
                        last = mm(out[:, P:T], val[:, at:at + 32], prob[:, h, T:T + P], False, True)
                    wrote(step, last)
                elif kind == "otr":
                    _, layer, b = step
                    pe.wait_ge(oraw_ready, layer * B + b + 1)
                    slot = acquire(step)
                    raw = oraw0.rearrange("p (g t) -> p g t", g=4) if layer == 0 else oraw(1, b)
                    for t in range(QT):
                        for g in range(4):
                            last = nc.tensor.transpose(wide(slot)[:, t, g * P:(g + 1) * P], raw[:, g, t * P:(t + 1) * P],
                                                       ident)
                    wrote(step, last)
                elif kind == "oT":
                    _, layer, b = step
                    pe.wait_ge(o_ready, layer * B + b + 1)
                    slot = acquire(step)
                    out = v3(big(slot, 0), CT)
                    for ct in range(CT):
                        for t in range(QT):
                            last = nc.tensor.transpose(out[:, ct, t * P:(t + 1) * P], otok[:, t, ct * P:(ct + 1) * P],
                                                       ident)
                    wrote(step, last)
                elif kind == "wo":
                    _, layer, b = step
                    pe.wait_ge(oT_ready, layer * B + b + 1)
                    slot = acquire(step)
                    out = v3(big(slot, 0), CT)
                    for co in range(CT):
                        for ci in range(CT):
                            last = mm(out[:, co, :], wo[:, ci, co * P:(co + 1) * P], oT[:, ci, :],
                                      ci == 0, ci == CT - 1)
                    wrote(step, last)
                elif kind == "fc1":
                    _, h, m = step
                    if i == 0:
                        pe.wait_ge(gated, NUMBER["gate", 1, B - 1] + 1)
                        pe.wait_ge(tern_ready, 2)
                    slot = acquire(step)
                    for ci in range(CT):
                        last = mm(big(slot, 0), w1[:, ci, m * P:(m + 1) * P], G[1][:, ci, h * 512:(h + 1) * 512],
                                  ci == 0, ci == CT - 1)
                    wrote(step, last)
                elif kind == "fc2":
                    _, h, c = step
                    pe.wait_ge(hid_ready, MT * (h + 1))
                    slot = acquire(step)
                    for m in range(MT):
                        last = mm(big(slot, 0), w2[:, m, c * P:(c + 1) * P], hid[:, m, h * 512:(h + 1) * 512],
                                  m == 0, m == MT - 1)
                    wrote(step, last)
                elif kind == "gather":
                    _, b, s = step
                    t, r = divmod(s, NB)
                    pe.wait_ge(u_ready, QT * NB * b + s)
                    slot = acquire(step)
                    kp, u = kprob[b % 2], uaug
                    rows = slice(r * BLK, (r + 1) * BLK)
                    for h in range(H):
                        out = single(slot)[rows, h * HD:(h + 1) * HD]
                        if t == 0:
                            last = mm(out, kp[0:r * BLK, h, rows], u[0:r * BLK, 0, h, 0:HD])
                        else:
                            last = mm(out, kp[:, h, P + r * BLK:P + (r + 1) * BLK], u[:, 0, h, 0:HD], True, r == 0)
                            if r:
                                last = mm(out, kp[0:r * BLK, h, T + r * BLK:T + (r + 1) * BLK],
                                          u[0:r * BLK, 1, h, 0:HD], False, True)
                    wrote(step, last)
                elif kind == "solve":
                    _, b, s = step
                    t, r = divmod(s, NB)
                    if s == 0:
                        pe.wait_ge(invT_ready, b + 1)
                        pe.wait_ge(kprobs_ready, NG * (b + 1))
                    pe.wait_ge(z_ready, QT * NB * b + s + 1)
                    slot = acquire(step)
                    rows = slice(r * BLK, (r + 1) * BLK)
                    for h in range(H):
                        n = t * H + h
                        last = mm(single(slot)[rows, h * HD:(h + 1) * HD], invT[b % 2][rows, n * BLK:(n + 1) * BLK],
                                  zz[rows, h * HD:(h + 1) * HD])
                    wrote(step, last)
                elif kind == "route":
                    pe.wait_ge(gated, NUMBER["gate", 3, B - 1] + 1)
                    slot = acquire(step)
                    wg = wb[:, :, 0:E]
                    pe.wait_ge(loaded["att1"], 16 * 5)
                    for t in range(NT):
                        for ci in range(CT):
                            last = mm(single(slot)[:, t * E:(t + 1) * E], G[1][:, ci, t * P:(t + 1) * P], wg[:, ci, :],
                                      ci == 0, ci == CT - 1)
                    wrote(step, last)
                elif kind in ("ytok", "xtok"):
                    n = step[1]
                    slot = acquire(step)
                    src = G[1] if kind == "ytok" else xT
                    out = big(slot, 0).rearrange("p (t c) -> p t c", t=2)
                    for t in range(2):
                        for ct in range(CT):
                            tok = (2 * n + t) * P
                            last = nc.tensor.transpose(out[:, t, ct * P:(ct + 1) * P], src[:, ct, tok:tok + P], ident)
                    wrote(step, last)
                elif kind == "rank":
                    pe.wait_ge(choice_ready, 1)
                    slot = acquire(step)
                    for s in range(2):
                        out = single(slot)[:, s * NT * E:(s + 1) * NT * E]
                        mm(out, tri, R["oh"][s], True, False)
                        last = mm(out, ones, R["pre"][s], False, True)
                    wrote(step, last)
                elif kind == "dispT":
                    e = step[1]
                    pe.wait_ge(dtok_loaded[e % 2], 16 * (e // 2 + 1))
                    slot = acquire(step)
                    out = v3(big(slot, 0), CT)
                    for ct in range(CT):
                        for s in range(2):
                            last = nc.tensor.transpose(out[:, ct, s * P:(s + 1) * P], dtok[e % 2][:, s, ct * P:(ct + 1) * P],
                                                       ident)
                    wrote(step, last)
                elif kind == "up":
                    _, e, half = step
                    if half == 0:
                        pe.wait_ge(dT_ready, e + 1)
                        pe.wait_ge(w_loaded[e % 2], 32 * (e // 2 + 1))
                    slot = acquire(step)
                    out = wide(slot).rearrange("p a (m t) -> p (a m) t", m=2)
                    for mm_ in range(MT // 2):
                        m = half * (MT // 2) + mm_
                        for ci in range(CT):
                            last = mm(out[:, mm_, :], fcw[e % 2][0][:, ci, m * P:(m + 1) * P], dT[e % 2][:, ci, :],
                                      ci == 0, ci == CT - 1)
                    wrote(step, last)
                elif kind == "down":
                    e = step[1]
                    pe.wait_ge(hE_ready, 2 * e + 2)
                    slot = acquire(step)
                    out = v3(big(slot, 0), 2)
                    for s in range(2):
                        for m in range(MT):
                            last = mm(out[:, s, :], hE[e % 2][:, m, s * P:(s + 1) * P], fcw[e % 2][1][:, m, :],
                                      m == 0, m == MT - 1)
                    wrote(step, last)

        @block.scalar
        def _(act):
            own = [0]

            def step_(ins):
                own[0] += 1
                ins.then_inc(act_own, 1)

            def settle():
                act.wait_ge(act_own, own[0])

            def filled(step):
                ring, slot, n, before = USE[step]
                act.wait_ge(written[ring], n + 1)
                return slot

            def give_back(step, ins):
                ring, slot, n, before = USE[step]
                ins.then_inc(freed[ring, slot, "act"], 1)

            A = nc.scalar.activation
            act.wait_ge(exps_ready, 1)
            A(tf[:, B:2 * B], tf[:, 0:B], ACT.Exp, scale=-1.0).then_inc(ek_ready, 1)
            act.wait_ge(loaded["const"], 32)
            A(small[:, 0:4 * CT], col["w"], ACT.Exp).then_inc(ek_ready, 1)
            act.wait_ge(exps_ready, 2)
            A(ek, ekv, ACT.Exp).then_inc(ek_ready, 1)
            act.wait_ge(exps_ready, 3)
            A(dec, dec, ACT.Exp).then_inc(ek_ready, 1)

            for step in ORDER:
                kind = step[0]
                if kind == "wkv":
                    _, c, b = step
                    n = NUMBER[step]
                    if n == 0:
                        act.wait_ge(loaded["fs"], 16)
                    if n >= 2:
                        act.wait_ge(euk_used, n - 1)
                    for ct in range(CT):
                        A(euks[n % 2][:, ct, :], fsT[:, ct, bt(b)], ACT.Exp, bias=col["u"][:, c * CT + ct:c * CT + ct + 1]
                          ).then_inc(euk_ready, 1)
                elif kind == "gate":
                    _, g, b = step
                    n = NUMBER[step]
                    if n == 0:
                        act.wait_ge(loaded["x"], 16)
                    if g:
                        act.wait_ge(x_ready, x_count(g, b))
                    if n:
                        act.wait_ge(gated, n)
                    A(th, xT[:, :, bt(b)], ACT.Tanh, scale=0.5).then_inc(tanh_ready, 1)
                elif kind == "proj":
                    _, layer, b = step
                    n = NUMBER[step]
                    slot = filled(step)
                    if layer == 0:
                        if n:
                            act.wait_ge(parts_ready, n)
                            act.wait_ge(parts_used, n)
                        for bank, o, bias in ((0, "q", col["bq"]), (1, "k", col["bk"])):
                            for ct in range(CT):
                                src = big(slot, bank)[:, ct * T:(ct + 1) * T]
                                step_(A(part[o][:, 0, ct, :], src, ACT.Identity, bias=bias[:, ct:ct + 1]))
                                ins = A(qf[o][:, ct, :], src, ACT.Identity, bias=bias[:, ct:ct + 1])
                                if o == "k" and ct == CT - 1:
                                    give_back(step, ins)
                                else:
                                    step_(ins)
                    else:
                        if b >= NV:
                            act.wait_ge(z_ready, QT * NB * (b - NV + 1))
                        else:
                            act.wait_ge(written["big"], USE["pv", 0, B - 1][2] + 1)
                        give_back(step, A(vaug[b % NV][:, :, :, 0:HD],
                                          big(slot, 2).rearrange("p (t h e) -> p t h e", t=QT, h=H), ACT.Copy))
                elif kind in ("max", "kmax"):
                    n = rows_order.index(step)
                    slot = filled(step)
                    if n >= 2:
                        prev = rows_order[n - 2]
                        nm = "q" if prev[0] == "max" else "kq"
                        act.wait_ge(mrows[nm, prev[2] % 2], row_count(nm, prev[1], prev[2]))
                    out = single(slot)[:, 0:P // 2].bitcast(BF16)
                    give_back(step, A(mT[n % 2][0:2 * QT * H, :], out[0:2 * QT * H, :], ACT.Copy))
                    ring, sl, nn, before = USE[step]
                    act.wait_ge(freed[ring, sl, "act"], before["act"] + 1)
                    act.nop().then_inc(mT_ready, 1)
                elif kind in ("probs", "kprobs"):
                    _, layer, b, j = step
                    slot = filled(step)
                    n = NUMBER[step]
                    if kind == "probs":
                        dst = prob
                        if b or layer:
                            pl, pb = (layer, b - 1) if b else (0, B - 1)
                            act.wait_ge(written["big"], USE["pv", pl, pb][2] + 1)
                    else:
                        dst = kprob[b % 2]
                        if b >= 2:
                            act.wait_ge(written["small"], USE["gather", b - 2, QT * NB - 1][2] + 1)
                            act.wait_ge(written["big"], USE["otr", 1, b - 2][2] + 1)
                        elif b == 0 and j == 0:
                            act.wait_ge(gate_ready, NUMBER["weigh", 3, B - 1] + 1)
                            act.wait_ge(written["big"], USE["fc2", 1, CT - 1][2] + 1)
                    hs = slice(j * GH, (j + 1) * GH)
                    step_(A(dst[:, hs, 0:T], wide(slot).rearrange("p a (h t) -> p (a h) t", h=2), ACT.Exp,
                            scale=SCORE_SCALE))
                    give_back(step, A(dst[:, hs, T:T + P], big(slot, 2).rearrange("p (h t) -> p h t", h=GH), ACT.Exp,
                                      scale=SCORE_SCALE))
                    ring, sl, nn, before = USE[step]
                    act.wait_ge(freed[ring, sl, "act"], before["act"] + 1)
                    act.nop().then_inc(probs_ready if kind == "probs" else kprobs_ready, 1)
                elif kind == "kscores":
                    _, layer, b, j = step
                    slot = filled(step)
                    act.wait_ge(nbias_ready, NUMBER[step] + 1)
                    if j == 0 and b >= 2:
                        act.wait_ge(z_ready, QT * NB * (b - 1))
                    for t in range(QT):
                        for jj in range(GH):
                            h = j * GH + jj
                            if t == 0:
                                s_ = big(slot, 2)[:, jj * P:(jj + 1) * P]
                            else:
                                s_ = wide(slot)[:, jj // 2, (jj % 2) * T:(jj % 2 + 1) * T]
                            n = t * H + h
                            ins = A(s_, s_, ACT.Exp, bias=nbias[:, n:n + 1], scale=SCORE_SCALE,
                                    accum_out=cc[b % 2][:, n:n + 1])
                            if t == QT - 1 and jj == GH - 1:
                                give_back(step, ins)
                elif kind == "pv":
                    _, layer, b = step
                    slot = filled(step)
                    n = NUMBER[step]
                    if layer == 0:
                        if b:
                            act.wait_ge(written["big"], USE["otr", 0, b - 1][2] + 1)
                        dst = oraw0.rearrange("p (a c) -> p a c", a=2)
                        src = wide(slot)
                    else:
                        act.wait_ge(written["small"], USE["gather", b, QT * NB - 1][2] + 1)
                        act.wait_ge(blocks_ready, b + 1)
                        dst = oraw(1, b)
                        src = wide(slot).rearrange("p a (g t) -> p (a g) t", g=2)
                    give_back(step, A(dst, src, ACT.Copy))
                    ring, sl, nn, before = USE[step]
                    act.wait_ge(freed[ring, sl, "act"], before["act"] + 1)
                    act.nop().then_inc(oraw_ready, 1)
                elif kind == "oT":
                    slot = filled(step)
                    n = NUMBER[step]
                    if n:
                        prev = [s for s in ORDER if s[0] == "wo"][n - 1]
                        act.wait_ge(written["big"], USE[prev][2] + 1)
                    give_back(step, A(oT, v3(big(slot, 0), CT), ACT.Copy))
                    ring, sl, nn, before = USE[step]
                    act.wait_ge(freed[ring, sl, "act"], before["act"] + 1)
                    act.nop().then_inc(oT_ready, 1)
                elif kind == "ternary":
                    i = step[1]
                    w_ = (w1, w2)[i]
                    act.wait_ge(tern_cnt, i + 1)
                    A(tern_tmp(i), w_, ACT.Square, accum_out=small[:, 43 + 2 * i:44 + 2 * i]).then_inc(tern_abs, 1)
                elif kind == "fc1":
                    _, h, m = step
                    slot = filled(step)
                    if NUMBER[step] == 0:
                        act.wait_ge(tern_ready, 2)
                        act.wait_ge(written["big"], USE["probs", 0, B - 1, NG - 1][2] + 1)
                    give_back(step, A(hid[:, m, h * 512:(h + 1) * 512], big(slot, 0), ACT.Gelu,
                                      bias=col["b1"][:, m:m + 1], scale=small[:, 56:57]))
                    ring, sl, nn, before = USE[step]
                    act.wait_ge(freed[ring, sl, "act"], before["act"] + 1)
                    act.nop().then_inc(hid_ready, 1)
                elif kind == "fc2":
                    _, h, c = step
                    slot = filled(step)
                    give_back(step, A(ffn[:, c, h * 512:(h + 1) * 512], big(slot, 0), ACT.Identity,
                                      bias=col["b2"][:, c:c + 1], scale=small[:, 57:58]))
                    ring, sl, nn, before = USE[step]
                    act.wait_ge(freed[ring, sl, "act"], before["act"] + 1)
                    act.nop().then_inc(ffn_ready, 1)
                elif kind == "route":
                    act.wait_ge(logits_exp_in, 1)
                    A(R["exp"], R["logit"], ACT.Exp).then_inc(logits_exp, 1)
                elif kind == "ytok":
                    n = step[1]
                    slot = filled(step)
                    give_back(step, A(ytok[:, 2 * n:2 * n + 2, :], v3(big(slot, 0), 2), ACT.Copy))
                    ring, sl, nn, before = USE[step]
                    act.wait_ge(freed[ring, sl, "act"], before["act"] + 1)
                    act.nop().then_inc(ytok_ready, 1)
                elif kind == "up":
                    _, e, half = step
                    slot = filled(step)
                    out = wide(slot).rearrange("p a (m t) -> p (a m) t", m=2)
                    if e >= 2:
                        act.wait_ge(written["big"], USE["down", e - 2][2] + 1)
                    for mm_ in range(MT // 2):
                        m = half * (MT // 2) + mm_
                        ins = A(hE[e % 2][:, m, :], out[:, mm_, :], ACT.Gelu,
                                bias=col["fb1"][:, e * MT + m:e * MT + m + 1])
                        if mm_ < MT // 2 - 1:
                            step_(ins)
                        else:
                            give_back(step, ins)
                    ring, sl, nn, before = USE[step]
                    act.wait_ge(freed[ring, sl, "act"], before["act"] + 1)
                    act.nop().then_inc(hE_ready, 1)

        @block.vector
        def _(dve):
            V = nc.vector
            own = [0]

            def st(ins):
                own[0] += 1
                ins.then_inc(dve_own, 1)

            def settle():
                dve.wait_ge(dve_own, own[0])

            def link(ins):
                st(ins)
                settle()

            def filled(step):
                ring, slot, n, before = USE[step]
                dve.wait_ge(written[ring], n + 1)
                return slot

            def give_back(step, ins):
                ring, slot, n, before = USE[step]
                ins.then_inc(freed[ring, slot, "dve"], 1)

            def after_give_back(step):
                ring, slot, n, before = USE[step]
                dve.wait_ge(freed[ring, slot, "dve"], before["dve"] + 1)

            dve.wait_ge(loaded["cond"], 16)
            V.tensor_reduce(tf[:, 0:B], cond, axis=AX.X, op=ALU.add).then_inc(exps_ready, 1)
            dve.wait_ge(loaded["fs"], 16)
            V.tensor_scalar_min(ekv, fsT, 30.0).then_inc(exps_ready, 1)
            dve.wait_ge(loaded["const"], 32)
            st(V.tensor_copy(identb, ident))
            st(V.tensor_copy(maskb, v3(c_["masks"], 4)))
            for flat in vflat + [uflat]:
                st(V.memset(flat, 1.0))
            dve.wait_ge(ek_ready, 2)
            link(V.tensor_scalar_add(tf[:, 0:B], tf[:, B:2 * B], 1.0))
            link(V.reciprocal(tf[:, B:2 * B], tf[:, 0:B]))
            st(V.tensor_scalar(tf[:, 2 * B:3 * B], tf[:, B:2 * B], 0.5, 0.5, ALU.mult, ALU.add))
            st(V.tensor_scalar(tf[:, 3 * B:4 * B], tf[:, B:2 * B], 0.1, 0.4, ALU.mult, ALU.add))
            dec3 = dec.rearrange("p (c b) -> p c b", b=B)
            V.tensor_scalar(dec3, small[:, 0:4 * CT].unsqueeze(2).to_broadcast([P, 4 * CT, B]), -1.0, None, ALU.mult
                            ).then_inc(exps_ready, 1)
            dve.wait_ge(ek_ready, 4)
            settle()
            link(V.tensor_tensor(dec3, dec3, tf[:, 2 * B:3 * B].unsqueeze(1).to_broadcast([P, 4 * CT, B]), ALU.mult))
            V.tensor_tensor(ekv, ek, fsT, ALU.mult).then_inc(consts_ready, 1)
            dve.wait_ge(consts_ready, 1)

            for step in ORDER:
                kind = step[0]
                if kind == "wkv":
                    _, c, b = step
                    n = NUMBER[step]
                    scan, euk, gk = scans[n % 2], euks[n % 2], gks[n % 2]
                    for ct in range(CT):
                        i = c * CT + ct
                        dd = dec[:, i * B + b:i * B + b + 1].to_broadcast([P, T])
                        for s, src in ((0, ekv), (2, ek)):
                            x_ = src[:, ct, bt(b)]
                            V.tensor_tensor_scan(scan[s][:, ct, :], dd, x_, 0.0, ALU.mult, ALU.add)
                            ins = V.tensor_tensor_scan(scan[s + 1][:, ct, ::-1], dd, x_[:, ::-1], 0.0, ALU.mult, ALU.add)
                    ins.then_inc(scanned, 1)
                    dve.wait_ge(euk_ready, CT * (n + 1))
                    V.scalar_tensor_tensor(out=gk, in0=euk, scalar=EXP30, in1=ek[:, :, bt(b)], op0=ALU.min,
                                           op1=ALU.subtract).then_inc(euk_used, 1)
                elif kind == "weigh":
                    _, c, b = step
                    n = NUMBER[step]
                    scan = scans[n % 2]
                    if c == 2:
                        dve.wait_ge(written["big"], USE["proj", 0, b][2] + 1)
                    elif c == 3:
                        dve.wait_ge(written["big"], USE["fc1", 1, MT - 1][2] + 1)
                    dve.wait_ge(summed, n + 1)
                    link(V.tensor_scalar_max(scan[2], scan[2], 1e-8))
                    link(V.reciprocal(scan[3], scan[2]))
                    V.scalar_tensor_tensor(out=G[c % 2][:, :, bt(b)], in0=scan[0], scalar=tf[:, 3 * B + b:3 * B + b + 1],
                                           in1=scan[3], op0=ALU.mult, op1=ALU.mult).then_inc(gate_ready, 1)
                    dve.wait_ge(gate_ready, n + 1)
                elif kind == "gate":
                    _, g, b = step
                    n = NUMBER[step]
                    dve.wait_ge(tanh_ready, n + 1)
                    y = G[g % 2][:, :, bt(b)]
                    V.scalar_tensor_tensor(out=y, in0=th, scalar=1.0, in1=y, op0=ALU.add, op1=ALU.mult
                                           ).then_inc(gated, 1)
                    dve.wait_ge(gated, n + 1)
                elif kind == "proj":
                    _, layer, b = step
                    n = NUMBER[step]
                    slot = filled(step)
                    if layer == 0:
                        if b >= NV:
                            dve.wait_ge(written["big"], USE["pv", 0, b - NV][2] + 1)
                        give_back(step, V.tensor_tensor(
                            vaug[b % NV][:, :, :, 0:HD], big(slot, 2).rearrange("p (t h e) -> p t h e", t=QT, h=H),
                            v3(bvb, H).unsqueeze(1).to_broadcast([P, QT, H, HD]), ALU.add))
                        after_give_back(step)
                        V.nop().then_inc(v_ready, 1)
                        ring, sl, nn, before = USE[step]
                        dve.wait_ge(freed[ring, sl, "act"], before["act"] + 1)
                    else:
                        if n:
                            dve.wait_ge(parts_used, n)
                        cosb = c_["cos"].unsqueeze(1).to_broadcast([P, CT, T])
                        for bank, o in ((0, "q"), (1, "k")):
                            src = v3(big(slot, bank), CT)
                            st(V.tensor_tensor(qf[o], src, cosb, ALU.mult))
                            ins = V.tensor_tensor(rest, src[:, ::-1, :], v3(c_["sin"], CT), ALU.mult)
                            if o == "k":
                                give_back(step, ins)
                                after_give_back(step)
                            else:
                                st(ins)
                            settle()
                            link(V.tensor_tensor(qf[o], qf[o], rest, ALU.add))
                            st(V.tensor_copy(part[o][:, 0], qf[o]))
                        settle()
                    for o in ("q", "k"):
                        link(V.tensor_tensor(rest, qf[o], part[o][:, 0], ALU.subtract))
                        link(V.tensor_copy(part[o][:, 1], rest))
                        ins = V.tensor_tensor(part[o][:, 2], rest, part[o][:, 1], ALU.subtract)
                        if o == "q":
                            link(ins)
                        else:
                            ins.then_inc(parts_ready, 1)
                            dve.wait_ge(parts_ready, n + 1)
                elif kind == "kscores":
                    _, layer, b, j = step
                    slot = filled(step)
                    hs = slice(j * GH, (j + 1) * GH)
                    n = rows_order.index(("kmax", layer, b))
                    mn, nb = v3(mneg, QT)[:, :, hs], v3(nbias, QT)[:, :, hs]
                    hi, lo = (v3(mpart[:, i * QT * H:(i + 1) * QT * H], QT)[:, :, hs] for i in range(2))
                    st(V.tensor_reduce(mneg[:, H + j * GH:H + (j + 1) * GH],
                                       wide(slot).rearrange("p a (h t) -> p (a h) t", h=2), axis=AX.X, op=ALU.max,
                                       negate=True))
                    link(V.tensor_reduce(mneg[:, j * GH:(j + 1) * GH],
                                         big(slot, 2).rearrange("p (h t) -> p h t", h=GH), axis=AX.X, op=ALU.max,
                                         negate=True))
                    link(V.tensor_scalar_min(mn, mn, NO_KEY))
                    if j == 0:
                        dve.wait_ge(written["small"], USE[rows_order[n - 1]][2] + 1)
                        if b:
                            ring, sl, nn, before = USE["kscores", layer, b - 1, NG - 1]
                            dve.wait_ge(freed[ring, sl, "act"], before["act"] + 1)
                    link(V.tensor_copy(hi, mn))
                    link(V.tensor_tensor(lo, mn, hi, ALU.subtract))
                    link(V.tensor_tensor(nb, hi, lo, ALU.add))
                    V.tensor_scalar_mul(nb, nb, SCORE_SCALE).then_inc(nbias_ready, 1)
                    if j == NG - 1:
                        dve.wait_ge(nbias_ready, NUMBER[step] + 1)
                        V.nop().then_inc(mparts_ready, 1)
                elif kind == "scores":
                    _, layer, b, j = step
                    slot = filled(step)
                    hs = slice(j * GH, (j + 1) * GH)
                    st(V.tensor_reduce(mneg[:, H + j * GH:H + (j + 1) * GH],
                                       wide(slot).rearrange("p a (h t) -> p (a h) t", h=2), axis=AX.X, op=ALU.max,
                                       negate=True))
                    give_back(step, V.tensor_reduce(mneg[:, j * GH:(j + 1) * GH],
                                                    big(slot, 2).rearrange("p (h t) -> p h t", h=GH), axis=AX.X,
                                                    op=ALU.max, negate=True))
                elif kind == "max":
                    _, layer, b = step
                    n = rows_order.index(step)
                    prev = ("scores", layer, b, NG - 1)
                    after_give_back(prev)
                    settle()
                    link(V.tensor_scalar_min(mneg, mneg, NO_KEY))
                    if n:
                        dve.wait_ge(written["small"], USE[rows_order[n - 1]][2] + 1)
                    link(V.tensor_copy(mpart[:, 0:QT * H], mneg))
                    V.tensor_tensor(mpart[:, QT * H:2 * QT * H], mneg, mpart[:, 0:QT * H], ALU.subtract
                                    ).then_inc(mparts_ready, 1)
                    dve.wait_ge(mparts_ready, n + 1)
                elif kind == "otr":
                    _, layer, b = step
                    n = NUMBER[step]
                    slot = filled(step)
                    o_ = wide(slot).rearrange("p t (h e) -> p t h e", h=H)
                    if n:
                        prev = [s for s in ORDER if s[0] == "oT"][n - 1]
                        dve.wait_ge(written["big"], USE[prev][2] + 1)
                    r_ = v3(rec, QT)
                    link(V.reciprocal(r_, o_[:, :, :, HD]))
                    give_back(step, V.tensor_tensor(otok.rearrange("p t (h e) -> p t h e", h=H), o_[:, :, :, 0:HD],
                                                    r_.unsqueeze(3).to_broadcast([P, QT, H, HD]), ALU.mult))
                    after_give_back(step)
                    V.nop().then_inc(o_ready, 1)
                elif kind == "wo":
                    _, layer, b = step
                    slot = filled(step)
                    y = xT[:, :, bt(b)]
                    src = v3(big(slot, 0), CT)
                    if layer == 0:
                        for ct in range(CT):
                            ins = V.scalar_tensor_tensor(out=y[:, ct, :], in0=src[:, ct, :],
                                                         scalar=col["bo"][:, ct:ct + 1], in1=y[:, ct, :], op0=ALU.add,
                                                         op1=ALU.add)
                            if ct < CT - 1:
                                st(ins)
                            else:
                                give_back(step, ins)
                    else:
                        give_back(step, V.tensor_tensor(y, src, y, ALU.add))
                    after_give_back(step)
                    V.nop().then_inc(x_ready, 1)
                elif kind == "largest":
                    i = step[1]
                    if i == 0:
                        dve.wait_ge(loaded["tern"], 32)
                    V.tensor_reduce(small[:, 32 + i:33 + i], (w1, w2)[i], axis=AX.XY, op=ALU.max,
                                    apply_absolute_value=True).then_inc(tern_in, 1)
                elif kind == "ternary":
                    i = step[1]
                    w_ = (w1, w2)[i]
                    s_ = small
                    dve.wait_ge(tern_max, i + 1)
                    st(V.tensor_scalar(s_[:, 36:37], s_[:, 34 + i:35 + i], THRESHOLD, None, ALU.mult))
                    link(V.tensor_scalar(s_[:, 37:38], s_[:, 34 + i:35 + i], -THRESHOLD, None, ALU.mult))
                    tmp = tern_tmp(i)
                    if i:
                        dve.wait_ge(tern_abs, i)
                    link(V.tensor_scalar(tmp, w_, s_[:, 36:37], None, ALU.is_gt))
                    link(V.scalar_tensor_tensor(out=tmp, in0=w_, scalar=s_[:, 37:38], in1=tmp, op0=ALU.is_lt,
                                                op1=ALU.subtract))
                    link(V.scalar_tensor_tensor(out=w_, in0=w_, scalar=1.0, in1=tmp, op0=ALU.mult, op1=ALU.mult,
                                                accum_out=s_[:, 42 + 2 * i:43 + 2 * i]))
                    V.tensor_copy(w_, tmp).then_inc(tern_cnt, 1)
                elif kind == "alpha":
                    i = step[1]
                    s_ = small
                    dve.wait_ge(tern_sum, i + 1)
                    link(V.tensor_scalar_max(s_[:, 48:49], s_[:, 47 + 4 * i:48 + 4 * i], 1.0))
                    link(V.reciprocal(s_[:, 49:50], s_[:, 48:49]))
                    V.tensor_tensor(s_[:, 56 + i:57 + i], s_[:, 46 + 4 * i:47 + 4 * i], s_[:, 49:50], ALU.mult
                                    ).then_inc(tern_ready, 1)
                    dve.wait_ge(tern_ready, i + 1)
                elif kind == "fc2":
                    _, h, c = step
                    n = NUMBER[step]
                    dve.wait_ge(ffn_ready, n + 1)
                    st(V.tensor_reduce(small[:, 60 + n:61 + n], ffn[:, c, h * 512:(h + 1) * 512], axis=AX.X,
                                       op=ALU.max, apply_absolute_value=True))
                elif kind == "quant":
                    settle()
                    V.tensor_reduce(small[:, 64:65], small[:, 60:64], axis=AX.X, op=ALU.max).then_inc(amax_in, 1)
                    dve.wait_ge(amax_out, 1)
                    link(V.tensor_scalar(small[:, 66:67], small[:, 65:66], 1.0 / QMAX, 1e-8, ALU.mult, ALU.add))
                    link(V.reciprocal(small[:, 67:68], small[:, 66:67]))
                elif kind == "requant":
                    b = step[1]
                    f = ffn[:, :, bt(b)]
                    link(V.tensor_scalar(f, f, small[:, 67:68], ROUND, ALU.mult, ALU.add))
                    link(V.tensor_scalar(f, f, -ROUND, QMAX, ALU.add, ALU.min))
                    link(V.tensor_scalar(f, f, -QMAX, small[:, 66:67], ALU.max, ALU.mult))
                    y = xT[:, :, bt(b)]
                    V.tensor_tensor(y, y, f, ALU.add).then_inc(x_ready, 1)
                elif kind == "beta":
                    b = step[1]
                    slot = filled(step)
                    give_back(step, V.tensor_tensor(v3(beta[b % 2], QT), v3(single(slot)[:, 0:QT * H], QT),
                                                    bbb.unsqueeze(1).to_broadcast([P, QT, H]), ALU.add))
                    after_give_back(step)
                elif kind == "den":
                    b = step[1]
                    ring, sl, nn, before = USE["kscores", 1, b, NG - 1]
                    dve.wait_ge(freed[ring, sl, "act"], before["act"] + 1)
                    link(V.tensor_scalar_max(cc[b % 2], cc[b % 2], 1e-20))
                    link(V.reciprocal(cT, cc[b % 2]))
                    link(V.tensor_tensor(cc[b % 2], cT, beta[b % 2], ALU.mult))
                elif kind == "blocks":
                    b = step[1]
                    if b:
                        dve.wait_ge(inv_ready, b)
                    if b >= 2:
                        dve.wait_ge(written["small"], USE["solve", b - 2, QT * NB - 1][2] + 1)
                    blk_src = invT[b % 2]
                    ring, sl, nn, before = USE["kprobs", 1, b, NG - 1]
                    dve.wait_ge(freed[ring, sl, "act"], before["act"] + 1)
                    st(V.transpose(cT, cc[b % 2]))
                    kp = kprob[b % 2]
                    for r in range(NB):
                        rows = slice(r * BLK, (r + 1) * BLK)
                        for t in range(QT):
                            at = t * T + r * BLK
                            st(V.tensor_copy(v3(blk_src[rows, t * H * BLK:(t + 1) * H * BLK], H),
                                             kp[rows, :, at:at + BLK]))
                    settle()
                    V.transpose(blkA.rearrange("p (i j) -> p i j", i=BLK),
                                blk_src.rearrange("p (n i) -> p i n", i=BLK)).then_inc(blocks_ready, 1)
                    dve.wait_ge(blocks_ready, b + 1)
                elif kind == "inverse":
                    b = step[1]
                    dve.wait_ge(inv_ready, b + 1)
                    if b >= 2:
                        dve.wait_ge(written["small"], USE["solve", b - 2, QT * NB - 1][2] + 1)
                    V.transpose(invT[b % 2].rearrange("p (n i) -> p i n", i=BLK),
                                blkX.rearrange("p (i j) -> p i j", i=BLK)).then_inc(invT_ready, 1)
                    dve.wait_ge(invT_ready, b + 1)
                    ring, sl, nn, before = USE["proj", 1, b]
                    dve.wait_ge(freed[ring, sl, "act"], before["act"] + 1)
                    rows = slice(0, BLK)
                    V.tensor_copy(v3(zz[rows, :], H), vaug[b % NV][rows, 0, :, 0:HD]).then_inc(z_ready, 1)
                elif kind == "gather":
                    _, b, s = step
                    t, r = divmod(s, NB)
                    rows = slice(r * BLK, (r + 1) * BLK)
                    slot = filled(step)
                    cb = cc[b % 2][rows, t * H:(t + 1) * H].unsqueeze(2).to_broadcast([BLK, H, HD])
                    give_back(step, V.tensor_tensor(v3(zt[rows, :], H), v3(single(slot)[rows, 0:H * HD], H), cb,
                                                    ALU.mult))
                    after_give_back(step)
                    V.tensor_tensor(v3(zz[rows, :], H), vaug[b % NV][rows, t, :, 0:HD], v3(zt[rows, :], H),
                                    ALU.subtract).then_inc(z_ready, 1)
                elif kind == "solve":
                    _, b, s = step
                    t, r = divmod(s, NB)
                    rows = slice(r * BLK, (r + 1) * BLK)
                    slot = filled(step)
                    if s == 0 and b:
                        dve.wait_ge(written["big"], USE["pv", 1, b - 1][2] + 1)
                    give_back(step, V.tensor_copy(uaug[rows, t, :, 0:HD], v3(single(slot)[rows, 0:H * HD], H)))
                    after_give_back(step)
                    V.nop().then_inc(u_ready, 1)
                elif kind == "route":
                    slot = filled(step)
                    lg = v3(single(slot)[:, 0:NT * E], NT)

                    def e8(ap):
                        return ap.unsqueeze(2).to_broadcast([P, NT, E])

                    def r3(k):
                        return v3(R[k], NT)
                    st(V.memset(zero, 0.0))
                    settle()
                    V.nop().then_inc(zeroed, 1)
                    link(V.reduce_max(R["mx"], lg, AX.X))
                    give_back(step, V.tensor_tensor(r3("logit"), lg, e8(R["mx"]), ALU.subtract))
                    after_give_back(step)
                    V.nop().then_inc(logits_exp_in, 1)
                    dve.wait_ge(logits_exp, 1)
                    link(V.reduce_sum(R["sum"], r3("exp"), AX.X))
                    link(V.reciprocal(R["rec"], R["sum"]))
                    link(V.tensor_tensor(r3("score"), r3("exp"), e8(R["rec"]), ALU.mult))
                    revb = c_["rev"].unsqueeze(1).to_broadcast([P, NT, E])
                    cur = "score"
                    for s in range(2):
                        link(V.reduce_max(R["m"][s], r3(cur), AX.X))
                        link(V.tensor_tensor(r3("t1"), r3(cur), e8(R["m"][s]), ALU.is_equal))
                        link(V.tensor_tensor(r3("t1"), r3("t1"), revb, ALU.mult))
                        link(V.reduce_max(R["key"][s], r3("t1"), AX.X))
                        link(V.tensor_tensor(v3(R["oh"][s], NT), revb, e8(R["key"][s]), ALU.is_equal))
                        if s == 0:
                            link(V.scalar_tensor_tensor(out=r3("score2"), in0=v3(R["oh"][0], NT), scalar=-2.0,
                                                        in1=r3("score"), op0=ALU.mult, op1=ALU.add))
                            cur = "score2"
                    link(V.tensor_tensor(R["tmp"][0], R["m"][0], R["m"][1], ALU.add))
                    link(V.tensor_scalar_max(R["tmp"][0], R["tmp"][0], 1e-9))
                    link(V.reciprocal(R["tmp"][1], R["tmp"][0]))
                    for s in range(2):
                        st(V.tensor_tensor(R["gate"][s], R["m"][s], R["tmp"][1], ALU.mult))
                    st(V.memset(R["pre"][0][:, 0:E], 0.0))
                    settle()
                    for s in range(2):
                        oh, pre = v3(R["oh"][s], NT), v3(R["pre"][s], NT)
                        for t in range(1, NT):
                            link(V.tensor_tensor(pre[:, t], pre[:, t - 1], oh[:, t - 1], ALU.add))
                        if s == 0:
                            link(V.tensor_tensor(R["pre"][1][:, 0:E], pre[:, NT - 1], oh[:, NT - 1], ALU.add))
                    V.nop().then_inc(choice_ready, 1)
                elif kind == "rank":
                    slot = filled(step)
                    for s in range(2):
                        lo = single(slot)[:, s * NT * E:(s + 1) * NT * E]
                        ins = V.tensor_tensor(R["t1"] if s == 0 else R["exp"], lo, R["oh"][s], ALU.mult)
                        if s == 0:
                            st(ins)
                        else:
                            give_back(step, ins)
                    after_give_back(step)
                    settle()
                    for s in range(2):
                        pos, key = R["pos"][s], R["key"][s]
                        link(V.reduce_sum(pos, v3(R["t1"] if s == 0 else R["exp"], NT), AX.X))
                        link(V.tensor_scalar(R["valid"][s], pos, float(CAP), None, ALU.is_le))
                        link(V.tensor_scalar(R["base"][s], key, -float(CAP), float(E * CAP), ALU.mult, ALU.add))
                        link(V.tensor_scalar(R["tmp"][0], pos, -1.0, None, ALU.add))
                        link(V.tensor_tensor(R["slot"][s], R["base"][s], R["tmp"][0], ALU.add))
                        link(V.tensor_tensor(R["tmp"][0], R["tmp"][0], R["valid"][s], ALU.mult))
                        link(V.tensor_tensor(R["tmp"][1], R["base"][s], R["tmp"][0], ALU.add))
                        link(V.tensor_copy(idx_g[s], R["tmp"][1]))
                        tr = c_["trash"][:, s * NT:(s + 1) * NT]
                        link(V.tensor_tensor(R["tmp"][0], R["slot"][s], tr, ALU.subtract))
                        link(V.tensor_tensor(R["tmp"][0], R["tmp"][0], R["valid"][s], ALU.mult))
                        link(V.tensor_tensor(R["tmp"][0], R["tmp"][0], tr, ALU.add))
                        link(V.tensor_copy(idx_s[s], R["tmp"][0]))
                        link(V.tensor_tensor(R["gate"][s], R["gate"][s], R["valid"][s], ALU.mult))
                    V.nop().then_inc(rt_ready, 1)
                elif kind == "xtok":
                    n = step[1]
                    slot = filled(step)
                    give_back(step, V.tensor_copy(xtok[:, 2 * n:2 * n + 2, :], v3(big(slot, 0), 2)))
                    after_give_back(step)
                elif kind == "dispT":
                    e = step[1]
                    slot = filled(step)
                    if e >= 2:
                        dve.wait_ge(written["big"], USE["up", e - 2, 1][2] + 1)
                    give_back(step, V.tensor_copy(dT[e % 2], v3(big(slot, 0), CT)))
                    after_give_back(step)
                    V.nop().then_inc(dT_ready, 1)
                elif kind == "down":
                    e = step[1]
                    slot = filled(step)
                    if e == 0:
                        dve.wait_ge(b2_loaded, 16)
                    if e >= 2:
                        dve.wait_ge(eo_stored[e % 2], 16 * (e // 2))
                    give_back(step, V.tensor_tensor(eo[e % 2], v3(big(slot, 0), 2),
                                                    b2b[:, e, :].unsqueeze(1).to_broadcast([P, 2, D]), ALU.add))
                    after_give_back(step)
                    V.nop().then_inc(eo_ready, 1)
                elif kind == "combine":
                    t = step[1]
                    dve.wait_ge(gathered, 16 * 2 * NT)
                    link(V.scalar_tensor_tensor(out=outt[:, t, :], in0=got[0][:, t, :], scalar=R["gate"][0][:, t:t + 1],
                                                in1=xtok[:, t, :], op0=ALU.mult, op1=ALU.add))
                    V.scalar_tensor_tensor(out=outt[:, t, :], in0=got[1][:, t, :], scalar=R["gate"][1][:, t:t + 1],
                                           in1=outt[:, t, :], op0=ALU.mult, op1=ALU.add).then_inc(out_ready, 1)

        @block.gpsimd
        def _(pool):
            own = [0]

            def link(ins):
                own[0] += 1
                ins.then_inc(pool_own, 1)
                pool.wait_ge(pool_own, own[0])

            RED = bass.bass_isa.ReduceOp
            G_ = nc.gpsimd

            def ones_rows(layer):
                for par in range(2):
                    two = stack["k", par][SROWS:MROWS, :, :].rearrange("p h t -> p (h t)").bitcast(F32)
                    G_.memset(two, TWO_BF16_ONES).then_inc(ones_ready, 1)
                    pool.wait_ge(ones_ready, 2 * layer + par + 1)
            ones_rows(0)
            for step in ORDER:
                kind = step[0]
                if kind == "wkv":
                    _, c, b = step
                    n = NUMBER[step]
                    scan, gk = scans[n % 2], gks[n % 2]
                    pool.wait_ge(scanned, n + 1)
                    link(G_.tensor_tensor(scan[0], scan[0], scan[1], ALU.add))
                    link(G_.tensor_tensor(scan[2], scan[2], scan[3], ALU.add))
                    pool.wait_ge(euk_used, n + 1)
                    link(G_.tensor_tensor(scan[2], scan[2], gk, ALU.add))
                    link(G_.tensor_tensor(gk, gk, fsT[:, :, bt(b)], ALU.mult))
                    G_.tensor_tensor(scan[0], scan[0], gk, ALU.add).then_inc(summed, 1)
                    pool.wait_ge(summed, n + 1)
                elif kind == "largest":
                    i = step[1]
                    pool.wait_ge(tern_in, i + 1)
                    G_.partition_all_reduce(small[:, 34 + i:35 + i], small[:, 32 + i:33 + i], P, RED.max
                                            ).then_inc(tern_max, 1)
                    pool.wait_ge(tern_max, i + 1)
                elif kind == "ternary":
                    i = step[1]
                    pool.wait_ge(tern_cnt, i + 1)
                    pool.wait_ge(tern_abs, i + 1)
                    G_.partition_all_reduce(small[:, 46 + 4 * i:48 + 4 * i], small[:, 42 + 2 * i:44 + 2 * i], P, RED.add
                                            ).then_inc(tern_sum, 1)
                    pool.wait_ge(tern_sum, i + 1)
                elif kind == "quant":
                    pool.wait_ge(amax_in, 1)
                    G_.partition_all_reduce(small[:, 65:66], small[:, 64:65], P, RED.max).then_inc(amax_out, 1)
                    pool.wait_ge(amax_out, 1)
                elif kind == "requant" and step[1] == 0:
                    pool.wait_ge(ffn_ready, 2 * CT)
                    ones_rows(1)
                elif kind == "wo" and step[1] == 0 and step[2] == B - 1:
                    pool.wait_ge(written["big"], USE[step][2] + 1)
                    for w_, n_ in ((wq, "wq1"), (wk, "wk1"), (wv, "wv1"), (wo, "wo1")):
                        G_.dma_start(w_, d[n_]).then_inc(loaded["att1"], 16)
                elif kind == "route":
                    pool.wait_ge(written["small"], USE["beta", B - 1][2] + 1)
                    G_.dma_start(wb[:, :, 0:E], d["wg"]).then_inc(loaded["att1"], 16)
                elif kind == "blocks":
                    b = step[1]
                    pool.wait_ge(blocks_ready, b + 1)
                    if b:
                        pool.wait_ge(invT_ready, b)
                    A3 = blkA.rearrange("p (i j) -> p i j", i=BLK)
                    X3 = blkX.rearrange("p (i j) -> p i j", i=BLK)
                    link(G_.tensor_tensor(A3, A3, cT.unsqueeze(2).to_broadcast([P, BLK, BLK]), ALU.mult))
                    link(G_.memset(blkX, 0.0))
                    link(G_.affine_select(out=X3, in_=X3, compare_op=ALU.not_equal, fill=1.0, base=0,
                                          pattern=[[1, BLK], [-1, BLK]], channel_multiplier=0))
                    for k in range(BLK - 1):
                        rows, w = BLK - 1 - k, k + 1
                        tmp = blkT[:, 0:rows * w].rearrange("p (i j) -> p i j", i=rows)
                        link(G_.tensor_tensor(tmp, A3[:, k + 1:BLK, k:k + 1].to_broadcast([P, rows, w]),
                                              X3[:, k:k + 1, 0:w].to_broadcast([P, rows, w]), ALU.mult))
                        ins = G_.tensor_tensor(X3[:, k + 1:BLK, 0:w], X3[:, k + 1:BLK, 0:w], tmp, ALU.subtract)
                        if k < BLK - 2:
                            link(ins)
                        else:
                            ins.then_inc(inv_ready, 1)
                            pool.wait_ge(inv_ready, b + 1)
                elif kind == "dispT" and step[1] == 0:
                    pool.wait_ge(rt_ready, 1)
                    pool.wait_ge(ytok_ready, B)
                    pool.wait_ge(disp_zero, 16)
                    for s in range(2):
                        for t in range(NT):
                            G_.indirect_dma_start(out=d["disp"], out_offset=bass.IndirectOffsetOnAxis(
                                ap=idx_s[s][:, t:t + 1], axis=0), in_=ytok[:, t, :], in_offset=None
                            ).then_inc(scattered, 16)
                elif kind == "combine":
                    t = step[1]
                    if t == 0:
                        pool.wait_ge(eo_stored[0], 16 * (E // 2))
                        pool.wait_ge(eo_stored[1], 16 * (E // 2))
                    for s in range(2):
                        G_.indirect_dma_start(out=got[s][:, t, :], out_offset=None, in_=d["eo"],
                                              in_offset=bass.IndirectOffsetOnAxis(ap=idx_g[s][:, t:t + 1], axis=0)
                                              ).then_inc(gathered, 16)



def _tables():
    p = np.arange(P)
    out = {"ident": np.eye(P), "tri": p[:, None] <= p[None, :], "ones": np.ones((P, P))}
    inv_freq = 1.0 / np.float32(10000.0) ** (np.arange(HALF, dtype=np.float32) / HALF)
    ang = (np.arange(T, dtype=np.float32)[:, None] * inv_freq[None, :].astype(np.float32)).astype(np.float32)
    of = p // H
    cos, sin = np.cos(ang).T[of], np.sin(ang).T[of]
    out["cos"] = cos
    out["sin"] = np.concatenate([-sin, sin], axis=1)
    later = p[None, :] > p[:, None]
    masks = [later, later.T, later | np.eye(P, dtype=bool), later.T | np.eye(P, dtype=bool)]
    out["masks"] = np.concatenate([np.where(m, MASKED, 0.0) for m in masks], axis=1)
    out["rev"] = np.tile(E - np.arange(E), (P, 1))
    out["trash"] = E * CAP + np.arange(2 * NT)[None, :] * P + p[:, None]
    return np.concatenate([np.asarray(out[k], np.float32) for k in CONSTS], axis=1)


def _rows(a):
    return np.ascontiguousarray(a.reshape(-1, P, a.shape[-1]).transpose(1, 0, 2))


def _col(a):
    return a.reshape(-1, P).T


def kernel(**inputs):
    import concourse.bacc as bacc
    from concourse.bass_utils import run_bass_kernel_spmd

    a = {k: np.asarray(v) for k, v in inputs.items()}
    ct, dd, hh = np.meshgrid(np.arange(CT), np.arange(HALF), np.arange(H), indexing="ij")
    perm = (hh * HD + ct * HALF + dd).reshape(-1)
    cols = [_col(a[f"{g}_{k}"]) for k in "wu" for g in ("L0_cond", "L0_cond2", "L1_cond", "L1_cond2")]
    cols += [_col(a["L0_attn_bq"][perm]), _col(a["L0_attn_bk"][perm]), _col(a["L0_attn_bo"]), _col(a["L0_ffn_b1"]),
             _col(a["L0_ffn_b2"]), _col(a["L1_ffn_fc1_b"].reshape(-1))]
    arrays = {
        "consts": _tables(), "columns": np.ascontiguousarray(np.concatenate(cols, axis=1)), "cond": a["cond_512"],
        "fsT": _rows(a["fside_BxSxS_0"].reshape(N, D).T), "xT": _rows(a["x"].reshape(N, D).T),
        "bv": a["L0_attn_bv"], "bb": a["L1_attn_bb"], "wb": _rows(a["L1_attn_Wb"]), "wg": _rows(a["L1_ffn_wg"]),
        "w1T": _rows(a["L0_ffn_W1"].T), "w2T": _rows(a["L0_ffn_W2"].T),
        "fc1": np.stack([_rows(w) for w in a["L1_ffn_fc1_w"]]), "fc2": np.stack([_rows(w) for w in a["L1_ffn_fc2_w"]]),
        "fb2": a["L1_ffn_fc2_b"],
    }
    for layer in range(2):
        for name, cols_ in (("q", perm), ("k", perm), ("v", slice(None)), ("o", slice(None))):
            arrays[f"w{name}{layer}"] = _rows(a[f"L{layer}_attn_W{name}"][:, cols_])
    nc = bacc.Bacc("TRN2", target_bir_lowering=False, num_devices=1)
    d = {}
    for name, arr in arrays.items():
        arrays[name] = np.ascontiguousarray(arr)
        d[name] = nc.dram_tensor(name, arr.shape, mybir.dt.from_np(arr.dtype), kind="ExternalInput").ap()
    d["disp"] = nc.dram_tensor("dispatched", (E * CAP + 2 * N, D), F32, kind="Internal").ap()
    d["eo"] = nc.dram_tensor("expert_rows", (E * CAP, D), F32, kind="Internal").ap()
    d["out"] = nc.dram_tensor("out", (N, D), F32, kind="ExternalOutput").ap()
    program(nc, d)
    r = run_bass_kernel_spmd(nc, [arrays], core_ids=[0])
    return r.results[0]["out"].reshape(B, T, D)
```

```python
from contextlib import ExitStack

import numpy as np

import concourse.bass as bass
from concourse import mybir

F32 = mybir.dt.float32
F32R = mybir.dt.float32r
BF16 = mybir.dt.bfloat16
I32 = mybir.dt.int32
ALU = mybir.AluOpType
ACT = mybir.ActivationFunctionType
AX = mybir.AxisListType

P = 128
B, T, D = 4, 256, 256
N = B * T
CT = D // P
H = 16
HD = D // H
HALF = HD // 2
QT = T // P
VW = HD + 1
NW = 2
NV = 3
GH = 4
NG = H // GH
HID = 1024
MT = HID // P
E = 8
CAP = 2 * N // E
TD = 64
NT = N // P
BLK = 32
NB = P // BLK
RUNS_Q = ((0, 1), (0, 2), (1, 3), (0, 1))
RUNS_K = ((0, 2), (0, 2), (0, 1), (2, 3))
SROWS = sum(hi - lo for lo, hi in RUNS_Q) * HD
MROWS = SROWS + 2
MASKED = -1e30
NO_KEY = 1e20
TWO_BF16_ONES = float(np.array([0x3F803F80], np.uint32).view(np.float32)[0])
EXP30 = float(np.exp(np.float32(30.0)))
ROUND = 12582912.0
QMAX = 7.0
THRESHOLD = 0.05
SCORE_SCALE = 1.0 / HD ** 0.5

PRODUCTS = ((0, 0), (0, 1), (1, 0))

RINGS = {
    "proj": ("big", ("act", "dve")), "scores": ("big", ("dve",)), "probs": ("big", ("act",)),
    "kscores": ("big", ("act",)), "kprobs": ("big", ("act",)),
    "pv": ("big", ("act",)), "otr": ("big", ("dve",)),
    "oT": ("big", ("act",)), "wo": ("big", ("dve",)),
    "fc1": ("big", ("act",)), "fc2": ("big", ("act",)),
    "ytok": ("big", ("act",)), "xtok": ("big", ("dve",)), "dispT": ("small", ("dve",)),
    "up": ("big", ("dve",)), "down": ("small", ("dve",)),
    "max": ("small", ("act",)), "kmax": ("small", ("act",)),
    "beta": ("big", ("dve",)),
    "gather": ("small", ("dve",)), "solve": ("small", ("dve",)),
    "route": ("small", ("dve",)), "rank": ("small", ("dve",)),
}


def interleave(first, second):
    o = []
    for i in range(max(len(first), len(second))):
        o += first[i:i + 1] + second[i:i + 1]
    return o


def make_order():
    def groups(kind, layer, b):
        return [(kind, layer, b, j) for j in range(NG)]

    o = [("wkv", 0, 0), ("wkv", 0, 1), ("weigh", 0, 0), ("gate", 0, 0), ("proj", 0, 0), ("split", 0, 0), ("weigh", 0, 1),
         ("gate", 0, 1), ("wkv", 0, 2), ("proj", 0, 1), ("split", 0, 1), ("wkv", 1, 0), ("weigh", 0, 2)]
    o += groups("scores", 0, 0) + [("minus", 0, 0), ("max", 0, 0), ("weigh", 1, 0)]
    units = [[("wkv", 0, 3), ("wkv", 1, 1), ("weigh", 0, 3), ("weigh", 1, 1), ("wkv", 2, 0), ("largest", 0), ("largest", 1),
              ("weigh", 2, 0)],
             [("wkv", 1, 2), ("ternary", 0), ("weigh", 1, 2), ("wkv", 2, 1), ("weigh", 2, 1)],
             [("wkv", 1, 3), ("ternary", 1), ("weigh", 1, 3), ("wkv", 2, 2), ("weigh", 2, 2)],
             [("wkv", 2, 3), ("alpha", 0), ("alpha", 1), ("weigh", 2, 3)]]
    for b in range(B):
        o += [("probs", 0, b, 0), ("probs", 0, b, 1)]
        if b + 1 < B:
            o.append(("scores", 0, b + 1, 0))
        o += [("probs", 0, b, 2), ("probs", 0, b, 3)]
        if b + 1 < B:
            o += [("scores", 0, b + 1, j) for j in range(1, NG)] + [("minus", 0, b + 1), ("max", 0, b + 1)]
        if b + 2 < B:
            o += [("gate", 0, b + 2), ("proj", 0, b + 2), ("split", 0, b + 2)]
        o += [("pv", 0, b)] + units[b][0:2] + [("otr", 0, b)] + units[b][2:3] + [("oT", 0, b), ("wo", 0, b), ("gate", 1, b)]
        o += units[b][3:]
    o += [("wkv", 3, 0), ("wkv", 3, 1)]
    o += [("fc1", h, m) for h in range(2) for m in range(MT)]
    o += [("weigh", 3, 0), ("wkv", 3, 2), ("weigh", 3, 1), ("fc2", 0, 0), ("wkv", 3, 3), ("weigh", 3, 2), ("fc2", 0, 1),
          ("weigh", 3, 3), ("fc2", 1, 0), ("fc2", 1, 1), ("quant",)]
    o += [("requant", 0), ("gate", 2, 0)] + [("requant", b) for b in range(1, B)] + [
        ("proj", 1, 0), ("split", 1, 0), ("beta", 0), ("gate", 2, 1)]
    o += [("proj", 1, 1)] + groups("kscores", 1, 0) + [("kmax", 1, 0)] + groups("scores", 1, 0)[:2] + groups("kprobs", 1, 0)
    o += [("den", 0), ("blocks", 0), ("split", 1, 1), ("beta", 1)]
    o += groups("scores", 1, 0)[2:] + [("minus", 1, 0), ("max", 1, 0)] + groups("kscores", 1, 1) + [("kmax", 1, 1), ("gate", 2, 2)]
    behind = [[g] for g in groups("probs", 1, 0) + groups("kprobs", 1, 1)]
    behind += [[("den", 1), ("blocks", 1)], [("proj", 1, 2)], [("split", 1, 2), ("beta", 2)]]
    for b in range(B):
        solve = [[("inverse", b), ("solve", b, 0, 0), ("solve", b, 0, 1)]]
        for s in range(1, QT * NB):
            solve += [[(kind, b, s, half) for half in range(2)] for kind in ("gather", "solve")]
        ahead = behind
        if b + 1 < B:
            ahead += [[g] for g in groups("scores", 1, b + 1)]
            ahead[-1].append(("minus", 1, b + 1))
        if b + 2 < B:
            ahead += [[g] for g in groups("kscores", 1, b + 2)]
            ahead[-3].append(("max", 1, b + 1))
            ahead.append([])
            ahead.append([("kmax", 1, b + 2)])
        elif b + 1 < B:
            ahead.append([])
            ahead.append([("max", 1, b + 1)])
        if b and b + 1 < B:
            ahead[0][0:0] = [("den", b + 1), ("blocks", b + 1)]
        o += sum(interleave(solve, ahead), [])
        o += [("pv", 1, b)]
        if b + 2 < B:
            o += groups("kprobs", 1, b + 2)
        behind = [[("otr", 1, b)]]
        if b + 1 < B:
            behind += [[g] for g in groups("probs", 1, b + 1)]
        behind += [[("oT", 1, b)], [("wo", 1, b), ("gate", 3, b)]]
        if b + 3 < B:
            behind[4:4] = [[("gate", 2, b + 3)], [("proj", 1, b + 3)], [("split", 1, b + 3), ("beta", b + 3)]]
    o += sum(behind, [])
    o += [("route",)] + [("ytok", i) for i in range(B)] + [("choice", 0), ("rank", 0), ("choice", 1), ("rank", 1)]
    o += [("xtok", i) for i in range(B)]
    o += [("wsplit", 0, 0), ("wsplit", 0, 1), ("wsplit", 1, 0), ("wsplit", 1, 1), ("dispT", 0), ("up", 0, 0), ("dispT", 1), ("hsplit", 0, 0), ("up", 0, 1)]
    for e in range(E - 2):
        o += [("hsplit", e, 1), ("wsplit", e + 2, 0), ("up", e + 1, 0), ("dispT", e + 2), ("hsplit", e + 1, 0), ("down", e),
              ("wsplit", e + 2, 1), ("up", e + 1, 1)]
    o += [("hsplit", E - 2, 1), ("up", E - 1, 0), ("up", E - 1, 1), ("hsplit", E - 1, 0), ("hsplit", E - 1, 1),
          ("down", E - 2), ("down", E - 1)]
    o += [("combine", t) for t in range(NT)]
    return o


ORDER = make_order()


def lag(order):
    o, held, solving = [], [], False
    for step in order:
        chain = step[0] in ("inverse", "gather", "solve")
        if step[0] == "inverse":
            solving = True
        if solving and not chain:
            held.append(step)
            continue
        o.append(step)
        if step[0] == "solve" and step[2] == QT * NB - 1 or not solving:
            solving = solving and step[-1] == 0
        if chain and step[-1] == 1 or not solving:
            o += held
            held = []
    return o + held


DVE_ORDER = lag(ORDER)


def count_rings():
    seen = {"big": 0, "small": 0}
    freed = {(r, s, e): 0 for r in seen for s in range(2) for e in ("act", "dve")}
    out = {}
    for step in ORDER:
        use = RINGS.get(step[0])
        if use is None:
            continue
        ring, engines = use
        n = seen[ring]
        slot = n % 2
        out[step] = (ring, slot, n, {e: freed[ring, slot, e] for e in ("act", "dve")})
        seen[ring] += 1
        for e in engines:
            freed[ring, slot, e] += 1
    return out


USE = count_rings()
NUMBER = {}
for _step in ORDER:
    NUMBER[_step] = sum(1 for s in NUMBER if s[0] == _step[0])

CONSTS = {"ident": P, "tri": P, "ones": P, "cos": T, "sin": CT * T, "masks": 4 * P, "rev": E,
          "trash": 2 * NT}
CONST_W = sum(CONSTS.values())
CONST_AT = {}
_at = 0
for _k, _w in CONSTS.items():
    CONST_AT[_k] = _at
    _at += _w
COLS = {"w": 4 * CT, "u": 4 * CT, "bq": CT, "bk": CT, "bo": CT, "b1": MT, "b2": CT, "fb1": E * MT}
COL_W = sum(COLS.values())
COL_AT = {}
_at = 0
for _k, _w in COLS.items():
    COL_AT[_k] = _at
    _at += _w


PARTS_W = 2 * 2 * (CT * HID + MT * D + MT * CAP + CT * CAP)


def program(nc, d):
    with ExitStack() as ctx:
        def sem(name):
            return ctx.enter_context(nc.semaphore(name))

        words = (nc.sbuf_usable_end - nc.sbuf_base) // 4 - 16
        with nc.sbuf_tensor("arena", [P, words], F32) as arena:
            pass
        ctx.enter_context(nc.sbuf_tensor("below_parts", [P, words - PARTS_W], F32))
        psum = ctx.enter_context(nc.psum_tensor("psum", [P, 8, 512], F32))
        top = [0]

        def take(n, at=None):
            if at is None:
                at, top[0] = top[0], top[0] + n
                assert top[0] <= words, (top[0], words)
            return arena[:, at:at + n]

        def v3(ap, a):
            return ap.rearrange("p (a b) -> p a b", a=a)

        const = take(CONST_W)
        c_ = {k: const[:, CONST_AT[k]:CONST_AT[k] + w] for k, w in CONSTS.items()}
        ident, tri, ones = c_["ident"], c_["tri"], c_["ones"]
        cols = take(COL_W)
        col = {k: cols[:, COL_AT[k]:COL_AT[k] + w] for k, w in COLS.items()}
        identb = take(P // 2).bitcast(BF16)
        maskb = take(4 * P // 2).bitcast(BF16).rearrange("p (a b) -> p a b", a=4)
        QK, KQ, QK_STRICT, KQ_STRICT = range(4)
        tf = take(4 * B)
        dec = take(4 * CT * B)
        bvb = take(D)
        bbb = take(H)
        small = take(80)

        xT = v3(take(CT * N), CT)
        G = [v3(take(CT * N), CT) for _ in range(2)]
        wq, wk, wv, wo = (v3(take(CT * D), CT) for _ in range(4))
        wb = v3(take(CT * H), CT)
        th = v3(take(CT * T), CT)
        cond = v3(th[:, 0, :], B)

        r1 = top[0]
        stack = {}
        for name in ("q", "k", "kq"):
            for par in range(2):
                stack[name, par] = take(H * T // 2).bitcast(BF16).rearrange("p (h t) -> p h t", h=H)
        hid = v3(take(MT * N, at=r1), MT)
        ffn = v3(take(CT * N, at=r1 + MT * N), CT)

        part = take(2 * 3 * CT * T // 2).bitcast(BF16).rearrange("p (o a c) -> p o a c", o=2, a=3)
        qf = v3(take(2 * CT * T), 2)
        vflat = [take(QT * H * VW + 32 - VW) for _ in range(NV)]
        uflat = take(QT * H * VW + 32 - VW)
        vaug = [f[:, 0:QT * H * VW].rearrange("p (t h e) -> p t h e", t=QT, h=H) for f in vflat]
        uaug = uflat[:, 0:QT * H * VW].rearrange("p (t h e) -> p t h e", t=QT, h=H)
        prob = take(H * (T + P)).rearrange("p (h t) -> p h t", h=H)
        otok = v3(take(QT * D), QT)
        oT = v3(take(CT * T), CT)
        mnegs = {k: take(QT * H) for k in ("max", "kmax")}
        mparts = {k: take(QT * H).bitcast(BF16) for k in ("max", "kmax")}
        mT = [take(P // 2).bitcast(BF16) for _ in range(2)]
        rec = take(QT * H)

        r2 = top[0]
        fsT, ek, ekv = (v3(take(CT * N), CT) for _ in range(3))
        scans = [[v3(take(CT * T), CT) for _ in range(4)] for _ in range(2)]
        euks, gks = ([v3(take(CT * T), CT) for _ in range(2)] for _ in range(2))
        w1 = v3(take(CT * HID), CT)
        w2 = v3(take(MT * D), MT)
        e_end = top[0]
        top[0] = r2
        kprob = [take(H * (T + P)).rearrange("p (h t) -> p h t", h=H) for _ in range(2)]
        blkA = take(BLK * BLK)
        blkX = take(BLK * BLK)
        blkT = take(BLK * BLK // 4)
        invT = [take(BLK * BLK) for _ in range(2)]
        cT = take(BLK)
        beta = [take(QT * H) for _ in range(2)]
        cc = [take(QT * H) for _ in range(3)]
        nbias = take(QT * H)
        zz, zt = (c_["masks"][:, i * D:(i + 1) * D] for i in range(2))
        top[0] = max(top[0], e_end)

        def oraw(layer, b):
            return v3(oraw0 if layer == 0 else invT[b % 2], 4)

        top_all = top[0]
        top[0] = r1
        fcw = [(v3(take(CT * HID), CT), v3(take(MT * D), MT)) for _ in range(NW)]
        b2b = v3(G[0].rearrange("p a b -> p (a b)"), E)
        ytok_flat = take(NT * D)
        ytok = v3(ytok_flat, NT)
        xtok = v3(take(NT * D), NT)
        dtok = [v3(ytok_flat[:, i * 2 * D:(i + 1) * 2 * D], 2) for i in range(2)]
        eo = [v3(ytok_flat[:, i * 2 * D:(i + 1) * 2 * D], 2) for i in range(2, 4)]
        got = [v3(fcw[0][i].rearrange("p a b -> p (a b)"), NT) for i in range(2)]
        outt = v3(fcw[1][0].rearrange("p a b -> p (a b)"), NT)
        rt = take(24 * NT * E)
        idx = take(4 * NT).bitcast(I32)
        assert top[0] <= words - PARTS_W, (top[0], words, PARTS_W, r1)
        top[0] = max(top[0], top_all)

        def parts_of(name, rows, n):
            return [[ctx.enter_context(nc.sbuf_tensor(f"{name}_{which}_parts{i}", [P, rows, n], F32R))
                     for which in ("first", "second")] for i in range(2)]

        w_parts = [parts_of("fc1", CT, HID), parts_of("fc2", MT, D)]
        h_parts = parts_of("hidden", MT, CAP)
        d_parts = parts_of("input", CT, CAP)

        rows_order = [s for s in ORDER if s[0] in ("max", "kmax")]
        tern_flat = take(CT * HID, at=r1 + 4 * (H * T // 2))
        oraw0 = take(QT * H * 32, at=r1 + 5 * (H * T // 2))
        zero = oraw0[:, 0:D]

        def tern_tmp(i):
            return v3(tern_flat, (CT, MT)[i])

        def x_count(g, b):
            return (g - 1) * B + b + 1

        def stack_count(name, layer, b):
            n = b // 2 + 1
            if layer and name != "kq":
                n += B // 2
            return 16 * len(RUNS_Q) * n

        def row_count(name, layer, b):
            n = b // 2 + 1
            if layer and name == "q":
                n += B // 2
            return 16 * n

        R = {}
        rt_at = [0]

        def ra(n):
            rt_at[0] += n
            return rt[:, rt_at[0] - n:rt_at[0]]
        for k in ("logit", "exp", "score", "score2", "t1"):
            R[k] = ra(NT * E)
        for k in ("oh", "pre"):
            R[k] = [ra(NT * E) for _ in range(2)]
        for k in ("mx", "sum", "rec"):
            R[k] = ra(NT)
        for k in ("m", "key", "gate", "pos", "valid", "slot", "tmp", "base"):
            R[k] = [ra(NT) for _ in range(2)]
        idx_s = [idx[:, s * NT:(s + 1) * NT] for s in range(2)]
        idx_g = [idx[:, (2 + s) * NT:(3 + s) * NT] for s in range(2)]

        def big(slot, bank):
            return psum[:, 3 * slot + bank, :]

        def wide(slot):
            return psum[:, 3 * slot:3 * slot + 2, :]

        def single(slot):
            return psum[:, 6 + slot, :]

        loaded = {k: sem(f"loaded_{k}") for k in
                  ("const", "cond", "fs", "x", "att0", "tern", "att1")}
        written = {"big": sem("big_psum_written"), "small": sem("small_psum_written")}
        freed = {(r, s, e): sem(f"{r}_slot{s}_freed_by_{e}")
                 for r in ("big", "small") for s in range(2) for e in ("act", "dve")}
        act_own, dve_own, pool_own = sem("act_steps"), sem("dve_steps"), sem("pool_steps")
        ones_ready = sem("ones_rows_ready")
        consts_ready = sem("consts_ready")
        exps_ready = sem("exps_ready")
        ek_ready = sem("ek_ready")
        euk_ready = sem("euk_ready")
        euk_used = sem("euk_used")
        scanned = sem("recurrences_ready")
        summed = sem("sums_ready")
        nbias_ready = sem("minus_max_ready")
        gate_ready = sem("gate_ready")
        tanh_ready = sem("tanh_ready")
        gated = sem("gated")
        x_ready = sem("x_ready")
        parts_ready = sem("parts_ready")
        stacked = {(o, p): sem(f"stacked_{o}{p}") for o in ("q", "k", "kq") for p in range(2)}
        parts_used = sem("parts_stored")
        mparts_ready = {k: sem(f"{k}_parts_ready") for k in ("max", "kmax")}
        mrows = {(o, p): sem(f"max_rows_{o}{p}") for o in ("q", "kq") for p in range(2)}
        tern_in = sem("ternary_abs")
        tern_max = sem("ternary_max")
        tern_sum = sem("ternary_sums")
        tern_abs = sem("ternary_absolute")
        tern_cnt = sem("ternary_counts")
        w_first = sem("expert_weight_first_parts")
        w_second = [sem(f"expert_fc{i + 1}_second_parts") for i in range(2)]
        h_whole = sem("expert_hidden_activated")
        tern_ready = sem("ternary_ready")
        amax_in, amax_out = sem("quant_max_in"), sem("quant_max_out")
        blocks_ready = sem("blocks_ready")
        inv_ready = sem("inverses_ready")
        invT_ready = sem("inverses_T_ready")
        z_ready = sem("rhs_ready")
        zeroed = sem("zero_rows_ready")
        disp_zero = sem("dispatch_zeroed")
        logits_exp_in, logits_exp = sem("logits_in"), sem("logits_exp")
        choice_ready = sem("choice_ready")
        rt_ready = sem("indices_ready")
        scattered = sem("scattered")
        gather_ready = sem("gather_indices_ready")
        w_loaded = [sem(f"expert_weights_{i}") for i in range(NW)]
        b2_loaded = sem("expert_bias_loaded")
        dtok_loaded = [sem(f"dispatched_{i}") for i in range(2)]
        eo_stored = [sem(f"expert_out_stored_{i}") for i in range(2)]
        gathered = [sem(f"gathered_{t}") for t in range(NT)]
        out_ready = sem("out_ready")
        stored = sem("out_stored")

        block = ctx.enter_context(nc.Block())

        HALVES = [slice(i * H // 2, (i + 1) * H // 2) for i in range(2)]

        def bt(b):
            return slice(b * T, (b + 1) * T)

        def wait_done(eng, step, by):
            ring, slot, n, before = USE[step]
            eng.wait_ge(freed[ring, slot, by], before[by] + 1)

        @block.sync
        def _(sp):
            sp.dma_start(cond, d["cond"].rearrange("(o b) t -> o b t", o=1).to_broadcast([P, B, TD])).then_inc(loaded["cond"], 16)
            sp.dma_start(cols, d["columns"]).then_inc(loaded["const"], 16)
            sp.dma_start(fsT, d["fsT"]).then_inc(loaded["fs"], 16)
            sp.dma_start(const, d["consts"]).then_inc(loaded["const"], 16)
            sp.dma_start(xT, d["xT"]).then_inc(loaded["x"], 16)
            for w_, n_ in ((wq, "wq0"), (wk, "wk0"), (wv, "wv0"), (wo, "wo0")):
                sp.dma_start(w_, d[n_]).then_inc(loaded["att0"], 16)
            sp.dma_start(bvb, d["bv"].rearrange("(o c) -> o c", o=1).to_broadcast([P, D])).then_inc(loaded["att0"], 16)
            sp.dma_start(bbb, d["bb"].rearrange("(o c) -> o c", o=1).to_broadcast([P, H])).then_inc(loaded["att0"], 16)
            sp.dma_start(wb, d["wb"]).then_inc(loaded["att0"], 16)
            sp.dma_start(w1, d["w1T"]).then_inc(loaded["tern"], 16)
            sp.dma_start(w2, d["w2T"]).then_inc(loaded["tern"], 16)

            sp.wait_ge(zeroed, 1)
            sp.dma_start(d["disp"][0:E * CAP, :].rearrange("(p a) c -> p a c", p=P),
                         zero.unsqueeze(1).to_broadcast([P, E * CAP // P, D])).then_inc(disp_zero, 16)

            def load_expert(e):
                for i in range(2):
                    if e >= NW:
                        sp.wait_ge(w_second[i], e - NW + 1)
                    sp.dma_start(fcw[e % NW][i], d[("fc1", "fc2")[i]][e]).then_inc(w_loaded[e % NW], 16)

            def load_dispatched(e):
                if e >= 2:
                    sp.wait_ge(written["small"], USE["dispT", e - 2][2] + 1)
                sp.dma_start(dtok[e % 2], d["disp"][e * CAP:(e + 1) * CAP, :].rearrange("(s p) c -> p s c", p=P)
                             ).then_inc(dtok_loaded[e % 2], 16)

            for step in ORDER:
                kind = step[0]
                if kind == "split":
                    _, layer, b = step
                    par = b % 2
                    n = NUMBER[step]
                    sp.wait_ge(parts_ready, n + 1)
                    for i in range(2):
                        sp.dma_start(d["parts"][n, i].rearrange("a c p t -> p a c t"),
                                     part[:, 1 - i].rearrange("p a (c t) -> p a c t", c=CT)).then_inc(parts_used, 16)
                    sp.wait_ge(parts_used, 32 * (n + 1))
                    if b >= 2:
                        sp.wait_ge(written["big"], USE["probs", layer, b - 2, NG - 1][2] + 1)
                    elif layer == 1:
                        sp.wait_ge(written["big"], USE["probs", 0, b + 2, NG - 1][2] + 1)
                    names = [("k", 0, RUNS_K)] + ([("kq", 0, RUNS_Q)] if layer else []) + [("q", 1, RUNS_Q)]
                    for name, i, runs in names:
                        if name == "kq" and b == 0:
                            sp.wait_ge(x_ready, 2 * B)
                        rows = d["parts"][n, i].rearrange("a c (e h) t -> (a c e) h t", h=H)
                        r = 0
                        for lo, hi in runs:
                            sp.dma_start(stack[name, par][r:r + (hi - lo) * HD, :, :], rows[lo * HD:hi * HD, :, :]
                                         ).then_inc(stacked[name, par], 16)
                            r += (hi - lo) * HD
                elif kind in ("max", "kmax"):
                    _, layer, b = step
                    name = "q" if kind == "max" else "kq"
                    wait_done(sp, step, "act")
                    src = mT[rows_order.index(step) % 2]
                    sp.dma_start(stack[name, b % 2][SROWS:MROWS, :, :], src[0:2 * QT * H, :]
                                 ).then_inc(mrows[name, b % 2], 16)
                elif kind == "route":
                    sp.wait_ge(gated, NUMBER["gate", 3, B - 1] + 1)
                    for e in range(NW):
                        load_expert(e)
                    sp.dma_start(b2b, d["fb2"].rearrange("(o e) c -> o e c", o=1).to_broadcast([P, E, D])).then_inc(b2_loaded, 16)
                elif kind == "up" and step[1] == 0:
                    load_expert(NW + step[2])
                elif kind == "wsplit" and step[2] == 1 and NW <= step[1] < E - NW:
                    load_expert(step[1] + NW)
                elif kind == "dispT":
                    if step[1] == 0:
                        sp.wait_ge(scattered, 16 * 2 * NT)
                        load_dispatched(0)
                        load_dispatched(1)
                    if step[1] + 2 < E:
                        load_dispatched(step[1] + 2)
                elif kind == "down":
                    e = step[1]
                    wait_done(sp, step, "dve")
                    sp.dma_start(d["eo"][e * CAP:(e + 1) * CAP, :].rearrange("(s p) c -> p s c", p=P), eo[e % 2]
                                 ).then_inc(eo_stored[e % 2], 16)
                elif kind == "combine":
                    t = step[1]
                    sp.wait_ge(out_ready, t + 1)
                    sp.dma_start(d["out"][t * P:(t + 1) * P, :], outt[:, t, :]).then_inc(stored, 16)
            sp.wait_ge(stored, 16 * NT)

        @block.tensor
        def _(pe):
            def acquire(step):
                ring, slot, n, before = USE[step]
                for e in ("act", "dve"):
                    if before[e]:
                        pe.wait_ge(freed[ring, slot, e], before[e])
                return slot

            def mm(out, lhsT, rhs, start=True, stop=True):
                return nc.tensor.matmul(out, lhsT, rhs, start=start, stop=stop)

            def wrote(step, ins):
                ins.then_inc(written[USE[step][0]], 1)

            count = {}
            for step in ORDER:
                kind = step[0]
                i = count.get(kind, 0)
                count[kind] = i + 1
                if kind == "proj":
                    _, layer, b = step
                    g = 0 if layer == 0 else 2
                    pe.wait_ge(gated, NUMBER["gate", g, b] + 1)
                    if b == 0:
                        pe.wait_ge(loaded[f"att{layer}"], 16 * (7 if layer == 0 else 4))
                    slot = acquire(step)
                    y = G[g % 2]
                    for bank, w_ in ((0, wq), (1, wk)):
                        for co in range(CT):
                            for ci in range(CT):
                                mm(big(slot, bank)[:, co * T:(co + 1) * T], w_[:, ci, co * P:(co + 1) * P],
                                   y[:, ci, bt(b)], ci == 0, ci == CT - 1)
                    for t in range(QT):
                        for ci in range(CT):
                            tok = b * T + t * P
                            last = mm(big(slot, 2)[:, t * D:(t + 1) * D], y[:, ci, tok:tok + P], wv[:, ci, :],
                                      ci == 0, ci == CT - 1)
                    wrote(step, last)
                elif kind == "beta":
                    b = step[1]
                    slot = acquire(step)
                    for t in range(QT):
                        for ci in range(CT):
                            tok = b * T + t * P
                            last = mm(big(slot, 0)[:, t * H:(t + 1) * H], G[0][:, ci, tok:tok + P], wb[:, ci, :],
                                      ci == 0, ci == CT - 1)
                    wrote(step, last)
                elif kind in ("scores", "kscores"):
                    _, layer, b, j = step
                    par = b % 2
                    qn = "q" if kind == "scores" else "kq"
                    if j == 0:
                        pe.wait_ge(stacked[qn, par], stack_count(qn, layer, b))
                        pe.wait_ge(stacked["k", par], stack_count("k", layer, b))
                        if i == 0 and kind == "scores":
                            pe.wait_ge(consts_ready, 1)
                    slot = acquire(step)
                    q_, k_ = stack[qn, par], stack["k", par]
                    mask = maskb[:, QK if kind == "scores" else QK_STRICT, :]
                    for jj in range(GH):
                        h = j * GH + jj
                        out = wide(slot)[:, jj // 2, (jj % 2) * T:(jj % 2 + 1) * T]
                        mm(out, q_[0:SROWS, h, P:T], k_[0:SROWS, h, 0:T], True, False)
                        mm(out[:, P:T], identb, mask, False, True)
                    for jj in range(GH):
                        h = j * GH + jj
                        out = big(slot, 2)[:, jj * P:(jj + 1) * P]
                        mm(out, q_[0:SROWS, h, 0:P], k_[0:SROWS, h, 0:P], True, False)
                        last = mm(out, identb, mask, False, True)
                    wrote(step, last)
                elif kind in ("max", "kmax"):
                    n = rows_order.index(step)
                    pe.wait_ge(mparts_ready[kind], NUMBER[step] + 1)
                    slot = acquire(step)
                    out = single(slot)[:, 0:P // 2].bitcast(BF16)
                    wrote(step, nc.tensor.transpose(out[0:2 * QT * H, :], mparts[kind], identb))
                elif kind in ("probs", "kprobs"):
                    _, layer, b, j = step
                    par = b % 2
                    qn = "q" if kind == "probs" else "kq"
                    if j == 0:
                        pe.wait_ge(mrows[qn, par], row_count(qn, layer, b))
                        if b == 0:
                            pe.wait_ge(ones_ready, 2 * (layer + 1))
                    slot = acquire(step)
                    q_, k_ = stack[qn, par], stack["k", par]
                    mask = maskb[:, KQ if kind == "probs" else KQ_STRICT, :]
                    for jj in range(GH):
                        h = j * GH + jj
                        out = wide(slot)[:, jj // 2, (jj % 2) * T:(jj % 2 + 1) * T]
                        mm(out, k_[0:MROWS, h, 0:P], q_[0:MROWS, h, 0:T], True, False)
                        mm(out[:, 0:P], identb, mask, False, True)
                    for jj in range(GH):
                        h = j * GH + jj
                        out = big(slot, 2)[:, jj * P:(jj + 1) * P]
                        mm(out, k_[0:MROWS, h, P:T], q_[0:MROWS, h, P:T], True, False)
                        last = mm(out, identb, mask, False, True)
                    wrote(step, last)
                elif kind == "pv":
                    _, layer, b = step
                    wait_done(pe, ("probs", layer, b, NG - 1), "act")
                    if layer == 0:
                        wait_done(pe, ("proj", 0, b), "dve")
                        val = vflat[b % NV]
                    else:
                        for half in range(2):
                            wait_done(pe, ("solve", b, QT * NB - 1, half), "dve")
                        val = uflat
                    slot = acquire(step)
                    for h in range(H):
                        out = wide(slot).rearrange("p a (g t) -> p (a g) t", g=2)[(h % 4) * 32:(h % 4) * 32 + 32, h // 4, :]
                        mm(out, val[:, h * VW:h * VW + 32], prob[:, h, 0:T], True, False)
                        at = (H + h) * VW
                        last = mm(out[:, P:T], val[:, at:at + 32], prob[:, h, T:T + P], False, True)
                    wrote(step, last)
                elif kind == "otr":
                    _, layer, b = step
                    wait_done(pe, ("pv", layer, b), "act")
                    slot = acquire(step)
                    raw = oraw(layer, b)
                    for t in range(QT):
                        for g in range(4):
                            last = nc.tensor.transpose(wide(slot)[:, t, g * P:(g + 1) * P], raw[:, g, t * P:(t + 1) * P],
                                                       ident)
                    wrote(step, last)
                elif kind == "oT":
                    _, layer, b = step
                    wait_done(pe, ("otr", layer, b), "dve")
                    slot = acquire(step)
                    out = v3(big(slot, 0), CT)
                    for ct in range(CT):
                        for t in range(QT):
                            last = nc.tensor.transpose(out[:, ct, t * P:(t + 1) * P], otok[:, t, ct * P:(ct + 1) * P],
                                                       ident)
                    wrote(step, last)
                elif kind == "wo":
                    _, layer, b = step
                    wait_done(pe, ("oT", layer, b), "act")
                    slot = acquire(step)
                    out = v3(big(slot, 0), CT)
                    for co in range(CT):
                        for ci in range(CT):
                            last = mm(out[:, co, :], wo[:, ci, co * P:(co + 1) * P], oT[:, ci, :],
                                      ci == 0, ci == CT - 1)
                    wrote(step, last)
                elif kind == "fc1":
                    _, h, m = step
                    if i == 0:
                        pe.wait_ge(gated, NUMBER["gate", 1, B - 1] + 1)
                        pe.wait_ge(tern_ready, 2)
                    slot = acquire(step)
                    for ci in range(CT):
                        last = mm(big(slot, 0), w1[:, ci, m * P:(m + 1) * P], G[1][:, ci, h * 512:(h + 1) * 512],
                                  ci == 0, ci == CT - 1)
                    wrote(step, last)
                elif kind == "fc2":
                    _, h, c = step
                    for m in (MT - 2, MT - 1):
                        wait_done(pe, ("fc1", h, m), "act")
                    slot = acquire(step)
                    for m in range(MT):
                        last = mm(big(slot, 0), w2[:, m, c * P:(c + 1) * P], hid[:, m, h * 512:(h + 1) * 512],
                                  m == 0, m == MT - 1)
                    wrote(step, last)
                elif kind == "gather":
                    _, b, s, half = step
                    t, r = divmod(s, NB)
                    wait_done(pe, ("solve", b, s - 1, half), "dve")
                    slot = acquire(step)
                    kp = kprob[b % 2]
                    rows = slice(r * BLK, (r + 1) * BLK)
                    for h in range(half * H // 2, (half + 1) * H // 2):
                        out = single(slot)[rows, h * HD:(h + 1) * HD]
                        if t == 0:
                            last = mm(out, kp[0:r * BLK, h, rows], uaug[0:r * BLK, 0, h, 0:HD])
                        else:
                            last = mm(out, kp[:, h, P + r * BLK:P + (r + 1) * BLK], uaug[:, 0, h, 0:HD], True, r == 0)
                            if r:
                                last = mm(out, kp[0:r * BLK, h, T + r * BLK:T + (r + 1) * BLK],
                                          uaug[0:r * BLK, 1, h, 0:HD], False, True)
                    wrote(step, last)
                elif kind == "solve":
                    _, b, s, half = step
                    t, r = divmod(s, NB)
                    if s == 0:
                        pe.wait_ge(invT_ready, b + 1)
                        wait_done(pe, ("kprobs", 1, b, NG - 1), "act")
                    pe.wait_ge(z_ready, 2 * (QT * NB * b + s) + half + 1)
                    slot = acquire(step)
                    rows = slice(r * BLK, (r + 1) * BLK)
                    for h in range(half * H // 2, (half + 1) * H // 2):
                        n = t * H + h
                        last = mm(single(slot)[rows, h * HD:(h + 1) * HD], invT[b % 2][rows, n * BLK:(n + 1) * BLK],
                                  zz[rows, h * HD:(h + 1) * HD])
                    wrote(step, last)
                elif kind == "route":
                    pe.wait_ge(gated, NUMBER["gate", 3, B - 1] + 1)
                    slot = acquire(step)
                    wg = wb[:, :, 0:E]
                    pe.wait_ge(loaded["att1"], 16 * 5)
                    for t in range(NT):
                        for ci in range(CT):
                            last = mm(single(slot)[:, t * E:(t + 1) * E], G[1][:, ci, t * P:(t + 1) * P], wg[:, ci, :],
                                      ci == 0, ci == CT - 1)
                    wrote(step, last)
                elif kind in ("ytok", "xtok"):
                    n = step[1]
                    slot = acquire(step)
                    src = G[1] if kind == "ytok" else xT
                    out = big(slot, 0).rearrange("p (t c) -> p t c", t=2)
                    for t in range(2):
                        for ct in range(CT):
                            tok = (2 * n + t) * P
                            last = nc.tensor.transpose(out[:, t, ct * P:(ct + 1) * P], src[:, ct, tok:tok + P], ident)
                    wrote(step, last)
                elif kind == "rank":
                    s = step[1]
                    pe.wait_ge(choice_ready, s + 1)
                    slot = acquire(step)
                    out = single(slot)[:, 0:NT * E]
                    mm(out, tri, R["oh"][s], True, False)
                    last = mm(out, ones, R["pre"][s], False, True)
                    wrote(step, last)
                elif kind == "dispT":
                    e = step[1]
                    pe.wait_ge(dtok_loaded[e % 2], 16 * (e // 2 + 1))
                    slot = acquire(step)
                    out = v3(single(slot), CT)
                    for ct in range(CT):
                        for s in range(2):
                            last = nc.tensor.transpose(out[:, ct, s * P:(s + 1) * P], dtok[e % 2][:, s, ct * P:(ct + 1) * P],
                                                       ident)
                    wrote(step, last)
                elif kind == "up":
                    _, e, half = step
                    if half == 0:
                        wait_done(pe, ("dispT", e), "dve")
                        pe.wait_ge(w_second[0], e + 1)
                    slot = acquire(step)
                    out = wide(slot).rearrange("p a (m t) -> p (a m) t", m=2)
                    parts = w_parts[0][e % 2]
                    for mm_ in range(MT // 2):
                        m = half * (MT // 2) + mm_
                        for n, (ci, i, j) in enumerate(((ci, i, j) for ci in range(CT) for i, j in PRODUCTS)):
                            last = mm(out[:, mm_, :], parts[i][:, ci, m * P:(m + 1) * P], d_parts[e % 2][j][:, ci, :],
                                      n == 0, n == CT * len(PRODUCTS) - 1)
                    wrote(step, last)
                elif kind == "down":
                    e = step[1]
                    pe.wait_ge(w_second[1], e + 1)
                    wait_done(pe, ("up", e, 0), "dve")
                    slot = acquire(step)
                    out = v3(single(slot), 2)
                    parts = w_parts[1][e % 2]
                    for s in range(2):
                        for n, (m, i, j) in enumerate(((m, i, j) for m in range(MT) for i, j in PRODUCTS)):
                            if s == 0 and n == MT // 2 * len(PRODUCTS):
                                wait_done(pe, ("up", e, 1), "dve")
                            last = mm(out[:, s, :], h_parts[e % 2][j][:, m, s * P:(s + 1) * P], parts[i][:, m, :],
                                      n == 0, n == MT * len(PRODUCTS) - 1)
                    wrote(step, last)

        @block.scalar
        def _(act):
            own = [0]

            def step_(ins):
                own[0] += 1
                ins.then_inc(act_own, 1)

            def settle():
                act.wait_ge(act_own, own[0])

            def filled(step):
                ring, slot, n, before = USE[step]
                act.wait_ge(written[ring], n + 1)
                return slot

            def give_back(step, ins):
                ring, slot, n, before = USE[step]
                ins.then_inc(freed[ring, slot, "act"], 1)

            A = nc.scalar.activation
            act.wait_ge(exps_ready, 1)
            A(tf[:, B:2 * B], tf[:, 0:B], ACT.Exp, scale=-1.0).then_inc(ek_ready, 1)
            act.wait_ge(loaded["const"], 32)
            A(small[:, 0:4 * CT], col["w"], ACT.Exp).then_inc(ek_ready, 1)
            act.wait_ge(exps_ready, 2)
            A(ek, ekv, ACT.Exp).then_inc(ek_ready, 1)
            act.wait_ge(exps_ready, 3)
            A(dec, dec, ACT.Exp).then_inc(ek_ready, 1)

            for step in ORDER:
                kind = step[0]
                if kind == "wkv":
                    _, c, b = step
                    n = NUMBER[step]
                    if n == 0:
                        act.wait_ge(loaded["fs"], 16)
                    if n >= 2:
                        act.wait_ge(euk_used, n - 1)
                    for ct in range(CT):
                        A(euks[n % 2][:, ct, :], fsT[:, ct, bt(b)], ACT.Exp, bias=col["u"][:, c * CT + ct:c * CT + ct + 1]
                          ).then_inc(euk_ready, 1)
                elif kind == "gate":
                    _, g, b = step
                    n = NUMBER[step]
                    if n == 0:
                        act.wait_ge(loaded["x"], 16)
                    if g:
                        act.wait_ge(x_ready, x_count(g, b))
                    if n:
                        act.wait_ge(gated, n)
                    A(th, xT[:, :, bt(b)], ACT.Tanh, scale=0.5).then_inc(tanh_ready, 1)
                elif kind == "proj":
                    _, layer, b = step
                    n = NUMBER[step]
                    slot = filled(step)
                    if layer == 0:
                        if n:
                            act.wait_ge(parts_ready, n)
                            act.wait_ge(parts_used, 32 * n)
                        for o, bias in ((0, col["bq"]), (1, col["bk"])):
                            for ct in range(CT):
                                cs = slice(ct * T, (ct + 1) * T)
                                src = big(slot, o)[:, cs]
                                step_(A(part[:, o, 0, cs], src, ACT.Identity, bias=bias[:, ct:ct + 1]))
                                ins = A(qf[:, o, cs], src, ACT.Identity, bias=bias[:, ct:ct + 1])
                                if o == 1 and ct == CT - 1:
                                    give_back(step, ins)
                                else:
                                    step_(ins)
                    else:
                        if b >= NV:
                            act.wait_ge(z_ready, 2 * QT * NB * (b - NV + 1))
                        else:
                            act.wait_ge(written["big"], USE["pv", 0, B - 1][2] + 1)
                        give_back(step, A(vaug[b % NV][:, :, :, 0:HD],
                                          big(slot, 2).rearrange("p (t h e) -> p t h e", t=QT, h=H), ACT.Copy))
                elif kind in ("max", "kmax"):
                    n = rows_order.index(step)
                    slot = filled(step)
                    if n >= 2:
                        prev = rows_order[n - 2]
                        nm = "q" if prev[0] == "max" else "kq"
                        act.wait_ge(mrows[nm, prev[2] % 2], row_count(nm, prev[1], prev[2]))
                    out = single(slot)[:, 0:P // 2].bitcast(BF16)
                    give_back(step, A(mT[n % 2][0:2 * QT * H, :], out[0:2 * QT * H, :], ACT.Copy))
                elif kind in ("probs", "kprobs"):
                    _, layer, b, j = step
                    slot = filled(step)
                    n = NUMBER[step]
                    if kind == "probs":
                        dst = prob
                        if b or layer:
                            pl, pb = (layer, b - 1) if b else (0, B - 1)
                            act.wait_ge(written["big"], USE["pv", pl, pb][2] + 1)
                    else:
                        dst = kprob[b % 2]
                        if b >= 2:
                            act.wait_ge(written["small"], USE["gather", b - 2, QT * NB - 1, 1][2] + 1)
                        elif b == 0 and j == 0:
                            act.wait_ge(gate_ready, NUMBER["weigh", 3, B - 1] + 1)
                            act.wait_ge(written["big"], USE["fc2", 1, CT - 1][2] + 1)
                    hs = slice(j * GH, (j + 1) * GH)
                    scale = 1.0 if layer else SCORE_SCALE
                    step_(A(dst[:, hs, 0:T], wide(slot).rearrange("p a (h t) -> p (a h) t", h=2), ACT.Exp, scale=scale))
                    give_back(step, A(dst[:, hs, T:T + P], big(slot, 2).rearrange("p (h t) -> p h t", h=GH), ACT.Exp,
                                      scale=scale))
                elif kind == "kscores":
                    _, layer, b, j = step
                    slot = filled(step)
                    if j == 0 and b >= 3:
                        act.wait_ge(z_ready, 2 * QT * NB * (b - 2))
                    for t in (1, 0):
                        act.wait_ge(nbias_ready, 2 * NUMBER[step] + 2 - t)
                        for jj in range(GH):
                            if t == 0:
                                s_ = big(slot, 2)[:, jj * P:(jj + 1) * P]
                            else:
                                s_ = wide(slot)[:, jj // 2, (jj % 2) * T:(jj % 2 + 1) * T]
                            n = t * H + j * GH + jj
                            ins = A(s_, s_, ACT.Exp, bias=nbias[:, n:n + 1], accum_out=cc[b % 3][:, n:n + 1])
                    give_back(step, ins)
                elif kind == "pv":
                    _, layer, b = step
                    slot = filled(step)
                    n = NUMBER[step]
                    if layer == 0:
                        if b:
                            act.wait_ge(written["big"], USE["otr", 0, b - 1][2] + 1)
                        else:
                            act.wait_ge(disp_zero, 16)
                    else:
                        act.wait_ge(written["small"], USE["solve", b, QT * NB - 1, 1][2] + 1)
                        act.wait_ge(invT_ready, b + 1)
                    give_back(step, A(oraw(layer, b), wide(slot).rearrange("p a (g t) -> p (a g) t", g=2), ACT.Copy))
                elif kind == "oT":
                    slot = filled(step)
                    n = NUMBER[step]
                    if n:
                        prev = [s for s in ORDER if s[0] == "wo"][n - 1]
                        act.wait_ge(written["big"], USE[prev][2] + 1)
                    give_back(step, A(oT, v3(big(slot, 0), CT), ACT.Copy))
                elif kind == "ternary":
                    i = step[1]
                    w_ = (w1, w2)[i]
                    act.wait_ge(tern_cnt, i + 1)
                    A(tern_tmp(i), w_, ACT.Square, accum_out=small[:, 43 + 2 * i:44 + 2 * i]).then_inc(tern_abs, 1)
                elif kind == "fc1":
                    _, h, m = step
                    slot = filled(step)
                    if NUMBER[step] == 0:
                        act.wait_ge(tern_ready, 2)
                        act.wait_ge(written["big"], USE["probs", 0, B - 1, NG - 1][2] + 1)
                    give_back(step, A(hid[:, m, h * 512:(h + 1) * 512], big(slot, 0), ACT.Gelu,
                                      bias=col["b1"][:, m:m + 1], scale=small[:, 56:57]))
                elif kind == "fc2":
                    _, h, c = step
                    slot = filled(step)
                    give_back(step, A(ffn[:, c, h * 512:(h + 1) * 512], big(slot, 0), ACT.Identity,
                                      bias=col["b2"][:, c:c + 1], scale=small[:, 57:58]))
                elif kind == "route":
                    act.wait_ge(logits_exp_in, 1)
                    A(R["exp"], R["logit"], ACT.Exp).then_inc(logits_exp, 1)
                elif kind == "ytok":
                    n = step[1]
                    slot = filled(step)
                    give_back(step, A(ytok[:, 2 * n:2 * n + 2, :], v3(big(slot, 0), 2), ACT.Copy))
                elif kind == "up":
                    _, e, half = step
                    slot = filled(step)
                    out = wide(slot).rearrange("p a (m t) -> p (a m) t", m=2)
                    for mm_ in range(MT // 2):
                        m = half * (MT // 2) + mm_
                        ins = A(out[:, mm_, :], out[:, mm_, :], ACT.Gelu,
                                bias=col["fb1"][:, e * MT + m:e * MT + m + 1])
                        if mm_ < MT // 2 - 1:
                            step_(ins)
                        else:
                            ins.then_inc(h_whole, 1)
                elif kind == "wsplit":
                    _, e, i = step
                    act.wait_ge(w_loaded[e % NW], 32 * (e // NW + 1))
                    if e >= 2:
                        use = USE[("up", e - 2, 1) if i == 0 else ("down", e - 2)]
                        act.wait_ge(written[use[0]], use[2] + 1)
                    A(w_parts[i][e % 2][0][:], fcw[e % NW][i], ACT.Copy).then_inc(w_first, 1)

        @block.vector
        def _(dve):
            V = nc.vector
            own = [0]

            def st(ins):
                own[0] += 1
                ins.then_inc(dve_own, 1)

            def settle():
                dve.wait_ge(dve_own, own[0])

            def link(ins):
                st(ins)
                settle()

            def filled(step):
                ring, slot, n, before = USE[step]
                dve.wait_ge(written[ring], n + 1)
                return slot

            def give_back(step, ins):
                ring, slot, n, before = USE[step]
                ins.then_inc(freed[ring, slot, "dve"], 1)

            def after_give_back(step):
                ring, slot, n, before = USE[step]
                dve.wait_ge(freed[ring, slot, "dve"], before["dve"] + 1)

            def r3(name, s=None):
                return v3(R[name] if s is None else R[name][s], NT)

            def e8(ap):
                return ap.unsqueeze(2).to_broadcast([P, NT, E])

            dve.wait_ge(loaded["cond"], 16)
            V.tensor_reduce(tf[:, 0:B], cond, axis=AX.X, op=ALU.add).then_inc(exps_ready, 1)
            dve.wait_ge(loaded["fs"], 16)
            V.tensor_scalar_min(ekv, fsT, 30.0).then_inc(exps_ready, 1)
            dve.wait_ge(loaded["const"], 32)
            st(V.tensor_copy(identb, ident))
            st(V.tensor_copy(maskb, v3(c_["masks"], 4)))
            for flat in vflat + [uflat]:
                st(V.memset(flat, 1.0))
            dve.wait_ge(ek_ready, 2)
            link(V.tensor_scalar_add(tf[:, 0:B], tf[:, B:2 * B], 1.0))
            link(V.reciprocal(tf[:, B:2 * B], tf[:, 0:B]))
            st(V.tensor_scalar(tf[:, 2 * B:3 * B], tf[:, B:2 * B], 0.5, 0.5, ALU.mult, ALU.add))
            st(V.tensor_scalar(tf[:, 3 * B:4 * B], tf[:, B:2 * B], 0.1, 0.4, ALU.mult, ALU.add))
            dec3 = dec.rearrange("p (c b) -> p c b", b=B)
            V.tensor_scalar(dec3, small[:, 0:4 * CT].unsqueeze(2).to_broadcast([P, 4 * CT, B]), -1.0, None, ALU.mult
                            ).then_inc(exps_ready, 1)
            dve.wait_ge(ek_ready, 4)
            settle()
            link(V.tensor_tensor(dec3, dec3, tf[:, 2 * B:3 * B].unsqueeze(1).to_broadcast([P, 4 * CT, B]), ALU.mult))
            V.tensor_tensor(ekv, ek, fsT, ALU.mult).then_inc(consts_ready, 1)
            dve.wait_ge(consts_ready, 1)

            for step in DVE_ORDER:
                kind = step[0]
                if kind == "wkv":
                    _, c, b = step
                    n = NUMBER[step]
                    scan, euk, gk = scans[n % 2], euks[n % 2], gks[n % 2]
                    for ct in range(CT):
                        i = c * CT + ct
                        dd = dec[:, i * B + b:i * B + b + 1].to_broadcast([P, T])
                        for s, src in ((0, ekv), (2, ek)):
                            x_ = src[:, ct, bt(b)]
                            V.tensor_tensor_scan(scan[s][:, ct, :], dd, x_, 0.0, ALU.mult, ALU.add)
                            ins = V.tensor_tensor_scan(scan[s + 1][:, ct, ::-1], dd, x_[:, ::-1], 0.0, ALU.mult, ALU.add)
                    ins.then_inc(scanned, 1)
                    dve.wait_ge(euk_ready, CT * (n + 1))
                    V.scalar_tensor_tensor(out=gk, in0=euk, scalar=EXP30, in1=ek[:, :, bt(b)], op0=ALU.min,
                                           op1=ALU.subtract).then_inc(euk_used, 1)
                elif kind == "weigh":
                    _, c, b = step
                    n = NUMBER[step]
                    scan = scans[n % 2]
                    if c == 2:
                        dve.wait_ge(written["big"], USE["proj", 0, b][2] + 1)
                    elif c == 3:
                        dve.wait_ge(written["big"], USE["fc1", 1, MT - 1][2] + 1)
                    dve.wait_ge(summed, n + 1)
                    link(V.tensor_scalar_max(scan[2], scan[2], 1e-8))
                    link(V.reciprocal(scan[3], scan[2]))
                    V.scalar_tensor_tensor(out=G[c % 2][:, :, bt(b)], in0=scan[0], scalar=tf[:, 3 * B + b:3 * B + b + 1],
                                           in1=scan[3], op0=ALU.mult, op1=ALU.mult).then_inc(gate_ready, 1)
                    dve.wait_ge(gate_ready, n + 1)
                elif kind == "gate":
                    _, g, b = step
                    n = NUMBER[step]
                    dve.wait_ge(tanh_ready, n + 1)
                    y = G[g % 2][:, :, bt(b)]
                    V.scalar_tensor_tensor(out=y, in0=th, scalar=1.0, in1=y, op0=ALU.add, op1=ALU.mult
                                           ).then_inc(gated, 1)
                    dve.wait_ge(gated, n + 1)
                elif kind == "proj":
                    _, layer, b = step
                    n = NUMBER[step]
                    slot = filled(step)
                    if layer == 0:
                        if b >= NV:
                            dve.wait_ge(written["big"], USE["pv", 0, b - NV][2] + 1)
                        give_back(step, V.tensor_tensor(
                            vaug[b % NV][:, :, :, 0:HD], big(slot, 2).rearrange("p (t h e) -> p t h e", t=QT, h=H),
                            v3(bvb, H).unsqueeze(1).to_broadcast([P, QT, H, HD]), ALU.add))
                    else:
                        if n:
                            dve.wait_ge(parts_used, 32 * n)
                        src = wide(slot).rearrange("p o (c t) -> p (o c) t", c=CT)
                        q4 = qf.rearrange("p o (c t) -> p (o c) t", c=CT)
                        st(V.tensor_tensor(q4, src, c_["cos"].unsqueeze(1).to_broadcast([P, 2 * CT, T]), ALU.mult))
                        settle()
                        st(V.tensor_tensor(wide(slot), wide(slot), c_["sin"].unsqueeze(1).to_broadcast([P, 2, CT * T]),
                                           ALU.mult))
                        settle()
                        give_back(step, V.tensor_tensor(
                            qf.rearrange("p o (c t) -> p o c t", c=CT), qf.rearrange("p o (c t) -> p o c t", c=CT),
                            wide(slot).rearrange("p o (c t) -> p o c t", c=CT)[:, :, ::-1, :], ALU.add))
                        after_give_back(step)
                elif kind == "split":
                    _, layer, b = step
                    n = NUMBER[step]
                    if layer:
                        link(V.tensor_copy(part[:, :, 0], qf))
                    else:
                        ring, sl, nn, before = USE["proj", layer, b]
                        dve.wait_ge(freed[ring, sl, "act"], before["act"] + 1)
                    link(V.tensor_tensor(qf, qf, part[:, :, 0], ALU.subtract))
                    link(V.tensor_copy(part[:, :, 1], qf))
                    V.tensor_tensor(part[:, :, 2], qf, part[:, :, 1], ALU.subtract).then_inc(parts_ready, 1)
                    dve.wait_ge(parts_ready, n + 1)
                elif kind == "kscores":
                    _, layer, b, j = step
                    slot = filled(step)
                    hs = slice(j * GH, (j + 1) * GH)
                    mneg, mpart = mnegs["kmax"], mparts["kmax"]
                    for t in (1, 0):
                        mn, nb = v3(mneg, QT)[:, t, hs], v3(nbias, QT)[:, t, hs]
                        hi, lo = (mpart[:, i * QT * H:(i + 1) * QT * H].rearrange("p (h t) -> p t h", t=QT)[:, t, hs]
                                  for i in range(2))
                        src = (wide(slot).rearrange("p a (h t) -> p (a h) t", h=2) if t else
                               big(slot, 2).rearrange("p (h t) -> p h t", h=GH))
                        link(V.tensor_reduce(mn, src, axis=AX.X, op=ALU.max, negate=True))
                        if j == 0 and b and t:
                            dve.wait_ge(written["small"], USE["kmax", 1, b - 1][2] + 1)
                            wait_done(dve, ("kscores", layer, b - 1, NG - 1), "act")
                        link(V.tensor_scalar_min(hi, mn, NO_KEY))
                        link(V.scalar_tensor_tensor(out=lo, in0=mn, scalar=NO_KEY, in1=hi, op0=ALU.min,
                                                    op1=ALU.subtract))
                        V.tensor_tensor(nb, hi, lo, ALU.add).then_inc(nbias_ready, 1)
                    if j == NG - 1:
                        dve.wait_ge(nbias_ready, 2 * (NUMBER[step] + 1))
                        V.nop().then_inc(mparts_ready["kmax"], 1)
                elif kind == "scores":
                    _, layer, b, j = step
                    slot = filled(step)
                    mneg = mnegs["max"]
                    hs = slice(j * GH, (j + 1) * GH)
                    st(V.tensor_reduce(mneg[:, H + j * GH:H + (j + 1) * GH],
                                       wide(slot).rearrange("p a (h t) -> p (a h) t", h=2), axis=AX.X, op=ALU.max,
                                       negate=True))
                    give_back(step, V.tensor_reduce(mneg[:, j * GH:(j + 1) * GH],
                                                    big(slot, 2).rearrange("p (h t) -> p h t", h=GH), axis=AX.X,
                                                    op=ALU.max, negate=True))
                elif kind == "minus":
                    _, layer, b = step
                    n = NUMBER[step]
                    mneg, mpart = mnegs["max"], mparts["max"]
                    after_give_back(("scores", layer, b, NG - 1))
                    settle()
                    link(V.tensor_scalar_min(mneg, mneg, NO_KEY))
                    if n:
                        dve.wait_ge(written["small"], USE[[s for s in ORDER if s[0] == "max"][n - 1]][2] + 1)
                    hi, lo = (mpart[:, i * QT * H:(i + 1) * QT * H].rearrange("p (h t) -> p t h", t=QT)
                              for i in range(2))
                    link(V.tensor_copy(hi, v3(mneg, QT)))
                    V.tensor_tensor(lo, v3(mneg, QT), hi, ALU.subtract).then_inc(mparts_ready["max"], 1)
                elif kind == "otr":
                    _, layer, b = step
                    n = NUMBER[step]
                    slot = filled(step)
                    o_ = wide(slot).rearrange("p t (h e) -> p t h e", h=H)
                    if n:
                        prev = [s for s in ORDER if s[0] == "oT"][n - 1]
                        dve.wait_ge(written["big"], USE[prev][2] + 1)
                    r_ = v3(rec, QT)
                    link(V.reciprocal(r_, o_[:, :, :, HD]))
                    give_back(step, V.tensor_tensor(otok.rearrange("p t (h e) -> p t h e", h=H), o_[:, :, :, 0:HD],
                                                    r_.unsqueeze(3).to_broadcast([P, QT, H, HD]), ALU.mult))
                elif kind == "wo":
                    _, layer, b = step
                    slot = filled(step)
                    y = xT[:, :, bt(b)]
                    src = v3(big(slot, 0), CT)
                    if layer == 0:
                        for ct in range(CT):
                            ins = V.scalar_tensor_tensor(out=y[:, ct, :], in0=src[:, ct, :],
                                                         scalar=col["bo"][:, ct:ct + 1], in1=y[:, ct, :], op0=ALU.add,
                                                         op1=ALU.add)
                            if ct < CT - 1:
                                st(ins)
                            else:
                                give_back(step, ins)
                    else:
                        give_back(step, V.tensor_tensor(y, src, y, ALU.add))
                    after_give_back(step)
                    V.nop().then_inc(x_ready, 1)
                elif kind == "largest":
                    i = step[1]
                    if i == 0:
                        dve.wait_ge(loaded["tern"], 32)
                    V.tensor_reduce(small[:, 32 + i:33 + i], (w1, w2)[i], axis=AX.XY, op=ALU.max,
                                    apply_absolute_value=True).then_inc(tern_in, 1)
                elif kind == "ternary":
                    i = step[1]
                    w_ = (w1, w2)[i]
                    s_ = small
                    dve.wait_ge(tern_max, i + 1)
                    st(V.tensor_scalar(s_[:, 36:37], s_[:, 34 + i:35 + i], THRESHOLD, None, ALU.mult))
                    link(V.tensor_scalar(s_[:, 37:38], s_[:, 34 + i:35 + i], -THRESHOLD, None, ALU.mult))
                    tmp = tern_tmp(i)
                    if i:
                        dve.wait_ge(tern_abs, i)
                    link(V.tensor_scalar(tmp, w_, s_[:, 36:37], None, ALU.is_gt))
                    link(V.scalar_tensor_tensor(out=tmp, in0=w_, scalar=s_[:, 37:38], in1=tmp, op0=ALU.is_lt,
                                                op1=ALU.subtract))
                    link(V.scalar_tensor_tensor(out=w_, in0=w_, scalar=1.0, in1=tmp, op0=ALU.mult, op1=ALU.mult,
                                                accum_out=s_[:, 42 + 2 * i:43 + 2 * i]))
                    V.tensor_copy(w_, tmp).then_inc(tern_cnt, 1)
                elif kind == "alpha":
                    i = step[1]
                    s_ = small
                    dve.wait_ge(tern_sum, i + 1)
                    link(V.tensor_scalar_max(s_[:, 48:49], s_[:, 47 + 4 * i:48 + 4 * i], 1.0))
                    link(V.reciprocal(s_[:, 49:50], s_[:, 48:49]))
                    V.tensor_tensor(s_[:, 56 + i:57 + i], s_[:, 46 + 4 * i:47 + 4 * i], s_[:, 49:50], ALU.mult
                                    ).then_inc(tern_ready, 1)
                    dve.wait_ge(tern_ready, i + 1)
                elif kind == "fc2":
                    _, h, c = step
                    n = NUMBER[step]
                    wait_done(dve, step, "act")
                    st(V.tensor_reduce(small[:, 60 + n:61 + n], ffn[:, c, h * 512:(h + 1) * 512], axis=AX.X,
                                       op=ALU.max, apply_absolute_value=True))
                elif kind == "quant":
                    settle()
                    V.tensor_reduce(small[:, 64:65], small[:, 60:64], axis=AX.X, op=ALU.max).then_inc(amax_in, 1)
                    dve.wait_ge(amax_out, 1)
                    link(V.tensor_scalar(small[:, 66:67], small[:, 65:66], 1.0 / QMAX, 1e-8, ALU.mult, ALU.add))
                    link(V.reciprocal(small[:, 67:68], small[:, 66:67]))
                elif kind == "requant":
                    b = step[1]
                    f = ffn[:, :, bt(b)]
                    link(V.tensor_scalar(f, f, small[:, 67:68], ROUND, ALU.mult, ALU.add))
                    link(V.tensor_scalar(f, f, -ROUND, QMAX, ALU.add, ALU.min))
                    link(V.tensor_scalar(f, f, -QMAX, small[:, 66:67], ALU.max, ALU.mult))
                    y = xT[:, :, bt(b)]
                    V.tensor_tensor(y, y, f, ALU.add).then_inc(x_ready, 1)
                elif kind == "beta":
                    b = step[1]
                    slot = filled(step)
                    give_back(step, V.tensor_tensor(v3(beta[b % 2], QT), v3(big(slot, 0)[:, 0:QT * H], QT),
                                                    bbb.unsqueeze(1).to_broadcast([P, QT, H]), ALU.add))
                    after_give_back(step)
                elif kind == "den":
                    b = step[1]
                    ring, sl, nn, before = USE["kscores", 1, b, NG - 1]
                    dve.wait_ge(freed[ring, sl, "act"], before["act"] + 1)
                    link(V.tensor_scalar_max(cc[b % 3], cc[b % 3], 1e-20))
                    link(V.reciprocal(cc[b % 3], cc[b % 3]))
                    link(V.tensor_tensor(cc[b % 3], cc[b % 3], beta[b % 2], ALU.mult))
                elif kind == "blocks":
                    b = step[1]
                    if b:
                        dve.wait_ge(inv_ready, b)
                    if b >= 2:
                        dve.wait_ge(written["big"], USE["otr", 1, b - 2][2] + 1)
                    blk_src = invT[b % 2]
                    ring, sl, nn, before = USE["kprobs", 1, b, NG - 1]
                    dve.wait_ge(freed[ring, sl, "act"], before["act"] + 1)
                    st(V.transpose(cT, cc[b % 3]))
                    kp = kprob[b % 2]
                    for r in range(NB):
                        rows = slice(r * BLK, (r + 1) * BLK)
                        for t in range(QT):
                            at = t * T + r * BLK
                            st(V.tensor_copy(v3(blk_src[rows, t * H * BLK:(t + 1) * H * BLK], H),
                                             kp[rows, :, at:at + BLK]))
                    settle()
                    V.transpose(blkA.rearrange("p (i j) -> p i j", i=BLK),
                                blk_src.rearrange("p (n i) -> p i n", i=BLK)).then_inc(blocks_ready, 1)
                    dve.wait_ge(blocks_ready, b + 1)
                elif kind == "inverse":
                    b = step[1]
                    dve.wait_ge(inv_ready, b + 1)
                    V.transpose(invT[b % 2].rearrange("p (n i) -> p i n", i=BLK),
                                blkX.rearrange("p (i j) -> p i j", i=BLK)).then_inc(invT_ready, 1)
                    dve.wait_ge(invT_ready, b + 1)
                    ring, sl, nn, before = USE["proj", 1, b]
                    dve.wait_ge(freed[ring, sl, "act"], before["act"] + 1)
                    rows = slice(0, BLK)
                    for hs in HALVES:
                        V.tensor_copy(v3(zz[rows, :], H)[:, hs], vaug[b % NV][rows, 0, hs, 0:HD]).then_inc(z_ready, 1)
                elif kind == "gather":
                    _, b, s, half = step
                    t, r = divmod(s, NB)
                    rows, hs = slice(r * BLK, (r + 1) * BLK), HALVES[half]
                    slot = filled(step)
                    cb = cc[b % 3][rows, t * H:(t + 1) * H][:, hs].unsqueeze(2).to_broadcast([BLK, H // 2, HD])
                    zt3, zz3 = v3(zt[rows, :], H)[:, hs], v3(zz[rows, :], H)[:, hs]
                    give_back(step, V.tensor_tensor(zt3, v3(single(slot)[rows, 0:H * HD], H)[:, hs], cb, ALU.mult))
                    after_give_back(step)
                    V.tensor_tensor(zz3, vaug[b % NV][rows, t, hs, 0:HD], zt3, ALU.subtract).then_inc(z_ready, 1)
                elif kind == "solve":
                    _, b, s, half = step
                    t, r = divmod(s, NB)
                    rows, hs = slice(r * BLK, (r + 1) * BLK), HALVES[half]
                    slot = filled(step)
                    if s == 0 and b:
                        dve.wait_ge(written["big"], USE["pv", 1, b - 1][2] + 1)
                    give_back(step, V.tensor_copy(uaug[rows, t, hs, 0:HD],
                                                  v3(single(slot)[rows, 0:H * HD], H)[:, hs]))
                elif kind == "route":
                    slot = filled(step)
                    lg = v3(single(slot)[:, 0:NT * E], NT)
                    link(V.reduce_max(R["mx"], lg, AX.X))
                    give_back(step, V.tensor_tensor(r3("logit"), lg, e8(R["mx"]), ALU.subtract))
                    after_give_back(step)
                    V.nop().then_inc(logits_exp_in, 1)
                    dve.wait_ge(logits_exp, 1)
                    link(V.reduce_sum(R["sum"], r3("exp"), AX.X))
                    link(V.reciprocal(R["rec"], R["sum"]))
                    link(V.tensor_tensor(r3("score"), r3("exp"), e8(R["rec"]), ALU.mult))
                elif kind == "choice":
                    s = step[1]
                    revb = c_["rev"].unsqueeze(1).to_broadcast([P, NT, E])
                    cur = r3("score" if s == 0 else "score2")
                    oh, pre = r3("oh", s), r3("pre", s)
                    if s == 0:
                        link(V.memset(pre[:, 0], 0.0))
                    else:
                        link(V.scalar_tensor_tensor(out=cur, in0=r3("oh", 0), scalar=-2.0, in1=r3("score"),
                                                    op0=ALU.mult, op1=ALU.add))
                    link(V.reduce_max(R["m"][s], cur, AX.X))
                    link(V.tensor_tensor(r3("t1"), cur, e8(R["m"][s]), ALU.is_equal))
                    link(V.tensor_tensor(r3("t1"), r3("t1"), revb, ALU.mult))
                    link(V.reduce_max(R["key"][s], r3("t1"), AX.X))
                    link(V.tensor_tensor(oh, revb, e8(R["key"][s]), ALU.is_equal))
                    for t in range(1, NT):
                        link(V.tensor_tensor(pre[:, t], pre[:, t - 1], oh[:, t - 1], ALU.add))
                    V.nop().then_inc(choice_ready, 1)
                    if s == 0:
                        st(V.tensor_tensor(r3("pre", 1)[:, 0], pre[:, NT - 1], oh[:, NT - 1], ALU.add))
                elif kind == "rank":
                    s = step[1]
                    slot = filled(step)
                    pos, key, tmp = R["pos"][s], R["key"][s], R["tmp"][s]
                    tr = c_["trash"][:, s * NT:(s + 1) * NT]
                    give_back(step, V.tensor_tensor(R["t1"], single(slot)[:, 0:NT * E], R["oh"][s], ALU.mult))
                    after_give_back(step)
                    st(V.tensor_scalar(R["base"][s], key, -float(CAP), float(E * CAP - 1), ALU.mult, ALU.add))
                    link(V.reduce_sum(pos, r3("t1"), AX.X))
                    st(V.tensor_scalar(R["valid"][s], pos, float(CAP), None, ALU.is_le))
                    link(V.tensor_tensor(R["slot"][s], R["base"][s], pos, ALU.add))
                    link(V.tensor_tensor(tmp, R["slot"][s], tr, ALU.subtract))
                    link(V.tensor_tensor(tmp, tmp, R["valid"][s], ALU.mult))
                    link(V.tensor_tensor(tmp, tmp, tr, ALU.add))
                    V.tensor_copy(idx_s[s], tmp).then_inc(rt_ready, 1)
                    if s == 1:
                        dve.wait_ge(rt_ready, 2)
                        link(V.tensor_tensor(R["tmp"][0], R["m"][0], R["m"][1], ALU.add))
                        link(V.tensor_scalar_max(R["tmp"][0], R["tmp"][0], 1e-9))
                        link(V.reciprocal(R["tmp"][1], R["tmp"][0]))
                        for i in range(2):
                            link(V.tensor_tensor(R["gate"][i], R["m"][i], R["tmp"][1], ALU.mult))
                            st(V.tensor_tensor(R["gate"][i], R["gate"][i], R["valid"][i], ALU.mult))
                            link(V.tensor_tensor(R["slot"][i], R["slot"][i], R["valid"][i], ALU.mult))
                            V.tensor_copy(idx_g[i], R["slot"][i]).then_inc(gather_ready, 1)
                        settle()
                elif kind == "xtok":
                    n = step[1]
                    slot = filled(step)
                    give_back(step, V.tensor_copy(xtok[:, 2 * n:2 * n + 2, :], v3(big(slot, 0), 2)))
                    after_give_back(step)
                elif kind == "dispT":
                    e = step[1]
                    slot = filled(step)
                    if e >= 2:
                        dve.wait_ge(written["big"], USE["up", e - 2, 1][2] + 1)
                    first, second = d_parts[e % 2]
                    link(V.tensor_copy(first[:], v3(single(slot), CT)))
                    give_back(step, V.tensor_tensor(second[:], v3(single(slot), CT), first[:].bitcast(F32), ALU.subtract))
                elif kind == "wsplit" and (step[2] == 0 or step[1] < 2):
                    _, e, i = step
                    dve.wait_ge(w_first, NUMBER[step] + 1)
                    first, second = w_parts[i][e % 2]
                    V.tensor_tensor(second[:], fcw[e % NW][i], first[:].bitcast(F32), ALU.subtract).then_inc(w_second[i], 1)
                elif kind == "hsplit":
                    _, e, half = step
                    ms = slice(half * (MT // 2), (half + 1) * (MT // 2))
                    dve.wait_ge(h_whole, 2 * e + half + 1)
                    if e >= 2:
                        dve.wait_ge(written["small"], USE["down", e - 2][2] + 1)
                    up = ("up", e, half)
                    hidden = wide(USE[up][1]).rearrange("p a (m t) -> p (a m) t", m=2)
                    first, second = (part[:, ms, :] for part in h_parts[e % 2])
                    link(V.tensor_copy(first, hidden))
                    give_back(up, V.tensor_tensor(second, hidden, first[:].bitcast(F32), ALU.subtract))
                elif kind == "down":
                    e = step[1]
                    slot = filled(step)
                    if e == 0:
                        dve.wait_ge(b2_loaded, 16)
                    if e >= 2:
                        dve.wait_ge(eo_stored[e % 2], 16 * (e // 2))
                    give_back(step, V.tensor_tensor(eo[e % 2], v3(single(slot), 2),
                                                    b2b[:, e, :].unsqueeze(1).to_broadcast([P, 2, D]), ALU.add))
                elif kind == "combine":
                    t = step[1]
                    dve.wait_ge(gathered[t], 16 * 2)
                    link(V.scalar_tensor_tensor(out=outt[:, t, :], in0=got[0][:, t, :], scalar=R["gate"][0][:, t:t + 1],
                                                in1=xtok[:, t, :], op0=ALU.mult, op1=ALU.add))
                    V.scalar_tensor_tensor(out=outt[:, t, :], in0=got[1][:, t, :], scalar=R["gate"][1][:, t:t + 1],
                                           in1=outt[:, t, :], op0=ALU.mult, op1=ALU.add).then_inc(out_ready, 1)

        @block.gpsimd
        def _(pool):
            own = [0]

            def link(ins):
                own[0] += 1
                ins.then_inc(pool_own, 1)
                pool.wait_ge(pool_own, own[0])

            RED = bass.bass_isa.ReduceOp
            G_ = nc.gpsimd

            def ones_rows(layer):
                for par in range(2):
                    two = stack["k", par][SROWS:MROWS, :, :].rearrange("p h t -> p (h t)").bitcast(F32)
                    G_.memset(two, TWO_BF16_ONES).then_inc(ones_ready, 1)
                    pool.wait_ge(ones_ready, 2 * layer + par + 1)
            G_.memset(zero, 0.0).then_inc(zeroed, 1)
            pool.wait_ge(zeroed, 1)
            ones_rows(0)
            for step in ORDER:
                kind = step[0]
                if kind == "wkv":
                    _, c, b = step
                    n = NUMBER[step]
                    scan, gk = scans[n % 2], gks[n % 2]
                    pool.wait_ge(scanned, n + 1)
                    link(G_.tensor_tensor(scan[0], scan[0], scan[1], ALU.add))
                    link(G_.tensor_tensor(scan[2], scan[2], scan[3], ALU.add))
                    pool.wait_ge(euk_used, n + 1)
                    link(G_.tensor_tensor(scan[2], scan[2], gk, ALU.add))
                    link(G_.tensor_tensor(gk, gk, fsT[:, :, bt(b)], ALU.mult))
                    G_.tensor_tensor(scan[0], scan[0], gk, ALU.add).then_inc(summed, 1)
                    pool.wait_ge(summed, n + 1)
                elif kind == "largest":
                    i = step[1]
                    pool.wait_ge(tern_in, i + 1)
                    G_.partition_all_reduce(small[:, 34 + i:35 + i], small[:, 32 + i:33 + i], P, RED.max
                                            ).then_inc(tern_max, 1)
                    pool.wait_ge(tern_max, i + 1)
                elif kind == "ternary":
                    i = step[1]
                    pool.wait_ge(tern_cnt, i + 1)
                    pool.wait_ge(tern_abs, i + 1)
                    G_.partition_all_reduce(small[:, 46 + 4 * i:48 + 4 * i], small[:, 42 + 2 * i:44 + 2 * i], P, RED.add
                                            ).then_inc(tern_sum, 1)
                    pool.wait_ge(tern_sum, i + 1)
                elif kind == "quant":
                    pool.wait_ge(amax_in, 1)
                    G_.partition_all_reduce(small[:, 65:66], small[:, 64:65], P, RED.max).then_inc(amax_out, 1)
                    pool.wait_ge(amax_out, 1)
                elif kind == "requant" and step[1] == 0:
                    wait_done(pool, ("fc2", 1, CT - 1), "act")
                    ones_rows(1)
                elif kind == "wo" and step[1] == 0 and step[2] == B - 1:
                    pool.wait_ge(written["big"], USE[step][2] + 1)
                    for w_, n_ in ((wq, "wq1"), (wk, "wk1"), (wv, "wv1"), (wo, "wo1")):
                        G_.dma_start(w_, d[n_]).then_inc(loaded["att1"], 16)
                elif kind == "route":
                    pool.wait_ge(written["big"], USE["beta", B - 1][2] + 1)
                    G_.dma_start(wb[:, :, 0:E], d["wg"]).then_inc(loaded["att1"], 16)
                elif kind == "blocks":
                    b = step[1]
                    pool.wait_ge(blocks_ready, b + 1)
                    if b:
                        pool.wait_ge(invT_ready, b)
                    A3 = blkA.rearrange("p (i j) -> p i j", i=BLK)
                    X3 = blkX.rearrange("p (i j) -> p i j", i=BLK)
                    link(G_.tensor_tensor(A3, A3, cT.unsqueeze(2).to_broadcast([P, BLK, BLK]), ALU.mult))
                    link(G_.memset(blkX, 0.0))
                    link(G_.affine_select(out=X3, in_=X3, compare_op=ALU.not_equal, fill=1.0, base=0,
                                          pattern=[[1, BLK], [-1, BLK]], channel_multiplier=0))
                    for k in range(BLK - 1):
                        rows, w = BLK - 1 - k, k + 1
                        tmp = blkT[:, 0:rows * w].rearrange("p (i j) -> p i j", i=rows)
                        link(G_.tensor_tensor(tmp, A3[:, k + 1:BLK, k:k + 1].to_broadcast([P, rows, w]),
                                              X3[:, k:k + 1, 0:w].to_broadcast([P, rows, w]), ALU.mult))
                        ins = G_.tensor_tensor(X3[:, k + 1:BLK, 0:w], X3[:, k + 1:BLK, 0:w], tmp, ALU.subtract)
                        if k < BLK - 2:
                            link(ins)
                        else:
                            ins.then_inc(inv_ready, 1)
                            pool.wait_ge(inv_ready, b + 1)
                elif kind == "wsplit" and step[2] == 1 and step[1] >= 2:
                    _, e, i = step
                    pool.wait_ge(w_second[1], e)
                    pool.wait_ge(w_first, NUMBER[step] + 1)
                    first, second = w_parts[1][e % 2]
                    G_.tensor_tensor(second[:], fcw[e % NW][1], first[:].bitcast(F32), ALU.subtract).then_inc(w_second[1], 1)
                elif kind == "dispT" and step[1] == 0:
                    wait_done(pool, ("ytok", B - 1), "act")
                    pool.wait_ge(disp_zero, 16)
                    for s in range(2):
                        pool.wait_ge(rt_ready, s + 1)
                        for t in range(NT):
                            G_.indirect_dma_start(out=d["disp"], out_offset=bass.IndirectOffsetOnAxis(
                                ap=idx_s[s][:, t:t + 1], axis=0), in_=ytok[:, t, :], in_offset=None
                            ).then_inc(scattered, 16)
                elif kind == "combine":
                    t = step[1]
                    if t == 0:
                        pool.wait_ge(gather_ready, 2)
                        pool.wait_ge(eo_stored[0], 16 * (E // 2))
                        pool.wait_ge(eo_stored[1], 16 * (E // 2))
                    for s in range(2):
                        G_.indirect_dma_start(out=got[s][:, t, :], out_offset=None, in_=d["eo"],
                                              in_offset=bass.IndirectOffsetOnAxis(ap=idx_g[s][:, t:t + 1], axis=0)
                                              ).then_inc(gathered[t], 16)


def _tables():
    p = np.arange(P)
    out = {"ident": np.eye(P), "tri": p[:, None] <= p[None, :], "ones": np.ones((P, P))}
    inv_freq = 1.0 / np.float32(10000.0) ** (np.arange(HALF, dtype=np.float32) / HALF)
    ang = (np.arange(T, dtype=np.float32)[:, None] * inv_freq[None, :].astype(np.float32)).astype(np.float32)
    of = p // H
    cos, sin = np.cos(ang).T[of], np.sin(ang).T[of]
    cos, sin = cos * SCORE_SCALE ** 0.5, sin * SCORE_SCALE ** 0.5
    out["cos"] = cos
    out["sin"] = np.concatenate([sin, -sin], axis=1)
    later = p[None, :] > p[:, None]
    masks = [later, later.T, later | np.eye(P, dtype=bool), later.T | np.eye(P, dtype=bool)]
    out["masks"] = np.concatenate([np.where(m, MASKED, 0.0) for m in masks], axis=1)
    out["rev"] = np.tile(E - np.arange(E), (P, 1))
    out["trash"] = E * CAP + np.arange(2 * NT)[None, :] * P + p[:, None]
    return np.concatenate([np.asarray(out[k], np.float32) for k in CONSTS], axis=1)


def _rows(a):
    return np.ascontiguousarray(a.reshape(-1, P, a.shape[-1]).transpose(1, 0, 2))


def _col(a):
    return a.reshape(-1, P).T


def kernel(**inputs):
    import concourse.bacc as bacc
    from concourse.bass_utils import run_bass_kernel_spmd

    a = {k: np.asarray(v) for k, v in inputs.items()}
    ct, dd, hh = np.meshgrid(np.arange(CT), np.arange(HALF), np.arange(H), indexing="ij")
    perm = (hh * HD + ct * HALF + dd).reshape(-1)
    cols = [_col(a[f"{g}_{k}"]) for k in "wu" for g in ("L0_cond", "L0_cond2", "L1_cond", "L1_cond2")]
    cols += [_col(a["L0_attn_bq"][perm]), _col(a["L0_attn_bk"][perm]), _col(a["L0_attn_bo"]), _col(a["L0_ffn_b1"]),
             _col(a["L0_ffn_b2"]), _col(a["L1_ffn_fc1_b"].reshape(-1))]
    arrays = {
        "consts": _tables(), "columns": np.ascontiguousarray(np.concatenate(cols, axis=1)), "cond": a["cond_512"],
        "fsT": _rows(a["fside_BxSxS_0"].reshape(N, D).T), "xT": _rows(a["x"].reshape(N, D).T),
        "bv": a["L0_attn_bv"], "bb": a["L1_attn_bb"], "wb": _rows(a["L1_attn_Wb"]), "wg": _rows(a["L1_ffn_wg"]),
        "w1T": _rows(a["L0_ffn_W1"].T), "w2T": _rows(a["L0_ffn_W2"].T),
        "fc1": np.stack([_rows(w) for w in a["L1_ffn_fc1_w"]]), "fc2": np.stack([_rows(w) for w in a["L1_ffn_fc2_w"]]),
        "fb2": a["L1_ffn_fc2_b"],
    }
    for layer in range(2):
        for name, cols_ in (("q", perm), ("k", perm), ("v", slice(None)), ("o", slice(None))):
            arrays[f"w{name}{layer}"] = _rows(a[f"L{layer}_attn_W{name}"][:, cols_])
    nc = bacc.Bacc("TRN2", target_bir_lowering=False, num_devices=1)
    d = {}
    for name, arr in arrays.items():
        arrays[name] = np.ascontiguousarray(arr)
        d[name] = nc.dram_tensor(name, arr.shape, mybir.dt.from_np(arr.dtype), kind="ExternalInput").ap()
    d["parts"] = nc.dram_tensor("parts", (2 * B, 2, 3, CT, P, T), BF16, kind="Internal").ap()
    d["disp"] = nc.dram_tensor("dispatched", (E * CAP + 2 * N, D), F32, kind="Internal").ap()
    d["eo"] = nc.dram_tensor("expert_rows", (E * CAP, D), F32, kind="Internal").ap()
    d["out"] = nc.dram_tensor("out", (N, D), F32, kind="ExternalOutput").ap()
    program(nc, d)
    r = run_bass_kernel_spmd(nc, [arrays], core_ids=[0])
    return r.results[0]["out"].reshape(B, T, D)
```
